# Optimizing a Trainium2 kernel written in Bass

```python
import numpy as np
import jax
import jax.numpy as jnp

def _softmax(x, axis=-1):
    return jax.nn.softmax(x, axis=axis)

def _gelu(x):
    return jax.nn.gelu(x, approximate=True)

def _silu(x):
    return jax.nn.silu(x)

def _sigmoid(x):
    return jax.nn.sigmoid(x)

def _layernorm(x, axis=-1, eps=1e-05):
    m = jnp.mean(x, axis=axis, keepdims=True)
    v = jnp.var(x, axis=axis, keepdims=True)
    return (x - m) / jnp.sqrt(v + eps)

def _scatter_add(tgt, idx, src, axis=0):
    return tgt.at[idx].add(src)

def _segment_sum(src, seg, n):
    return jax.ops.segment_sum(src, seg, n)
kernel_name = 'mk_seq_preln_d4_jaxref_r8_d0f744'

def setup_inputs(seed: int=0):
    np.random.seed(seed)
    _w = jnp.asarray

    def _L0_attn_setup():
        import jax, jax.numpy as jnp
        import numpy as np
        DIM = 128
        HEADS = 16
        HEAD_DIM = DIM // HEADS
        B, S = (4, 512)
        key = jax.random.key(seed)
        ks = jax.random.split(key, 8)
        sc = 1.0 / np.sqrt(DIM)
        return {'x': jax.random.normal(ks[0], (B, S, DIM), dtype=jnp.float32), 'Wq': jax.random.normal(ks[1], (DIM, DIM), dtype=jnp.float32) * sc, 'Wk': jax.random.normal(ks[2], (DIM, DIM), dtype=jnp.float32) * sc, 'Wv': jax.random.normal(ks[3], (DIM, DIM), dtype=jnp.float32) * sc, 'Wp': jax.random.normal(ks[4], (DIM, DIM), dtype=jnp.float32) * sc, 'bp': jnp.zeros((DIM,), dtype=jnp.float32), 'conv_w': jax.random.normal(ks[5], (DIM, 3), dtype=jnp.float32) * (1.0 / np.sqrt(3.0)), 'conv_b': jnp.zeros((DIM,), dtype=jnp.float32)}
    _L0_attn_in = _L0_attn_setup()

    def _L0_ffn_setup():
        import jax, jax.numpy as jnp
        import numpy as np
        LN_EPS = 0.001
        EPS = 1e-05
        QB = 128.0

        def ste_round(x):
            return x + jax.lax.stop_gradient(jnp.round(x) - x)
        key = jax.random.key(seed)
        k1, k2 = jax.random.split(key)
        x = jax.random.normal(k1, (4, 1024, 128), dtype=jnp.float32)
        weight = jax.random.normal(k2, (128, 128), dtype=jnp.float32) * 0.02
        ln_gamma = jnp.ones((128,), dtype=jnp.float32)
        ln_beta = jnp.zeros((128,), dtype=jnp.float32)
        return {'x': x, 'weight': weight, 'ln_gamma': ln_gamma, 'ln_beta': ln_beta}
    _L0_ffn_in = _L0_ffn_setup()

    def _L1_attn_setup():
        import jax, jax.numpy as jnp
        import numpy as np
        DIM = 128
        NUM_HEADS = 16
        HEAD_DIM = DIM // NUM_HEADS

        def _rope_tables(seq_len, dim, dtype):
            inv_freq = 1.0 / 10000.0 ** (jnp.arange(0, dim, 2, dtype=jnp.float32) / dim)
            t = jnp.arange(seq_len, dtype=jnp.float32)
            freqs = jnp.outer(t, inv_freq)
            return (jnp.cos(freqs).astype(dtype), jnp.sin(freqs).astype(dtype))

        def _apply_rope(x, cos_emb, sin_emb):
            x1 = x[..., 0::2]
            x2 = x[..., 1::2]
            return jnp.concatenate((x1 * cos_emb - x2 * sin_emb, x1 * sin_emb + x2 * cos_emb), axis=-1)
        key = jax.random.key(seed)
        k_x, k_qkv, k_out, k_b = jax.random.split(key, 4)
        B, S, D = (2, 256, DIM)
        x = jax.random.normal(k_x, (B, S, D), dtype=jnp.float32)
        w_qkv = jax.random.normal(k_qkv, (3 * D, D), dtype=jnp.float32) * (1.0 / np.sqrt(D))
        w_out = jax.random.normal(k_out, (D, D), dtype=jnp.float32) * (1.0 / np.sqrt(D))
        b_out = jax.random.normal(k_b, (D,), dtype=jnp.float32) * 0.01
        return {'x': x, 'w_qkv': w_qkv, 'w_out': w_out, 'b_out': b_out}
    _L1_attn_in = _L1_attn_setup()

    def _L1_ffn_setup():
        import jax, jax.numpy as jnp
        import numpy as np
        DIM = 128
        DEPTH = 2
        HEADS = 8
        DIM_HEAD = 64
        WINDOW = 64
        INNER = HEADS * DIM_HEAD
        HID = int(DIM * 4 * 2 / 3)
        B, N = (2, 1024)
        QK_SCALE = 8.0

        def shift_token(t):
            t1, t2 = jnp.split(t, 2, axis=-1)
            t2 = jnp.pad(t2, ((0, 0), (1, 0), (0, 0)))[:, :-1]
            return jnp.concatenate([t1, t2], axis=-1)

        def l2norm(t):
            return t / jnp.clip(jnp.linalg.norm(t, axis=-1, keepdims=True), 1e-12)

        def rotate_half(x):
            x1, x2 = jnp.split(x, 2, axis=-1)
            return jnp.concatenate([-x2, x1], axis=-1)

        def rotary_xpos(q, k):
            n = q.shape[-2]
            half_idx = jnp.arange(0, DIM_HEAD, 2, dtype=jnp.float32)
            inv_freq = 1.0 / 10000.0 ** (half_idx / DIM_HEAD)
            t = jnp.arange(n, dtype=jnp.float32)
            freqs = t[:, None] * inv_freq[None, :]
            freqs = jnp.concatenate([freqs, freqs], axis=-1)
            base = (half_idx + 0.4 * DIM_HEAD) / (1.4 * DIM_HEAD)
            power = (t - n // 2) / float(WINDOW // 2)
            scale = base[None, :] ** power[:, None]
            scale = jnp.concatenate([scale, scale], axis=-1)
            cos, sin = (jnp.cos(freqs), jnp.sin(freqs))
            q = q * cos * scale + rotate_half(q) * sin * scale
            k = k * cos / scale + rotate_half(k) * sin / scale
            return (q, k)

        def local_attention(q, k, v):
            b, h, n, d = q.shape
            w = n // WINDOW
            bq = q.reshape(b, h, w, WINDOW, d) * QK_SCALE
            bk = k.reshape(b, h, w, WINDOW, d)
            bv = v.reshape(b, h, w, WINDOW, d)

            def look_around(t):
                p = jnp.pad(t, ((0, 0), (0, 0), (1, 0), (0, 0), (0, 0)))
                return jnp.concatenate([p[:, :, :w], p[:, :, 1:]], axis=3)
            bk, bv = (look_around(bk), look_around(bv))
            bt = jnp.arange(n).reshape(w, WINDOW)
            btp = jnp.pad(bt, ((1, 0), (0, 0)), constant_values=-1)
            btk = jnp.concatenate([btp[:w], btp[1:]], axis=1)
            sim = jnp.einsum('bhwid,bhwjd->bhwij', bq, bk)
            i = bt[:, :, None]
            j = btk[:, None, :]
            mask = (i < j) | (i > j + WINDOW) | (j == -1)
            sim = jnp.where(mask, -jnp.finfo(sim.dtype).max, sim)
            attn = jax.nn.softmax(sim, axis=-1)
            out = jnp.einsum('bhwij,bhwjd->bhwid', attn, bv)
            return out.reshape(b, h, n, d)

        def _layer(x, wqkv, qs, ksc, wo, lg, lb, w1, b1, w2, b2):
            b, n, _ = x.shape
            h = shift_token(x)
            qkv = h @ wqkv
            q, k, v = jnp.split(qkv, 3, axis=-1)
            to_heads = lambda t: t.reshape(b, n, HEADS, DIM_HEAD).transpose(0, 2, 1, 3)
            q, k, v = (to_heads(q), to_heads(k), to_heads(v))
            q = l2norm(q) * qs
            k = l2norm(k) * ksc
            q, k = rotary_xpos(q, k)
            o = local_attention(q, k, v)
            o = o.transpose(0, 2, 1, 3).reshape(b, n, INNER)
            x = x + o @ wo
            h = shift_token(x)
            mu = h.mean(-1, keepdims=True)
            var = h.var(-1, keepdims=True)
            h = (h - mu) / jnp.sqrt(var + 1e-05) * lg + lb
            h = h @ w1 + b1
            a, g = jnp.split(h, 2, axis=-1)
            h = a * jax.nn.gelu(g, approximate=False)
            x = x + h @ w2 + b2
            return x
        key = jax.random.key(seed)
        ks = jax.random.split(key, 6)
        return {'x': jax.random.normal(ks[0], (B, N, DIM), jnp.float32), 'wqkv': jax.random.normal(ks[1], (DEPTH, DIM, 3 * INNER), jnp.float32) * 0.02, 'q_scale': jnp.ones((DEPTH, DIM_HEAD), jnp.float32), 'k_scale': jnp.ones((DEPTH, DIM_HEAD), jnp.float32), 'wo': jax.random.normal(ks[2], (DEPTH, INNER, DIM), jnp.float32) * 0.02, 'ln_g': jnp.ones((DEPTH, DIM), jnp.float32), 'ln_b': jnp.zeros((DEPTH, DIM), jnp.float32), 'w1': jax.random.normal(ks[3], (DEPTH, DIM, 2 * HID), jnp.float32) * 0.02, 'b1': jnp.zeros((DEPTH, 2 * HID), jnp.float32), 'w2': jax.random.normal(ks[4], (DEPTH, HID, DIM), jnp.float32) * 0.02, 'b2': jnp.zeros((DEPTH, DIM), jnp.float32)}
    _L1_ffn_in = _L1_ffn_setup()

    def _L2_attn_setup():
        import jax, jax.numpy as jnp
        import numpy as np
        D_MODEL, N_HEADS, D_FF = (128, 16, 512)
        SCALE = 0.1
        NUM_BITS = 8
        LEVELS = 1 << NUM_BITS
        HALF = LEVELS // 2
        MAX_EXP = 4
        EPS = 1e-05

        def pow2_weight(key, shape, max_exp=MAX_EXP):
            k1, k2 = jax.random.split(key)
            sign = jax.random.randint(k1, shape, -1, 2).astype(jnp.float32)
            e = jax.random.randint(k2, shape, max_exp, max_exp + 4).astype(jnp.float32)
            return sign * jnp.exp2(-e)

        def _layernorm(x, g, b):
            mu = jnp.mean(x, axis=-1, keepdims=True)
            var = jnp.var(x, axis=-1, keepdims=True)
            return (x - mu) * jax.lax.rsqrt(var + EPS) * g + b

        def _lookup_act(x):
            grid = (jnp.arange(LEVELS, dtype=jnp.float32) - HALF) * SCALE
            table = jax.nn.gelu(grid)
            idx = jnp.clip(jnp.round(x / SCALE).astype(jnp.int32) + HALF, 0, LEVELS - 1)
            return table[idx]

        def _linear_attention(x, wq, wk, wv, wo):
            B, S, D = x.shape
            H, Dh = (N_HEADS, D // N_HEADS)
            q = (x @ wq).reshape(B, S, H, Dh)
            k = (x @ wk).reshape(B, S, H, Dh)
            v = (x @ wv).reshape(B, S, H, Dh)
            phi_q = jax.nn.elu(q) + 1.0
            phi_k = jax.nn.elu(k) + 1.0
            kv = jnp.einsum('bshd,bshe->bhde', phi_k, v)
            z = jnp.sum(phi_k, axis=1)
            num = jnp.einsum('bshd,bhde->bshe', phi_q, kv)
            den = jnp.einsum('bshd,bhd->bsh', phi_q, z)[..., None] + 1e-06
            out = (num / den).reshape(B, S, D)
            return out @ wo
        key = jax.random.key(seed)
        ks = jax.random.split(key, 8)
        x = jax.random.normal(ks[0], (4, 256, D_MODEL), dtype=jnp.float32)
        return {'x': x, 'ln1_g': jnp.ones((D_MODEL,), jnp.float32), 'ln1_b': jnp.zeros((D_MODEL,), jnp.float32), 'wq': pow2_weight(ks[1], (D_MODEL, D_MODEL)), 'wk': pow2_weight(ks[2], (D_MODEL, D_MODEL)), 'wv': pow2_weight(ks[3], (D_MODEL, D_MODEL)), 'wo': pow2_weight(ks[4], (D_MODEL, D_MODEL)), 'ln2_g': jnp.ones((D_MODEL,), jnp.float32), 'ln2_b': jnp.zeros((D_MODEL,), jnp.float32), 'w1': pow2_weight(ks[5], (D_MODEL, D_FF)), 'w2': pow2_weight(ks[6], (D_FF, D_MODEL))}
    _L2_attn_in = _L2_attn_setup()

    def _L2_ffn_setup():
        import jax, jax.numpy as jnp
        import numpy as np
        import math
        B, S, D = (4, 256, 128)
        E, DFF = (16, 256)
        CAP_FACTOR = 2.0
        ROUTER_HIDDEN = 128
        CAPACITY = int(math.ceil(S * CAP_FACTOR / E))
        key = jax.random.key(seed)
        ks = jax.random.split(key, 6)

        def uinit(k, shape, fan_in):
            bound = math.sqrt(3.0) * math.sqrt(1.0 / 3.0) / math.sqrt(fan_in)
            return jax.random.uniform(k, shape, jnp.float32, -bound, bound)
        return {'hidden_states': jax.random.normal(ks[0], (B, S, D), jnp.float32), 'router_w1': jax.random.normal(ks[1], (D, ROUTER_HIDDEN), jnp.float32) / math.sqrt(D), 'router_w2': jax.random.normal(ks[2], (ROUTER_HIDDEN, E), jnp.float32) / math.sqrt(ROUTER_HIDDEN), 'w1': uinit(ks[3], (E, D, DFF), D), 'w2': uinit(ks[4], (E, D, DFF), D), 'w3': uinit(ks[5], (E, DFF, D), DFF)}
    _L2_ffn_in = _L2_ffn_setup()

    def _L3_attn_setup():
        import jax, jax.numpy as jnp
        import numpy as np
        B, S, E, H, Dh = (2, 256, 128, 16, 64)
        key = jax.random.key(seed)
        ks = jax.random.split(key, 8)
        w = 0.02
        return {'x': jax.random.normal(ks[0], (B, S, E), jnp.float32), 'Wq': jax.random.normal(ks[1], (H, Dh, E), jnp.float32) * w, 'bq': jax.random.normal(ks[2], (H, Dh), jnp.float32) * w, 'Wk': jax.random.normal(ks[3], (H, Dh, E), jnp.float32) * w, 'bk': jax.random.normal(ks[4], (H, Dh), jnp.float32) * w, 'Wv': jax.random.normal(ks[5], (H, Dh, E), jnp.float32) * w, 'bv': jax.random.normal(ks[6], (H, Dh), jnp.float32) * w, 'proj': jax.random.normal(ks[7], (H * Dh, E), jnp.float32) * w}
    _L3_attn_in = _L3_attn_setup()

    def _L3_ffn_setup():
        import jax, jax.numpy as jnp
        import numpy as np
        TOP_K = 2
        key = jax.random.key(seed)
        k1, k2, k3, k4 = jax.random.split(key, 4)
        B, S, H, I, E = (2, 256, 128, 512, 8)
        return {'hidden_states': jax.random.normal(k1, (B, S, H), jnp.float32), 'gate_w': jax.random.normal(k2, (E, H), jnp.float32) * 0.02, 'gate_up_proj': jax.random.normal(k3, (E, 2 * I, H), jnp.float32) * 0.02, 'down_proj': jax.random.normal(k4, (E, H, I), jnp.float32) * 0.02}
    _L3_ffn_in = _L3_ffn_setup()
    _d = {'L0_attn_x': _L0_attn_in['x'], 'L0_attn_Wq': _L0_attn_in['Wq'], 'L0_attn_Wk': _L0_attn_in['Wk'], 'L0_attn_Wv': _L0_attn_in['Wv'], 'L0_attn_Wp': _L0_attn_in['Wp'], 'L0_attn_bp': _L0_attn_in['bp'], 'L0_attn_conv_w': _L0_attn_in['conv_w'], 'L0_attn_conv_b': _L0_attn_in['conv_b'], 'L0_ffn_weight': _L0_ffn_in['weight'], 'L0_ffn_ln_gamma': _L0_ffn_in['ln_gamma'], 'L0_ffn_ln_beta': _L0_ffn_in['ln_beta'], 'L1_attn_w_qkv': _L1_attn_in['w_qkv'], 'L1_attn_w_out': _L1_attn_in['w_out'], 'L1_attn_b_out': _L1_attn_in['b_out'], 'L1_ffn_wqkv': _L1_ffn_in['wqkv'], 'L1_ffn_q_scale': _L1_ffn_in['q_scale'], 'L1_ffn_k_scale': _L1_ffn_in['k_scale'], 'L1_ffn_wo': _L1_ffn_in['wo'], 'L1_ffn_ln_g': _L1_ffn_in['ln_g'], 'L1_ffn_ln_b': _L1_ffn_in['ln_b'], 'L1_ffn_w1': _L1_ffn_in['w1'], 'L1_ffn_b1': _L1_ffn_in['b1'], 'L1_ffn_w2': _L1_ffn_in['w2'], 'L1_ffn_b2': _L1_ffn_in['b2'], 'L2_attn_ln1_g': _L2_attn_in['ln1_g'], 'L2_attn_ln1_b': _L2_attn_in['ln1_b'], 'L2_attn_wq': _L2_attn_in['wq'], 'L2_attn_wk': _L2_attn_in['wk'], 'L2_attn_wv': _L2_attn_in['wv'], 'L2_attn_wo': _L2_attn_in['wo'], 'L2_attn_ln2_g': _L2_attn_in['ln2_g'], 'L2_attn_ln2_b': _L2_attn_in['ln2_b'], 'L2_attn_w1': _L2_attn_in['w1'], 'L2_attn_w2': _L2_attn_in['w2'], 'L2_ffn_router_w1': _L2_ffn_in['router_w1'], 'L2_ffn_router_w2': _L2_ffn_in['router_w2'], 'L2_ffn_w1': _L2_ffn_in['w1'], 'L2_ffn_w2': _L2_ffn_in['w2'], 'L2_ffn_w3': _L2_ffn_in['w3'], 'L3_attn_Wq': _L3_attn_in['Wq'], 'L3_attn_bq': _L3_attn_in['bq'], 'L3_attn_Wk': _L3_attn_in['Wk'], 'L3_attn_bk': _L3_attn_in['bk'], 'L3_attn_Wv': _L3_attn_in['Wv'], 'L3_attn_bv': _L3_attn_in['bv'], 'L3_attn_proj': _L3_attn_in['proj'], 'L3_ffn_gate_w': _L3_ffn_in['gate_w'], 'L3_ffn_gate_up_proj': _L3_ffn_in['gate_up_proj'], 'L3_ffn_down_proj': _L3_ffn_in['down_proj']}
    _x0 = _d['L0_attn_x']
    _d['L0_attn_x'] = jax.random.normal(jax.random.fold_in(jax.random.key(seed), 1), (1, 2048, 128), dtype=_x0.dtype)
    del _x0
    return _d

def reference(L0_attn_x, L0_attn_Wq, L0_attn_Wk, L0_attn_Wv, L0_attn_Wp, L0_attn_bp, L0_attn_conv_w, L0_attn_conv_b, L0_ffn_weight, L0_ffn_ln_gamma, L0_ffn_ln_beta, L1_attn_w_qkv, L1_attn_w_out, L1_attn_b_out, L1_ffn_wqkv, L1_ffn_q_scale, L1_ffn_k_scale, L1_ffn_wo, L1_ffn_ln_g, L1_ffn_ln_b, L1_ffn_w1, L1_ffn_b1, L1_ffn_w2, L1_ffn_b2, L2_attn_ln1_g, L2_attn_ln1_b, L2_attn_wq, L2_attn_wk, L2_attn_wv, L2_attn_wo, L2_attn_ln2_g, L2_attn_ln2_b, L2_attn_w1, L2_attn_w2, L2_ffn_router_w1, L2_ffn_router_w2, L2_ffn_w1, L2_ffn_w2, L2_ffn_w3, L3_attn_Wq, L3_attn_bq, L3_attn_Wk, L3_attn_bk, L3_attn_Wv, L3_attn_bv, L3_attn_proj, L3_ffn_gate_w, L3_ffn_gate_up_proj, L3_ffn_down_proj):

    def _L0_attn_ref(x, Wq, Wk, Wv, Wp, bp, conv_w, conv_b):
        import jax, jax.numpy as jnp
        import numpy as np
        DIM = 128
        HEADS = 16
        HEAD_DIM = DIM // HEADS
        B, S = (4, 512)
        b, s, d = x.shape

        def split_heads(t):
            return t.reshape(b, s, HEADS, HEAD_DIM).transpose(0, 2, 1, 3)
        q = split_heads(x @ Wq.T)
        k = split_heads(x @ Wk.T)
        v = split_heads(x @ Wv.T)
        q = jax.nn.elu(q) + 1.0
        k = jax.nn.elu(k) + 1.0
        kv_state = jnp.einsum('bhnd,bhne->bhde', k, v)
        k_state = k.sum(axis=2)
        attn_out = jnp.einsum('bhnd,bhde->bhne', q, kv_state)
        denom = jnp.maximum(jnp.einsum('bhnd,bhd->bhn', q, k_state), 1e-06)[..., None]
        attn_out = (attn_out / denom).transpose(0, 2, 1, 3).reshape(b, s, d)
        xp = jnp.pad(x, ((0, 0), (1, 1), (0, 0)))
        local = xp[:, :-2, :] * conv_w[:, 0] + xp[:, 1:-1, :] * conv_w[:, 1] + xp[:, 2:, :] * conv_w[:, 2] + conv_b
        return (attn_out + local) @ Wp.T + bp

    def _L0_ffn_ref(x, weight, ln_gamma, ln_beta):
        import jax, jax.numpy as jnp
        import numpy as np
        LN_EPS = 0.001
        EPS = 1e-05
        QB = 128.0

        def ste_round(x):
            return x + jax.lax.stop_gradient(jnp.round(x) - x)
        mu = jnp.mean(x, axis=-1, keepdims=True)
        var = jnp.var(x, axis=-1, keepdims=True)
        xn = (x - mu) * jax.lax.rsqrt(var + LN_EPS) * ln_gamma + ln_beta
        beta = jnp.mean(jnp.abs(weight))
        w_q = jnp.clip(ste_round(weight / (beta + EPS)), -1.0, 1.0)
        gamma = jnp.max(jnp.abs(xn))
        xq = jnp.clip(xn * QB / gamma, -QB + EPS, QB - EPS)
        y = jnp.einsum('bsd,du->bsu', xq, w_q)
        return y * (gamma * beta / QB)

    def _L1_attn_ref(x, w_qkv, w_out, b_out):
        import jax, jax.numpy as jnp
        import numpy as np
        DIM = 128
        NUM_HEADS = 16
        HEAD_DIM = DIM // NUM_HEADS

        def _rope_tables(seq_len, dim, dtype):
            inv_freq = 1.0 / 10000.0 ** (jnp.arange(0, dim, 2, dtype=jnp.float32) / dim)
            t = jnp.arange(seq_len, dtype=jnp.float32)
            freqs = jnp.outer(t, inv_freq)
            return (jnp.cos(freqs).astype(dtype), jnp.sin(freqs).astype(dtype))

        def _apply_rope(x, cos_emb, sin_emb):
            x1 = x[..., 0::2]
            x2 = x[..., 1::2]
            return jnp.concatenate((x1 * cos_emb - x2 * sin_emb, x1 * sin_emb + x2 * cos_emb), axis=-1)
        B, S, D = x.shape
        H, hd = (NUM_HEADS, HEAD_DIM)
        qkv = jnp.einsum('bsd,ed->bse', x, w_qkv)
        q, k, v = jnp.split(qkv, 3, axis=-1)
        q, k, v = (t.reshape(B, S, H, hd).transpose(0, 2, 1, 3) for t in (q, k, v))
        cos_emb, sin_emb = _rope_tables(S, hd, x.dtype)
        q = _apply_rope(q, cos_emb, sin_emb)
        k = _apply_rope(k, cos_emb, sin_emb)
        scores = jnp.einsum('bhqd,bhkd->bhqk', q, k) / jnp.sqrt(jnp.asarray(hd, x.dtype))
        attn = jax.nn.softmax(scores, axis=-1)
        out = jnp.einsum('bhqk,bhkd->bhqd', attn, v)
        out = out.transpose(0, 2, 1, 3).reshape(B, S, D)
        return jnp.einsum('bsd,ed->bse', out, w_out) + b_out

    def _L1_ffn_ref(x, wqkv, q_scale, k_scale, wo, ln_g, ln_b, w1, b1, w2, b2):
        import jax, jax.numpy as jnp
        import numpy as np
        DIM = 128
        DEPTH = 2
        HEADS = 8
        DIM_HEAD = 64
        WINDOW = 64
        INNER = HEADS * DIM_HEAD
        HID = int(DIM * 4 * 2 / 3)
        B, N = (2, 1024)
        QK_SCALE = 8.0

        def shift_token(t):
            t1, t2 = jnp.split(t, 2, axis=-1)
            t2 = jnp.pad(t2, ((0, 0), (1, 0), (0, 0)))[:, :-1]
            return jnp.concatenate([t1, t2], axis=-1)

        def l2norm(t):
            return t / jnp.clip(jnp.linalg.norm(t, axis=-1, keepdims=True), 1e-12)

        def rotate_half(x):
            x1, x2 = jnp.split(x, 2, axis=-1)
            return jnp.concatenate([-x2, x1], axis=-1)

        def rotary_xpos(q, k):
            n = q.shape[-2]
            half_idx = jnp.arange(0, DIM_HEAD, 2, dtype=jnp.float32)
            inv_freq = 1.0 / 10000.0 ** (half_idx / DIM_HEAD)
            t = jnp.arange(n, dtype=jnp.float32)
            freqs = t[:, None] * inv_freq[None, :]
            freqs = jnp.concatenate([freqs, freqs], axis=-1)
            base = (half_idx + 0.4 * DIM_HEAD) / (1.4 * DIM_HEAD)
            power = (t - n // 2) / float(WINDOW // 2)
            scale = base[None, :] ** power[:, None]
            scale = jnp.concatenate([scale, scale], axis=-1)
            cos, sin = (jnp.cos(freqs), jnp.sin(freqs))
            q = q * cos * scale + rotate_half(q) * sin * scale
            k = k * cos / scale + rotate_half(k) * sin / scale
            return (q, k)

        def local_attention(q, k, v):
            b, h, n, d = q.shape
            w = n // WINDOW
            bq = q.reshape(b, h, w, WINDOW, d) * QK_SCALE
            bk = k.reshape(b, h, w, WINDOW, d)
            bv = v.reshape(b, h, w, WINDOW, d)

            def look_around(t):
                p = jnp.pad(t, ((0, 0), (0, 0), (1, 0), (0, 0), (0, 0)))
                return jnp.concatenate([p[:, :, :w], p[:, :, 1:]], axis=3)
            bk, bv = (look_around(bk), look_around(bv))
            bt = jnp.arange(n).reshape(w, WINDOW)
            btp = jnp.pad(bt, ((1, 0), (0, 0)), constant_values=-1)
            btk = jnp.concatenate([btp[:w], btp[1:]], axis=1)
            sim = jnp.einsum('bhwid,bhwjd->bhwij', bq, bk)
            i = bt[:, :, None]
            j = btk[:, None, :]
            mask = (i < j) | (i > j + WINDOW) | (j == -1)
            sim = jnp.where(mask, -jnp.finfo(sim.dtype).max, sim)
            attn = jax.nn.softmax(sim, axis=-1)
            out = jnp.einsum('bhwij,bhwjd->bhwid', attn, bv)
            return out.reshape(b, h, n, d)

        def _layer(x, wqkv, qs, ksc, wo, lg, lb, w1, b1, w2, b2):
            b, n, _ = x.shape
            h = shift_token(x)
            qkv = h @ wqkv
            q, k, v = jnp.split(qkv, 3, axis=-1)
            to_heads = lambda t: t.reshape(b, n, HEADS, DIM_HEAD).transpose(0, 2, 1, 3)
            q, k, v = (to_heads(q), to_heads(k), to_heads(v))
            q = l2norm(q) * qs
            k = l2norm(k) * ksc
            q, k = rotary_xpos(q, k)
            o = local_attention(q, k, v)
            o = o.transpose(0, 2, 1, 3).reshape(b, n, INNER)
            x = x + o @ wo
            h = shift_token(x)
            mu = h.mean(-1, keepdims=True)
            var = h.var(-1, keepdims=True)
            h = (h - mu) / jnp.sqrt(var + 1e-05) * lg + lb
            h = h @ w1 + b1
            a, g = jnp.split(h, 2, axis=-1)
            h = a * jax.nn.gelu(g, approximate=False)
            x = x + h @ w2 + b2
            return x
        for l in range(DEPTH):
            x = _layer(x, wqkv[l], q_scale[l], k_scale[l], wo[l], ln_g[l], ln_b[l], w1[l], b1[l], w2[l], b2[l])
        return x

    def _L2_attn_ref(x, ln1_g, ln1_b, wq, wk, wv, wo, ln2_g, ln2_b, w1, w2):
        import jax, jax.numpy as jnp
        import numpy as np
        D_MODEL, N_HEADS, D_FF = (128, 16, 512)
        SCALE = 0.1
        NUM_BITS = 8
        LEVELS = 1 << NUM_BITS
        HALF = LEVELS // 2
        MAX_EXP = 4
        EPS = 1e-05

        def pow2_weight(key, shape, max_exp=MAX_EXP):
            k1, k2 = jax.random.split(key)
            sign = jax.random.randint(k1, shape, -1, 2).astype(jnp.float32)
            e = jax.random.randint(k2, shape, max_exp, max_exp + 4).astype(jnp.float32)
            return sign * jnp.exp2(-e)

        def _layernorm(x, g, b):
            mu = jnp.mean(x, axis=-1, keepdims=True)
            var = jnp.var(x, axis=-1, keepdims=True)
            return (x - mu) * jax.lax.rsqrt(var + EPS) * g + b

        def _lookup_act(x):
            grid = (jnp.arange(LEVELS, dtype=jnp.float32) - HALF) * SCALE
            table = jax.nn.gelu(grid)
            idx = jnp.clip(jnp.round(x / SCALE).astype(jnp.int32) + HALF, 0, LEVELS - 1)
            return table[idx]

        def _linear_attention(x, wq, wk, wv, wo):
            B, S, D = x.shape
            H, Dh = (N_HEADS, D // N_HEADS)
            q = (x @ wq).reshape(B, S, H, Dh)
            k = (x @ wk).reshape(B, S, H, Dh)
            v = (x @ wv).reshape(B, S, H, Dh)
            phi_q = jax.nn.elu(q) + 1.0
            phi_k = jax.nn.elu(k) + 1.0
            kv = jnp.einsum('bshd,bshe->bhde', phi_k, v)
            z = jnp.sum(phi_k, axis=1)
            num = jnp.einsum('bshd,bhde->bshe', phi_q, kv)
            den = jnp.einsum('bshd,bhd->bsh', phi_q, z)[..., None] + 1e-06
            out = (num / den).reshape(B, S, D)
            return out @ wo
        x = x + _linear_attention(_layernorm(x, ln1_g, ln1_b), wq, wk, wv, wo)
        h = _layernorm(x, ln2_g, ln2_b)
        x = x + _lookup_act(h @ w1) @ w2
        return x

    def _L2_ffn_ref(hidden_states, router_w1, router_w2, w1, w2, w3):
        import jax, jax.numpy as jnp
        import numpy as np
        import math
        B, S, D = (4, 256, 128)
        E, DFF = (16, 256)
        CAP_FACTOR = 2.0
        ROUTER_HIDDEN = 128
        CAPACITY = int(math.ceil(S * CAP_FACTOR / E))
        b, s, d = hidden_states.shape
        e = w1.shape[0]
        cap = CAPACITY
        router_logits = jax.nn.silu(hidden_states @ router_w1) @ router_w2
        expert_probs = jax.nn.softmax(router_logits.transpose(0, 2, 1), axis=-1)
        expert_weights, token_indices = jax.lax.top_k(expert_probs, cap)
        expert_weights = expert_weights / (expert_weights.sum(-1, keepdims=True) + 1e-09)
        expert_inputs = jax.vmap(lambda h, i: h[i])(hidden_states, token_indices)
        gate = jax.nn.silu(jnp.einsum('becd,edf->becf', expert_inputs, w1))
        value = jnp.einsum('becd,edf->becf', expert_inputs, w2)
        expert_out = jnp.einsum('becf,efd->becd', gate * value, w3)
        weighted = expert_out * expert_weights[..., None]

        def combine(idx, vals):
            return jnp.zeros((s, d), vals.dtype).at[idx.reshape(-1)].add(vals.reshape(-1, d))
        output = jax.vmap(combine)(token_indices, weighted)
        return output

    def _L3_attn_ref(x, Wq, bq, Wk, bk, Wv, bv, proj):
        import jax, jax.numpy as jnp
        import numpy as np
        B, S, E, H, Dh = (2, 256, 128, 16, 64)
        b, s, e = x.shape
        h, dh, _ = Wq.shape
        scale = jnp.sqrt(jnp.asarray(dh, x.dtype))
        q = jnp.einsum('bse,hde->bhsd', x, Wq) + bq[None, :, None, :]
        k = jnp.einsum('bse,hde->bhsd', x, Wk) + bk[None, :, None, :]
        v = jnp.einsum('bse,hde->bhsd', x, Wv) + bv[None, :, None, :]
        causal = jnp.triu(jnp.ones((s, s), bool), 1)
        scores = jnp.einsum('bhsd,bhtd->bhst', q, k) / scale
        scores = jnp.where(causal[None, None], -jnp.inf, scores)
        att = jax.nn.softmax(scores, axis=-1) / scale
        z = jnp.einsum('bhst,bhtd->bhsd', att, v)
        z = z.reshape(b, s, h * dh)
        return z @ proj

    def _L3_ffn_ref(hidden_states, gate_w, gate_up_proj, down_proj):
        import jax, jax.numpy as jnp
        import numpy as np
        TOP_K = 2
        B, S, H = hidden_states.shape
        E = gate_w.shape[0]
        x = hidden_states.reshape(-1, H)
        T = x.shape[0]
        probs = jax.nn.softmax(x @ gate_w.T, axis=-1)
        w, idx = jax.lax.top_k(probs, TOP_K)
        w = w / jnp.sum(w, axis=-1, keepdims=True)
        combine = jnp.zeros((T, E), x.dtype).at[jnp.arange(T)[:, None], idx].add(w)

        def step(acc, inputs):
            gup, dn, ce = inputs
            g, u = jnp.split(x @ gup.T, 2, axis=-1)
            acc = acc + ce[:, None] * (jax.nn.silu(g) * u @ dn.T)
            return (acc, None)
        out, _ = jax.lax.scan(step, jnp.zeros_like(x), (gate_up_proj, down_proj, combine.T))
        return out.reshape(B, S, H)
    x = L0_attn_x
    x = x + _L0_attn_ref(_layernorm(x, axis=-1), L0_attn_Wq, L0_attn_Wk, L0_attn_Wv, L0_attn_Wp, L0_attn_bp, L0_attn_conv_w, L0_attn_conv_b)
    x = x + _L0_ffn_ref(_layernorm(x, axis=-1), L0_ffn_weight, L0_ffn_ln_gamma, L0_ffn_ln_beta)
    x = x + _L1_attn_ref(_layernorm(x, axis=-1), L1_attn_w_qkv, L1_attn_w_out, L1_attn_b_out)
    x = x + _L1_ffn_ref(_layernorm(x, axis=-1), L1_ffn_wqkv, L1_ffn_q_scale, L1_ffn_k_scale, L1_ffn_wo, L1_ffn_ln_g, L1_ffn_ln_b, L1_ffn_w1, L1_ffn_b1, L1_ffn_w2, L1_ffn_b2)
    x = x + _L2_attn_ref(_layernorm(x, axis=-1), L2_attn_ln1_g, L2_attn_ln1_b, L2_attn_wq, L2_attn_wk, L2_attn_wv, L2_attn_wo, L2_attn_ln2_g, L2_attn_ln2_b, L2_attn_w1, L2_attn_w2)
    x = x + _L2_ffn_ref(_layernorm(x, axis=-1), L2_ffn_router_w1, L2_ffn_router_w2, L2_ffn_w1, L2_ffn_w2, L2_ffn_w3)
    x = x + _L3_attn_ref(_layernorm(x, axis=-1), L3_attn_Wq, L3_attn_bq, L3_attn_Wk, L3_attn_bk, L3_attn_Wv, L3_attn_bv, L3_attn_proj)
    x = x + _L3_ffn_ref(_layernorm(x, axis=-1), L3_ffn_gate_w, L3_ffn_gate_up_proj, L3_ffn_down_proj)
    return x

_drawn_inputs = setup_inputs


def setup_inputs(seed=0):
    import zlib

    import numpy as np

    out = dict(_drawn_inputs(seed))
    spreads = {'L0_attn_bp': (0.0, 0.1),
     'L0_attn_conv_b': (0.0, 0.1),
     'L0_ffn_ln_gamma': (1.0, 0.6),
     'L0_ffn_ln_beta': (0.0, 0.609),
     'L1_ffn_q_scale': (1.0, 0.6),
     'L1_ffn_k_scale': (1.0, 0.6),
     'L1_ffn_ln_g': (1.0, 0.6),
     'L1_ffn_ln_b': (0.0, 0.8),
     'L1_ffn_b1': (0.0, 0.8),
     'L1_ffn_b2': (0.0, 0.51),
     'L2_attn_ln1_g': (1.0, 0.6),
     'L2_attn_ln1_b': (0.0, 0.8),
     'L2_attn_ln2_g': (1.0, 0.6),
     'L2_attn_ln2_b': (0.0, 2.0)}
    factors = {'L0_attn_Wq': 5.805,
     'L1_attn_b_out': 8.0,
     'L1_ffn_wqkv': 4.215,
     'L1_ffn_wo': 4.093,
     'L1_ffn_w1': 8.0,
     'L1_ffn_w2': 7.865,
     'L2_attn_wq': 8.0,
     'L2_attn_wk': 8.0,
     'L2_attn_wv': 8.0,
     'L2_attn_wo': 8.0,
     'L2_ffn_router_w1': 8.0,
     'L2_ffn_router_w2': 8.0,
     'L2_ffn_w1': 8.0,
     'L2_ffn_w2': 8.0,
     'L2_ffn_w3': 8.0,
     'L3_attn_Wq': 30.829,
     'L3_attn_bq': 200.0,
     'L3_attn_Wk': 32.671,
     'L3_attn_bk': 200.0,
     'L3_attn_Wv': 8.0,
     'L3_attn_bv': 64.0,
     'L3_attn_proj': 8.0,
     'L3_ffn_gate_w': 8.0,
     'L3_ffn_gate_up_proj': 8.0,
     'L3_ffn_down_proj': 8.0,
     'L2_attn_w1': 3.853,
     'L2_attn_w2': 3.517}
    for name, (base, spread) in spreads.items():
        noise = np.random.default_rng([zlib.crc32(name.encode()), seed]).standard_normal(out[name].shape)
        drawn = base * np.exp(spread * noise) if base else spread * noise
        out[name] = jnp.asarray(drawn.astype(out[name].dtype))
    for name, factor in factors.items():
        out[name] = (out[name] * factor).astype(out[name].dtype)
    return out
```

```python
from contextlib import ExitStack, contextmanager

import concourse.bass as bass
from concourse import mybir

ALU = mybir.AluOpType
ACT = mybir.ActivationFunctionType
AX = mybir.AxisListType
F32 = mybir.dt.float32
BF16 = mybir.dt.bfloat16
U32 = mybir.dt.uint32

P = 128
D = 128
T = 2048
CH = 512
NC = T // CH
NT = T // P
ROUND = 12582912.0
MASKED = -3.0e38


@contextmanager
def phase(nc, sems, tiles):
    with ExitStack() as ctx:
        tag = nc.next_id()
        got_tiles = [ctx.enter_context(nc.sbuf_tensor(f"{n}_{tag}", s, d)) for n, s, d in tiles]
        got_sems = [nc.alloc_semaphore(name=f"{n}_{tag}") for n in sems.split()]
        yield (*got_sems, *got_tiles)
        nc.clear_and_free_semaphores(got_sems)
        nc.all_engine_barrier()


class Core:

    def __init__(self, nc, ctx):
        self.nc = nc

        def sb(name, shape, dt=F32):
            return ctx.enter_context(nc.sbuf_tensor(name, shape, dt))

        self.xpad = sb("xpad", [P, T + 1])
        self.xnpad = sb("xnpad", [P, T + 2])
        self.scratch = sb("scratch", [P, 4, T])
        self.s1, self.s2, self.s3, self.s4 = (self.scratch[:, n, :] for n in range(4))
        self.mats = sb("mats", [P, N_MATS, P])
        self.mean_mat = sb("mean_mat", [P, P])
        self.cols = sb("cols", [P, 4])
        self.out_stored = ctx.enter_context(nc.semaphore("out_stored"))
        self.psum = ctx.enter_context(nc.psum_tensor("psum", [P, 8 * CH], F32))

    def mat(self, name):
        return self.mats[:, MATS.index(name), :]

    def bank(self, b, n=CH, rows=P):
        return self.psum[0:rows, CH * b:CH * b + n]

    def x(self, c, rows=slice(0, P)):
        return self.xpad[rows, 1 + CH * c:1 + CH * (c + 1)]

    def xn(self, c, shift=0):
        return self.xnpad[:, 1 + shift + CH * c:1 + shift + CH * (c + 1)]

    def xn_tile(self, t):
        return self.xnpad[:, 1 + P * t:1 + P * (t + 1)]

    def eps(self, value):
        return self.cols[:, EPS.index(value):EPS.index(value) + 1]


MATS = ["ident", "heads8", "heads64", "rotate", "den", "causal"]
N_MATS = len(MATS)
EPS = [1e-5, 1e-3, 0.0]


def part(tile, c):
    return tile[:, CH * c:CH * (c + 1)]


def load(k, pairs, zero=()):
    nc = k.nc
    with phase(nc, "landed cleared", []) as (landed, cleared):
        with nc.Block() as block:
            @block.gpsimd
            def _(pool):
                for z in zero:
                    pool.memset(z, 0.0).then_inc(cleared, 1)

            @block.sync
            def _(sp):
                if zero:
                    sp.wait_ge(cleared, len(zero))
                for dst, src in pairs:
                    sp.dma_start(dst, src).then_inc(landed, 16)
                sp.wait_ge(landed, 16 * len(pairs))


def setup(k, x_t, const_mats):
    nc = k.nc
    with phase(nc, "landed cleared", []) as (landed, cleared):
        with nc.Block() as block:
            @block.sync
            def _(sp):
                sp.dma_start(k.xpad[:, 1:1 + T], x_t).then_inc(landed, 16)
                sp.dma_start(k.mats[:, :, :], const_mats).then_inc(landed, 16)
                sp.wait_ge(landed, 32)

            @block.vector
            def _(dve):
                dve.memset(k.mean_mat[:, :], 1.0 / D).then_inc(cleared, 1)
                dve.memset(k.xpad[:, 0:1], 0.0).then_inc(cleared, 1)
                dve.memset(k.xnpad[:, 0:1], 0.0).then_inc(cleared, 1)
                dve.memset(k.xnpad[:, T + 1:T + 2], 0.0).then_inc(cleared, 1)
                for n, e in enumerate(EPS):
                    dve.memset(k.cols[:, n:n + 1], e).then_inc(cleared, 1)
                dve.wait_ge(cleared, 4 + len(EPS))


def layernorm(k, src, dst, eps, gain=None, bias=None):
    nc = k.nc
    names = "mean_done centred squared var_done log_done inverted scaled normed"
    with phase(nc, names, []) as (mean_done, centred, squared, var_done, log_done, inverted, scaled, normed):
        with nc.Block() as block:
            @block.tensor
            def _(pe):
                for c in range(NC):
                    pe.matmul(k.bank(c), k.mean_mat[:, :], src(c), start=True, stop=True).then_inc(mean_done, 1)
                for c in range(NC):
                    pe.wait_ge(squared, c + 1)
                    pe.matmul(k.bank(4 + c), k.mean_mat[:, :], part(k.s2, c), start=True, stop=True)\
                        .then_inc(var_done, 1)

            @block.scalar
            def _(act):
                act.preload_act_table_set("natural_log_exp_and_others")
                for c in range(NC):
                    act.wait_ge(centred, c + 1)
                    act.activation(part(k.s2, c), part(k.s1, c), ACT.Square).then_inc(squared, 1)
                for c in range(NC):
                    act.wait_ge(var_done, c + 1)
                    act.activation(part(k.s3, c), k.bank(4 + c), ACT.Ln, bias=k.eps(eps)).then_inc(log_done, 1)
                    act.wait_ge(log_done, c + 1)
                    act.activation(part(k.s2, c), part(k.s3, c), ACT.Exp, scale=-0.5).then_inc(inverted, 1)

            @block.vector
            def _(dve):
                for c in range(NC):
                    dve.wait_ge(mean_done, c + 1)
                    dve.tensor_tensor(part(k.s1, c), src(c), k.bank(c), ALU.subtract).then_inc(centred, 1)
                for c in range(NC):
                    dve.wait_ge(inverted, c + 1)
                    dve.tensor_tensor(dst(c), part(k.s1, c), part(k.s2, c), ALU.mult).then_inc(scaled, 1)
                    if gain is not None:
                        dve.wait_ge(scaled, c + 1)
                        dve.tensor_scalar(dst(c), dst(c), gain, bias, ALU.mult, ALU.add).then_inc(normed, 1)


def project(k, jobs):
    nc = k.nc
    by = {e: [n for n, job in enumerate(jobs) if job[0] == e] for e in ("vector", "scalar")}
    with phase(nc, "product_done left_by_vector left_by_scalar", []) as (product_done, by_vector, by_scalar):
        left = {"vector": by_vector, "scalar": by_scalar}
        with nc.Block() as block:
            @block.tensor
            def _(pe):
                for n, (_, pairs, rows, cols, _) in enumerate(jobs):
                    if n >= 8:
                        e = jobs[n - 8][0]
                        pe.wait_ge(left[e], by[e].index(n - 8) + 1)
                    for i, (lhs, rhs) in enumerate(pairs):
                        mm = pe.matmul(k.bank(n % 8, cols, rows), lhs, rhs,
                                       start=(i == 0), stop=(i == len(pairs) - 1))
                    mm.then_inc(product_done, 1)

            @block.vector
            def _(dve):
                for n in by["vector"]:
                    dve.wait_ge(product_done, n + 1)
                    jobs[n][4](dve, k.bank(n % 8, jobs[n][3], jobs[n][2])).then_inc(by_vector, 1)

            @block.scalar
            def _(act):
                for n in by["scalar"]:
                    act.wait_ge(product_done, n + 1)
                    jobs[n][4](act, k.bank(n % 8, jobs[n][3], jobs[n][2])).then_inc(by_scalar, 1)


def add_to_x(k, c, bias=None):
    def leave(dve, ps):
        if bias is None:
            return dve.tensor_tensor(k.x(c), k.x(c), ps, ALU.add)
        return dve.scalar_tensor_tensor(out=k.x(c), in0=ps, scalar=bias, in1=k.x(c), op0=ALU.add, op1=ALU.add)
    return leave


def copy_out(dst):
    def leave(eng, ps):
        return eng.activation(dst, ps, ACT.Copy)
    return leave


def copy_any(dst):
    def leave(eng, ps):
        if eng.engine == mybir.EngineType.Activation:
            return eng.activation(dst, ps, ACT.Copy)
        return eng.tensor_copy(dst, ps)
    return leave


def linear_attention(k, wq, wkv, y, floor, guard):
    nc = k.nc
    units = 12
    names = "product_done low_done exp_done phi_done v_done ones_done kv_done state_done out_done den_done log_done inverse_done y_done"
    tiles = [("phi_q", [P, T], F32), ("phi_k", [P, NT, P], F32), ("v1", [P, NT, P + 1], F32),
             ("kv_state", [P, P], F32), ("z_state", [P, P], F32), ("z_col", [P, 1], F32)]
    with phase(nc, names, tiles) as (product_done, low_done, exp_done, phi_done, v_done, ones_done, kv_done,
                                     state_done, out_done, den_done, log_done, inverse_done, y_done,
                                     phi_q, phi_k, v1, kv_state, z_state, z_col):
        def views(n):
            if n < 4:
                return k.bank(n), part(k.s1, n), part(k.s2, n), part(phi_q, n)
            m = n - 4
            ps = k.bank(n % 6).rearrange("p (a b) -> p a b", a=2)[:, :, 0:P]
            lo = k.s3[:, 256 * m:256 * m + 256].rearrange("p (a b) -> p a b", a=2)
            ex = y[:, 256 * m:256 * m + 256].rearrange("p (a b) -> p a b", a=2)
            return ps, lo, ex, phi_k[:, 2 * m:2 * m + 2, :]

        with nc.Block() as block:
            @block.tensor
            def _(pe):
                for n in range(units):
                    if n >= 6:
                        pe.wait_ge(phi_done, n - 5)
                        if n - 6 >= 4:
                            pe.wait_ge(v_done, n - 6 - 3)
                    if n < 4:
                        mm = pe.matmul(k.bank(n), wq, k.xn(n), start=True, stop=True)
                    else:
                        for a in range(2):
                            mm = pe.matmul(k.bank(n % 6)[:, 256 * a:256 * a + 256], k.xn_tile(2 * (n - 4) + a), wkv,
                                           start=True, stop=True)
                    mm.then_inc(product_done, 1)
                pe.wait_ge(ones_done, 1)
                for t in range(NT):
                    pe.wait_ge(phi_done, 4 + t // 2 + 1)
                    pe.wait_ge(v_done, t // 2 + 1)
                    mm = pe.matmul(k.bank(6, P + 1), phi_k[:, t, :], v1[:, t, :], start=(t == 0), stop=(t == NT - 1))
                mm.then_inc(kv_done, 1)
                pe.wait_ge(state_done, 3)
                for c in range(NC):
                    if c >= 3:
                        pe.wait_ge(y_done, c - 2)
                    pe.matmul(k.bank(c % 3), kv_state[:, :], part(phi_q, c), start=True, stop=True)
                    pe.matmul(k.bank(3 + c % 3), z_state[:, :], part(phi_q, c), start=True, stop=True).then_inc(out_done, 1)

            @block.scalar
            def _(act):
                act.preload_act_table_set("natural_log_exp_and_others")
                for n in range(units):
                    act.wait_ge(low_done, n + 1)
                    _, lo, ex, _ = views(n)
                    act.activation(ex, lo, ACT.Exp).then_inc(exp_done, 1)
                    if n >= 4:
                        v_ps = k.bank(n % 6).rearrange("p (a b) -> p a b", a=2)[:, :, P:2 * P]
                        act.activation(v1[:, 2 * (n - 4):2 * (n - 4) + 2, 0:P], v_ps, ACT.Copy).then_inc(v_done, 1)
                for c in range(NC):
                    act.wait_ge(den_done, c + 1)
                    act.activation(part(k.s3, c), part(k.s1, c), ACT.Ln).then_inc(log_done, 1)
                    act.wait_ge(log_done, c + 1)
                    act.activation(part(k.s2, c), part(k.s3, c), ACT.Exp, scale=-1.0).then_inc(inverse_done, 1)

            @block.vector
            def _(dve):
                dve.memset(v1[:, :, P:P + 1], 1.0).then_inc(ones_done, 1)
                for n in range(units + 1):
                    if n < units:
                        dve.wait_ge(product_done, n + 1)
                        ps, lo, _, _ = views(n)
                        dve.tensor_scalar(lo, ps, 0.0, None, ALU.min).then_inc(low_done, 1)
                    if n >= 1:
                        dve.wait_ge(exp_done, n)
                        if n - 1 >= 4:
                            dve.wait_ge(v_done, n - 4)
                        ps, _, ex, phi = views(n - 1)
                        dve.scalar_tensor_tensor(out=phi, in0=ps, scalar=0.0, in1=ex, op0=ALU.max, op1=ALU.add)\
                            .then_inc(phi_done, 1)
                dve.wait_ge(kv_done, 1)
                dve.tensor_tensor(kv_state[:, :], k.bank(6, P), k.mat("heads8"), ALU.mult).then_inc(state_done, 1)
                dve.tensor_copy(z_col[:, :], k.bank(6, P + 1)[:, P:P + 1]).then_inc(state_done, 1)
                dve.wait_ge(state_done, 2)
                dve.tensor_scalar(z_state[:, :], k.mat("heads8"), z_col[:, 0:1], None, ALU.mult).then_inc(state_done, 1)
                for c in range(NC + 1):
                    if c < NC:
                        dve.wait_ge(out_done, c + 1)
                        op, bound = (ALU.max, floor) if guard is None else (ALU.add, guard)
                        dve.tensor_scalar(part(k.s1, c), k.bank(3 + c % 3), bound, None, op).then_inc(den_done, 1)
                    if c >= 1:
                        dve.wait_ge(inverse_done, c)
                        dve.tensor_tensor(part(y, c - 1), k.bank((c - 1) % 3), part(k.s2, c - 1), ALU.mult)\
                            .then_inc(y_done, 1)


def layer0_attention(k, A):
    nc = k.nc
    with ExitStack() as ctx:
        w = ctx.enter_context(nc.sbuf_tensor("w_l0a", [P, 4, P], F32))
        vec = ctx.enter_context(nc.sbuf_tensor("vec_l0a", [P, 5], F32))
        y = ctx.enter_context(nc.sbuf_tensor("y_l0a", [P, T], F32))
        load(k, [(w[:, n, :], A[name]) for n, name in enumerate(
            ("L0_attn_WqT", "L0_attn_WkT", "L0_attn_WvT", "L0_attn_WpT"))]
            + [(vec[:, 0:3], A["L0_attn_conv_w"]), (vec[:, 3:4], A["L0_attn_conv_b"]), (vec[:, 4:5], A["L0_attn_bp"])])
        layernorm(k, k.x, k.xn, 1e-5)
        linear_attention(k, w[:, 0, :], w[:, 1:3, :].rearrange("p a b -> p (a b)"), y, 1e-6, None)
        with phase(nc, "middle_done step_done", []) as (middle_done, step_done):
            with nc.Block() as block:
                @block.scalar
                def _(act):
                    for c in range(NC):
                        act.activation(part(k.s1, c), k.xn(c), ACT.Identity, scale=vec[:, 1:2], bias=vec[:, 3:4])\
                            .then_inc(middle_done, 1)

                @block.vector
                def _(dve):
                    for c in range(NC):
                        dve.scalar_tensor_tensor(out=part(y, c), in0=k.xn(c, -1), scalar=vec[:, 0:1], in1=part(y, c),
                                                 op0=ALU.mult, op1=ALU.add).then_inc(step_done, 1)
                        dve.wait_ge(step_done, 3 * c + 1)
                        dve.scalar_tensor_tensor(out=part(y, c), in0=k.xn(c, 1), scalar=vec[:, 2:3], in1=part(y, c),
                                                 op0=ALU.mult, op1=ALU.add).then_inc(step_done, 1)
                        dve.wait_ge(step_done, 3 * c + 2)
                        dve.wait_ge(middle_done, c + 1)
                        dve.tensor_tensor(part(y, c), part(y, c), part(k.s1, c), ALU.add).then_inc(step_done, 1)
        project(k, [("vector", [(w[:, 3, :], part(y, c))], P, CH, add_to_x(k, c, vec[:, 4:5])) for c in range(NC)])


def layer0_ffn(k, A):
    nc = k.nc
    QB, QEPS = 128.0, 1e-5
    with ExitStack() as ctx:
        w = ctx.enter_context(nc.sbuf_tensor("w_l0f", [P, P], F32))
        wq = ctx.enter_context(nc.sbuf_tensor("wq_l0f", [P, P], F32))
        vec = ctx.enter_context(nc.sbuf_tensor("vec_l0f", [P, 2], F32))
        st = ctx.enter_context(nc.sbuf_tensor("st_l0f", [P, 8], F32))
        load(k, [(w[:, :], A["L0_ffn_weight"]), (vec[:, 0:1], A["L0_ffn_ln_gamma"]), (vec[:, 1:2], A["L0_ffn_ln_beta"])])
        layernorm(k, k.x, k.xn, 1e-5)
        layernorm(k, k.xn, k.xn, 1e-3, vec[:, 0:1], vec[:, 1:2])
        with phase(nc, "step all_max beta_done", []) as (step, all_max, beta_done):
            with nc.Block() as block:
                @block.tensor
                def _(pe):
                    pe.wait_ge(step, 2)
                    pe.matmul(k.bank(0, 1), k.mean_mat[:, :], st[:, 0:1], start=True, stop=True).then_inc(beta_done, 1)

                @block.gpsimd
                def _(pool):
                    pool.wait_ge(step, 1)
                    pool.partition_all_reduce(st[:, 2:3], st[:, 1:2], P, bass.bass_isa.ReduceOp.max).then_inc(all_max, 1)

                @block.vector
                def _(dve):
                    n = 0

                    def then(ins):
                        ins.then_inc(step, 1)

                    then(dve.tensor_reduce(st[:, 1:2], k.xnpad[:, 1:1 + T], AX.X, ALU.max, apply_absolute_value=True))
                    then(dve.tensor_reduce(st[:, 0:1], w[:, :], AX.X, ALU.add, apply_absolute_value=True))
                    dve.wait_ge(beta_done, 1)
                    then(dve.tensor_scalar(st[:, 3:4], k.bank(0, 1), 1.0 / D, None, ALU.mult))
                    dve.wait_ge(step, 3)
                    then(dve.tensor_scalar(st[:, 4:5], st[:, 3:4], QEPS, None, ALU.add))
                    dve.wait_ge(step, 4)
                    then(dve.reciprocal(st[:, 5:6], st[:, 4:5]))
                    dve.wait_ge(step, 5)
                    then(dve.tensor_scalar(wq[:, :], w[:, :], st[:, 5:6], ROUND, ALU.mult, ALU.add))
                    dve.wait_ge(step, 6)
                    then(dve.tensor_scalar(wq[:, :], wq[:, :], ROUND, 1.0, ALU.subtract, ALU.min))
                    dve.wait_ge(step, 7)
                    then(dve.tensor_scalar(wq[:, :], wq[:, :], -1.0, None, ALU.max))
                    dve.wait_ge(all_max, 1)
                    then(dve.reciprocal(st[:, 6:7], st[:, 2:3]))
                    dve.wait_ge(step, 9)
                    then(dve.tensor_scalar(st[:, 6:7], st[:, 6:7], QB, None, ALU.mult))
                    then(dve.tensor_scalar(st[:, 7:8], st[:, 3:4], st[:, 2:3], 1.0 / QB, ALU.mult, ALU.mult))
                    dve.wait_ge(step, 11)
                    xn = k.xnpad[:, 1:1 + T]
                    then(dve.tensor_scalar(xn, xn, st[:, 6:7], QB - QEPS, ALU.mult, ALU.min))
                    dve.wait_ge(step, 12)
                    then(dve.tensor_scalar(xn, xn, QEPS - QB, None, ALU.max))

        def scaled(c):
            def leave(dve, ps):
                return dve.scalar_tensor_tensor(out=k.x(c), in0=ps, scalar=st[:, 7:8], in1=k.x(c),
                                                op0=ALU.mult, op1=ALU.add)
            return leave
        project(k, [("vector", [(wq[:, :], k.xn(c))], P, CH, scaled(c)) for c in range(NC)])


def lookup_ffn(k, w1, w2, hidden):
    nc = k.nc
    tiles = [("raw", [P, 2, CH], F32), ("low", [P, 2, CH], F32), ("grid", [P, 2, CH], F32), ("h", [P, NC, hidden, CH], F32)]
    with phase(nc, "product_done rounded lowered gridded acted out_done added", tiles) as (
            product_done, rounded, lowered, gridded, acted, out_done, added, raw, low, grid, h):
        units = [(c, j) for c in range(NC) for j in range(hidden)]
        with nc.Block() as block:
            @block.tensor
            def _(pe):
                for n, (c, j) in enumerate(units):
                    if n >= 4:
                        pe.wait_ge(rounded, n - 3)
                    pe.matmul(k.bank(n % 4), w1[:, P * j:P * (j + 1)], k.xn(c), start=True, stop=True).then_inc(product_done, 1)
                for c in range(NC):
                    for j in range(hidden):
                        pe.wait_ge(acted, hidden * c + j + 1)
                        mm = pe.matmul(k.bank(4 + c), w2[:, j, :], h[:, c, j, :], start=(j == 0), stop=(j == hidden - 1))
                    mm.then_inc(out_done, 1)

            @block.vector
            def _(dve):
                for n in range(len(units)):
                    dve.wait_ge(product_done, n + 1)
                    dve.tensor_scalar(raw[:, n % 2, :], k.bank(n % 4), 10.0, ROUND, ALU.mult, ALU.add).then_inc(rounded, 1)
                    dve.wait_ge(rounded, n + 1)
                    dve.tensor_scalar(low[:, n % 2, :], raw[:, n % 2, :], ROUND, -128.0, ALU.subtract, ALU.max).then_inc(lowered, 1)
                    dve.wait_ge(lowered, n + 1)
                    if n >= 2:
                        dve.wait_ge(acted, n - 1)
                    dve.tensor_scalar(grid[:, n % 2, :], low[:, n % 2, :], 127.0, 0.1, ALU.min, ALU.mult).then_inc(gridded, 1)
                for c in range(NC):
                    dve.wait_ge(out_done, c + 1)
                    dve.tensor_tensor(k.x(c), k.x(c), k.bank(4 + c), ALU.add).then_inc(added, 1)

            @block.scalar
            def _(act):
                for n, (c, j) in enumerate(units):
                    act.wait_ge(gridded, n + 1)
                    act.activation(h[:, c, j, :], grid[:, n % 2, :], ACT.Gelu_apprx_tanh).then_inc(acted, 1)


def layer2_attention(k, A):
    nc = k.nc
    with ExitStack() as ctx:
        w = ctx.enter_context(nc.sbuf_tensor("w_l2a", [P, 4, P], F32))
        w1 = ctx.enter_context(nc.sbuf_tensor("w1_l2a", [P, 512], F32))
        w2 = ctx.enter_context(nc.sbuf_tensor("w2_l2a", [P, 4, P], F32))
        vec = ctx.enter_context(nc.sbuf_tensor("vec_l2a", [P, 4], F32))
        y = ctx.enter_context(nc.sbuf_tensor("y_l2a", [P, T], F32))
        load(k, [(w[:, n, :], A["L2_attn_" + name]) for n, name in enumerate(("wq", "wk", "wv", "wo"))]
             + [(vec[:, n:n + 1], A["L2_attn_" + name]) for n, name in enumerate(("ln1_g", "ln1_b", "ln2_g", "ln2_b"))]
             + [(w1[:, :], A["L2_attn_w1"]), (w2[:, :, :], A["L2_attn_w2"].rearrange("(j p) d -> p j d", p=P))])
        z = ctx.enter_context(nc.sbuf_tensor("z_l2a", [P, T], F32))

        def z_part(c):
            return part(z, c)

        layernorm(k, k.x, z_part, 1e-5)
        layernorm(k, z_part, k.xn, 1e-5, vec[:, 0:1], vec[:, 1:2])
        linear_attention(k, w[:, 0, :], w[:, 1:3, :].rearrange("p a b -> p (a b)"), y, None, 1e-6)
        project(k, [("vector", [(w[:, 3, :], part(y, c))], P, CH, lambda dve, ps, c=c: dve.tensor_tensor(
            z_part(c), z_part(c), ps, ALU.add)) for c in range(NC)])
        layernorm(k, z_part, k.xn, 1e-5, vec[:, 2:3], vec[:, 3:4])
        add_tile(k, z[:, :])
        lookup_ffn(k, w1, w2, 4)


def add_tile(k, tile):
    nc = k.nc
    with phase(nc, "added", []) as (added,):
        with nc.Block() as block:
            @block.vector
            def _(dve):
                dve.tensor_tensor(k.xpad[:, 1:1 + T], k.xpad[:, 1:1 + T], tile, ALU.add).then_inc(added, 1)


def store(k, out):
    with k.nc.Block() as block:
        @block.sync
        def _(sp):
            sp.dma_start(out, k.xpad[:, 1:1 + T]).then_inc(k.out_stored, 16)
            sp.wait_ge(k.out_stored, 16)


def split_into_bf16(k, qk_w, rope, pieces):
    nc = k.nc
    units = [(m, c) for m in range(2) for c in range(NC)]
    names = "straight_done turned_done by_cos by_sin rotated high_done rest_done middle_done low_done"
    tiles = [("cos_part", [P, 2, CH], F32), ("sin_part", [P, 2, CH], F32), ("value", [P, 2, CH], F32), ("rest", [P, 2, CH], F32)]
    with phase(nc, names, tiles) as (straight_done, turned_done, by_cos, by_sin, rotated, high_done, rest_done, middle_done,
                                     low_done, cos_part, sin_part, value, rest):
        with nc.Block() as block:
            @block.tensor
            def _(pe):
                for n, (m, c) in enumerate(units):
                    if n >= 2:
                        pe.wait_ge(by_cos, n - 1)
                        pe.wait_ge(by_sin, n - 1)
                    pe.matmul(k.bank(n % 2), qk_w[:, 2 * m, :], k.xn(c), start=True, stop=True).then_inc(straight_done, 1)
                    pe.matmul(k.bank(2 + n % 2), qk_w[:, 2 * m + 1, :], k.xn(c), start=True, stop=True).then_inc(turned_done, 1)

            @block.vector
            def _(dve):
                for n, (m, c) in enumerate(units):
                    dve.wait_ge(straight_done, n + 1)
                    dve.tensor_tensor(cos_part[:, n % 2, :], k.bank(n % 2), part(rope[:, 0, :], c), ALU.mult).then_inc(by_cos, 1)
                    dve.wait_ge(turned_done, n + 1)
                    dve.tensor_tensor(sin_part[:, n % 2, :], k.bank(2 + n % 2), part(rope[:, 1, :], c), ALU.mult)\
                        .then_inc(by_sin, 1)
                    dve.wait_ge(by_cos, n + 1)
                    dve.wait_ge(by_sin, n + 1)
                    if n >= 2:
                        dve.wait_ge(high_done, n - 1)
                    dve.tensor_tensor(value[:, n % 2, :], cos_part[:, n % 2, :], sin_part[:, n % 2, :], ALU.add).then_inc(rotated, 1)
                    dve.wait_ge(high_done, n + 1)
                    if n >= 2:
                        dve.wait_ge(middle_done, n - 1)
                    dve.tensor_tensor(rest[:, n % 2, :], value[:, n % 2, :], pieces[:, m, 0, CH * c:CH * (c + 1)], ALU.subtract)\
                        .then_inc(rest_done, 1)
                    dve.wait_ge(middle_done, n + 1)
                    dve.tensor_tensor(pieces[:, m, 2, CH * c:CH * (c + 1)], rest[:, n % 2, :],
                                      pieces[:, m, 1, CH * c:CH * (c + 1)], ALU.subtract).then_inc(low_done, 1)

            @block.scalar
            def _(act):
                for n, (m, c) in enumerate(units):
                    act.wait_ge(rotated, n + 1)
                    act.activation(pieces[:, m, 0, CH * c:CH * (c + 1)], value[:, n % 2, :], ACT.Copy).then_inc(high_done, 1)
                    act.wait_ge(rest_done, n + 1)
                    act.activation(pieces[:, m, 1, CH * c:CH * (c + 1)], rest[:, n % 2, :], ACT.Copy).then_inc(middle_done, 1)


def softmax_schedule():
    order = []
    units = 4 * NT * NC
    steps = NC * NT * 2
    order += [("top", 0, u) for u in range(units)] + [("close", 0, 0)]
    for g in range(4):
        done = 0
        for m in range(steps):
            order.append(("step", g, m))
            if g < 3 and m >= 16:
                upto = min(units, (m - 15) * units // (steps - 24))
                order += [("top", g + 1, u) for u in range(done, upto)]
                if upto == units and done < units:
                    order.append(("close", g + 1, 0))
                done = upto
    return order


def grouped_attention(k, pieces_dram, v_pad, mixed_heads):
    nc = k.nc
    order = softmax_schedule()
    R = 72
    units, steps = 4 * NT * NC, NC * NT * 2
    names = ("ones_set loaded_even loaded_odd top_scored top_found closed turned high_done rest_done middle_done low_done laid_out scored "
             "exped mixed emptied")
    tiles = [("qs", [P, 2, 4, T], BF16), ("ks", [P, 2, 4, T], BF16), ("probs_t", [P, 4, 2 * CH], F32),
             ("tops", [P, 4 * NT, NC], F32), ("neg_max", [P, 4 * NT], F32), ("max_pieces", [4 * NT, 3, P], BF16),
             ("rest", [4 * NT, P], F32)]
    with phase(nc, names, tiles) as (ones_set, loaded_even, loaded_odd, top_scored, top_found, closed, turned, high_done, rest_done, middle_done,
                                     low_done, laid_out, scored, exped, mixed, emptied, qs, ks, probs_t, tops, neg_max,
                                     max_pieces, rest):
        loaded = (loaded_even, loaded_odd)

        def top_number(g, u):
            return units * g + u

        with nc.Block() as block:
            @block.gpsimd
            def _(pool):
                pool.memset(ks[64:96, :, :, :].rearrange("p a b t -> p (a b t)"), 1.0).then_inc(ones_set, 1)

            @block.sync
            def _(sp):
                def load_group(g):
                    if g >= 2:
                        sp.wait_ge(scored, steps * (g - 1))
                    for j in range(4):
                        h = 4 * g + j
                        for a in range(3):
                            q_src = pieces_dram[0, a, 8 * h:8 * h + 8, :].unsqueeze(0).to_broadcast([3, 8, T])
                            sp.dma_start(qs[24 * a:24 * a + 24, g % 2, j, :], q_src).then_inc(loaded[g % 2], 16)
                            sp.dma_start(ks[24 * a:24 * a + 24, g % 2, j, :], pieces_dram[1, :, 8 * h:8 * h + 8, :])\
                                .then_inc(loaded[g % 2], 16)

                def lay_out(g):
                    sp.wait_ge(low_done, g + 1)
                    for a in range(3):
                        dst = qs[R + a:R + a + 1, g % 2, :, :].rearrange("p j (t q) -> p (j t) q", q=P)
                        sp.dma_start(dst, max_pieces[:, a, :]).then_inc(laid_out, 16)

                sp.wait_ge(ones_set, 1)
                load_group(0)
                load_group(1)
                lay_out(0)
                for g in range(1, 4):
                    lay_out(g)
                    if g + 1 < 4:
                        load_group(g + 1)
                sp.wait_ge(laid_out, 48 * 4)

            @block.tensor
            def _(pe):
                def mix(g, m):
                    qc, kt, pair = m // (2 * NT), m // 2 % NT, m % 2
                    pe.wait_ge(exped, steps * g + m + 1)
                    if kt == 0 and pair == 0 and NC * g + qc >= 2:
                        pe.wait_ge(emptied, NC * g + qc - 1)
                    for i in range(2):
                        j = 2 * pair + i
                        mm = pe.matmul(k.bank(6 + qc % 2)[32 * j:32 * j + 32, :],
                                       v_pad[:, kt, 4 * g + j, :], probs_t[:, m % 4, CH * i:CH * (i + 1)],
                                       start=(kt == 0), stop=(kt == NT - 1))
                    mm.then_inc(mixed, 1)

                for kind, g, m in order:
                    if kind == "top":
                        n = top_number(g, m)
                        j, t, c = m // (NT * NC), m // NC % NT, m % NC
                        if m == 0:
                            pe.wait_ge(loaded[g % 2], 16 * 24 * (g // 2 + 1))
                        if n >= 2:
                            pe.wait_ge(top_found, n - 1)
                        if m == 0 and g >= 1:
                            pe.wait_ge(low_done, g)
                        pe.matmul(k.bank(4 + n % 2), qs[0:R, g % 2, j, P * t:P * (t + 1)], ks[0:R, g % 2, j, CH * c:CH * (c + 1)],
                                  start=True, stop=True).then_inc(top_scored, 1)
                    elif kind == "close":
                        pe.wait_ge(closed, g + 1)
                        pe.transpose(k.bank(4, P, 4 * NT), neg_max[:, :], k.mat("ident")).then_inc(turned, 1)
                    else:
                        qc, kt, pair = m // (2 * NT), m // 2 % NT, m % 2
                        if m == 0:
                            pe.wait_ge(laid_out, 48 * (g + 1))
                        if steps * g + m >= 2:
                            pe.wait_ge(exped, steps * g + m - 1)
                        for i in range(2):
                            j = 2 * pair + i
                            mm = pe.matmul(k.bank(2 * (m % 2) + i), ks[0:R + 3, g % 2, j, P * kt:P * (kt + 1)],
                                           qs[0:R + 3, g % 2, j, CH * qc:CH * (qc + 1)], start=True, stop=True)
                        mm.then_inc(scored, 1)
                        if m % 2 and m >= 3:
                            mix(g, m - 3)
                            mix(g, m - 2)
                        if m == steps - 1:
                            mix(g, m - 1)
                            mix(g, m)

            @block.scalar
            def _(act):
                for kind, g, m in order:
                    if kind != "step":
                        continue
                    n = steps * g + m
                    act.wait_ge(scored, n + 1)
                    if n >= 4:
                        act.wait_ge(mixed, n - 3)
                    act.activation(probs_t[:, m % 4, :], k.psum[:, 2 * CH * (m % 2):2 * CH * (m % 2) + 2 * CH], ACT.Exp,
                                   scale=8.0 ** -0.5).then_inc(exped, 1)

            @block.vector
            def _(dve):
                def empty(g, qc):
                    dve.wait_ge(mixed, steps * g + 2 * NT * (qc + 1))
                    dve.tensor_copy(mixed_heads[:, g, CH * qc:CH * (qc + 1)], k.bank(6 + qc % 2)).then_inc(emptied, 1)

                for kind, g, m in order:
                    if kind == "top":
                        n = top_number(g, m)
                        dve.wait_ge(top_scored, n + 1)
                        dve.tensor_reduce(tops[:, m // NC, m % NC:m % NC + 1], k.bank(4 + n % 2), AX.X, ALU.max)\
                            .then_inc(top_found, 1)
                    elif kind == "close":
                        dve.wait_ge(top_found, units * (g + 1))
                        dve.tensor_reduce(neg_max[:, :], tops[:, :, :], AX.X, ALU.max, negate=True).then_inc(closed, 1)
                        dve.wait_ge(turned, g + 1)
                        if g >= 1:
                            dve.wait_ge(laid_out, 48 * g)
                        row = k.bank(4, P, 4 * NT)
                        dve.tensor_copy(max_pieces[:, 0, :], row).then_inc(high_done, 1)
                        dve.wait_ge(high_done, g + 1)
                        dve.tensor_tensor(rest[:, :], row, max_pieces[:, 0, :], ALU.subtract).then_inc(rest_done, 1)
                        dve.wait_ge(rest_done, g + 1)
                        dve.tensor_copy(max_pieces[:, 1, :], rest[:, :]).then_inc(middle_done, 1)
                        dve.wait_ge(middle_done, g + 1)
                        dve.tensor_tensor(max_pieces[:, 2, :], rest[:, :], max_pieces[:, 1, :], ALU.subtract).then_inc(low_done, 1)
                    elif m % (2 * NT) == 3 and m > 3:
                        empty(g, m // (2 * NT) - 1)
                    elif m == steps - 1:
                        empty(g, NC - 1)


def layer1_attention(k, A):
    nc = k.nc
    with ExitStack() as ctx:
        def sb(name, shape, dt=F32):
            return ctx.enter_context(nc.sbuf_tensor(name + "_l1a", shape, dt))

        qk_w, v_w, out_w, bias = sb("qk_w", [P, 4, P]), sb("v_w", [P, P]), sb("out_w", [P, 4, P]), sb("bias", [P, 1])
        mixed_heads = sb("mixed_heads", [P, 4, T])
        v_pad = k.scratch[:, :, :].rearrange("p a b -> p (a b)").rearrange("p (t h e) -> p t h e", t=NT, h=16)
        pieces_dram = nc.dram_tensor("pieces_dram", (2, 3, P, T), BF16).ap()
        out_rows = [(out_w[32 * j:32 * j + 8, g, :], A["L1_attn_outT"][8 * (4 * g + j):8 * (4 * g + j) + 8, :])
                    for g in range(4) for j in range(4)]
        load(k, [(qk_w[:, :, :], A["L1_attn_qkT"]), (v_w[:, :], A["L1_attn_vT"]), (bias[:, :], A["L1_attn_b_out"])] + out_rows,
             zero=[out_w[:, :, :]])
        layernorm(k, k.x, k.xn, 1e-5)
        with nc.sbuf_tensor("rope_l1a", [P, 2, T], F32) as rope, nc.sbuf_tensor("pieces_l1a", [P, 2, 3, T], BF16) as pieces:
            load(k, [(rope[:, :, :], A["const_rope"])])
            split_into_bf16(k, qk_w, rope, pieces)
            load(k, [(pieces_dram[m].rearrange("a p t -> p a t"), pieces[:, m, :, :]) for m in range(2)],
                 zero=[k.scratch[:, :, :]])
        project(k, [("vector" if t % 2 else "scalar", [(k.xn_tile(t), v_w[:, :])], P, P, copy_heads(v_pad[:, t, :, 0:8]))
                    for t in range(NT)])
        with phase(nc, "ones_set", []) as (ones_set,):
            with nc.Block() as block:
                @block.vector
                def _(dve):
                    dve.memset(v_pad[:, :, :, 8:9].rearrange("p t h e -> p t (h e)"), 1.0).then_inc(ones_set, 1)
        grouped_attention(k, pieces_dram, v_pad, mixed_heads)

        with phase(nc, "spread log_done inverted divided", [("log", [P, 2, CH], F32), ("inv", [P, 2, CH], F32)]) as (
                spread, log_done, inverted, divided, log, inv):
            units = [(g, c) for g in range(4) for c in range(NC)]
            with nc.Block() as block:
                @block.tensor
                def _(pe):
                    for n, (g, c) in enumerate(units):
                        if n >= 4:
                            pe.wait_ge(log_done, n - 3)
                        pe.matmul(k.bank(n % 4), k.mat("den"), part(mixed_heads[:, g, :], c), start=True, stop=True)\
                            .then_inc(spread, 1)

                @block.scalar
                def _(act):
                    act.preload_act_table_set("natural_log_exp_and_others")
                    for n in range(len(units)):
                        act.wait_ge(spread, n + 1)
                        if n >= 2:
                            act.wait_ge(inverted, n - 1)
                        act.activation(log[:, n % 2, :], k.bank(n % 4), ACT.Ln).then_inc(log_done, 1)
                        act.wait_ge(log_done, n + 1)
                        if n >= 2:
                            act.wait_ge(divided, n - 1)
                        act.activation(inv[:, n % 2, :], log[:, n % 2, :], ACT.Exp, scale=-1.0).then_inc(inverted, 1)

                @block.vector
                def _(dve):
                    for n, (g, c) in enumerate(units):
                        dve.wait_ge(inverted, n + 1)
                        u = part(mixed_heads[:, g, :], c)
                        dve.tensor_tensor(u, u, inv[:, n % 2, :], ALU.mult).then_inc(divided, 1)
        project(k, [("vector", [(out_w[:, g, :], part(mixed_heads[:, g, :], c)) for g in range(4)], P, CH,
                     add_to_x(k, c, bias[:, 0:1])) for c in range(NC)])


def copy_heads(dst):
    def leave(eng, ps):
        ps = ps.rearrange("p (h e) -> p h e", e=8)
        if eng.engine == mybir.EngineType.Activation:
            return eng.activation(dst, ps, ACT.Copy)
        return eng.tensor_copy(dst, ps)
    return leave


def shifted_tokens(k, src_pad, h, n_chunks=NC):
    nc = k.nc
    with phase(nc, "low_copied high_copied", []) as (low_copied, high_copied):
        with nc.Block() as block:
            @block.vector
            def _(dve):
                dve.tensor_copy(h[0:64, :], src_pad[0:64, 1:1 + T]).then_inc(low_copied, 1)

            @block.scalar
            def _(act):
                act.activation(h[64:P, :], src_pad[64:P, 0:T], ACT.Copy).then_inc(high_copied, 1)


def window_qk(k, h, w_qk, scales, xpos, qk):
    nc = k.nc
    units = [(m, c) for m in range(8) for c in range(NC)]
    names = "projected squared summed rooted floored inverted normed turned by_cos by_sin rotated"
    tiles = [("sq", [P, 2, CH], F32), ("root", [P, 2, CH], F32), ("inv", [P, 2, CH], F32), ("qn", [P, 2, CH], F32),
             ("cos_part", [P, 2, CH], F32), ("sin_part", [P, 2, CH], F32)]
    with phase(nc, names, tiles) as (projected, squared, summed, rooted, floored, inverted, normed, turned, by_cos, by_sin,
                                     rotated, sq, root, inv, qn, cos_part, sin_part):
        with nc.Block() as block:
            @block.tensor
            def _(pe):
                for n in range(len(units) + 2):
                    if n < len(units):
                        m, c = units[n]
                        if n >= 3:
                            pe.wait_ge(normed, n - 2)
                        pe.matmul(k.bank(n % 3), w_qk[:, P * m:P * (m + 1)], part(h, c), start=True, stop=True)\
                            .then_inc(projected, 1)
                    if 1 <= n <= len(units):
                        u = n - 1
                        pe.wait_ge(squared, u + 1)
                        if u >= 2:
                            pe.wait_ge(rooted, u - 1)
                        pe.matmul(k.bank(3 + u % 2), k.mat("heads64"), sq[:, u % 2, :], start=True, stop=True)\
                            .then_inc(summed, 1)
                    if n >= 2:
                        u = n - 2
                        pe.wait_ge(normed, u + 1)
                        if u >= 2:
                            pe.wait_ge(by_sin, u - 1)
                        pe.matmul(k.bank(5 + u % 2), k.mat("rotate"), qn[:, u % 2, :], start=True, stop=True)\
                            .then_inc(turned, 1)

            @block.scalar
            def _(act):
                for n in range(len(units)):
                    act.wait_ge(projected, n + 1)
                    if n >= 2:
                        act.wait_ge(summed, n - 1)
                    act.activation(sq[:, n % 2, :], k.bank(n % 3), ACT.Square).then_inc(squared, 1)
                    act.wait_ge(summed, n + 1)
                    if n >= 2:
                        act.wait_ge(inverted, n - 1)
                    act.activation(root[:, n % 2, :], k.bank(3 + n % 2), ACT.Sqrt).then_inc(rooted, 1)

            @block.gpsimd
            def _(pool):
                for n, (m, c) in enumerate(units):
                    pool.wait_ge(normed, n + 1)
                    if n >= 2:
                        pool.wait_ge(rotated, n - 1)
                    pool.tensor_tensor(cos_part[:, n % 2, :], qn[:, n % 2, :], part(xpos[:, 2 * (m // 4), :], c), ALU.mult)\
                        .then_inc(by_cos, 1)

            @block.vector
            def _(dve):
                for n in range(len(units) + 1):
                    if n < len(units):
                        m, c = units[n]
                        dve.wait_ge(rooted, n + 1)
                        dve.tensor_scalar(root[:, n % 2, :], root[:, n % 2, :], 1e-12, None, ALU.max).then_inc(floored, 1)
                        dve.wait_ge(floored, n + 1)
                        dve.reciprocal(inv[:, n % 2, :], root[:, n % 2, :]).then_inc(inverted, 1)
                        dve.wait_ge(inverted, n + 1)
                        if n >= 2:
                            dve.wait_ge(turned, n - 1)
                            dve.wait_ge(by_cos, n - 1)
                        dve.scalar_tensor_tensor(out=qn[:, n % 2, :], in0=k.bank(n % 3), scalar=scales[:, m // 4:m // 4 + 1],
                                                 in1=inv[:, n % 2, :], op0=ALU.mult, op1=ALU.mult).then_inc(normed, 1)
                    if n >= 1:
                        u = n - 1
                        m, c = units[u]
                        dve.wait_ge(turned, u + 1)
                        dve.tensor_tensor(sin_part[:, u % 2, :], k.bank(5 + u % 2), part(xpos[:, 2 * (m // 4) + 1, :], c),
                                          ALU.mult).then_inc(by_sin, 1)
                        dve.wait_ge(by_sin, u + 1)
                        dve.wait_ge(by_cos, u + 1)
                        dve.tensor_tensor(part(qk[:, m, P:P + T], c), sin_part[:, u % 2, :], cos_part[:, u % 2, :], ALU.add)\
                            .then_inc(rotated, 1)


SLOTS = [0, 2, 1, 3]


def window_attention(k, qk, v, bands, o):
    nc = k.nc
    units = [(t, g) for t in range(NT) for g in range(2)]
    names = "scored masked max_done exp_done inverted scaled transposed copied_low copied_high mixed out_done"
    tiles = [("s", [P, 2, 4, 2 * P], F32), ("neg_max", [P, 2, 4], F32), ("total", [P, 2, 4], F32), ("inv", [P, 2, 4], F32),
             ("probs_t", [P, 2, 8, P], F32)]
    with phase(nc, names, tiles) as (scored, masked, max_done, exp_done, inverted, scaled, transposed, copied_low,
                                     copied_high, mixed, out_done, s, neg_max, total, inv, probs_t):
        def scores(n):
            return k.psum[:, 2 * CH * (n % 2):2 * CH * (n % 2) + 2 * CH].rearrange("p (h j) -> p h j", h=4)

        with nc.Block() as block:
            @block.tensor
            def _(pe):
                for n in range(len(units) + 1):
                    if n < len(units):
                        t, g = units[n]
                        if n >= 2:
                            pe.wait_ge(masked, n - 1)
                        for i in range(4):
                            m, r = 2 * g + i // 2, 64 * (i % 2)
                            mm = pe.matmul(scores(n)[:, SLOTS.index(i), :], qk[r:r + 64, m, P + P * t:P + P * (t + 1)],
                                           qk[r:r + 64, 4 + m, P * t:P * t + 2 * P], start=True, stop=True)
                        mm.then_inc(scored, 1)
                    if n >= 1:
                        u = n - 1
                        t, g = units[u]
                        pe.wait_ge(scaled, u + 1)
                        if u >= 1:
                            pe.wait_ge(copied_low, u)
                            pe.wait_ge(copied_high, u)
                        for i in range(4):
                            for b in range(2):
                                a = 2 * i + b
                                mm = pe.transpose(k.bank(4 + a // 4)[:, P * (a % 4):P * (a % 4 + 1)],
                                                  s[:, u % 2, i, P * b:P * (b + 1)], k.mat("ident"))
                        mm.then_inc(transposed, 1)
                        pe.wait_ge(copied_low, u + 1)
                        pe.wait_ge(copied_high, u + 1)
                        if u >= 2:
                            pe.wait_ge(out_done, u - 1)
                        for slot, i in enumerate(SLOTS):
                            r = 64 * (i % 2)
                            for b in range(2):
                                mm = pe.matmul(k.bank(6 + u % 2)[r:r + 64, P * (i // 2):P * (i // 2 + 1)],
                                               v[:, t + b, 64 * (4 * g + i):64 * (4 * g + i + 1)],
                                               probs_t[:, u % 2, 2 * slot + b, :], start=(b == 0), stop=(b == 1))
                        mm.then_inc(mixed, 1)

            @block.vector
            def _(dve):
                for n in range(len(units) + 1):
                    if n < len(units):
                        t, g = units[n]
                        dve.wait_ge(scored, n + 1)
                        if n >= 2:
                            dve.wait_ge(transposed, n - 1)
                        mask = bands[:, min(t, 1), :].unsqueeze(1).to_broadcast([P, 4, 2 * P])
                        dve.tensor_tensor(s[:, n % 2, :, :], scores(n), mask, ALU.add).then_inc(masked, 1)
                        dve.wait_ge(masked, n + 1)
                        dve.tensor_reduce(neg_max[:, n % 2, :], s[:, n % 2, :, :], AX.X, ALU.max, negate=True)\
                            .then_inc(max_done, 1)
                    if n >= 1:
                        u = n - 1
                        dve.wait_ge(exp_done, u + 1)
                        dve.reciprocal(inv[:, u % 2, :], total[:, u % 2, :]).then_inc(inverted, 1)
                        dve.wait_ge(transposed, u + 1)
                        if u >= 2:
                            dve.wait_ge(mixed, u - 1)
                        dve.tensor_copy(probs_t[:, u % 2, 0:4, :].rearrange("p a b -> p (a b)"), k.bank(4)).then_inc(copied_low, 1)

            @block.gpsimd
            def _(pool):
                for n in range(len(units)):
                    pool.wait_ge(inverted, n + 1)
                    share = inv[:, n % 2, :].unsqueeze(2).to_broadcast([P, 4, 2 * P])
                    pool.tensor_tensor(s[:, n % 2, :, :], s[:, n % 2, :, :], share, ALU.mult).then_inc(scaled, 1)

            @block.scalar
            def _(act):
                for n in range(len(units) + 1):
                    if n < len(units):
                        act.wait_ge(max_done, n + 1)
                        if n >= 2:
                            act.wait_ge(inverted, n - 1)
                        for i in range(4):
                            ins = act.activation(s[:, n % 2, i, :], s[:, n % 2, i, :], ACT.Exp, bias=neg_max[:, n % 2, i:i + 1],
                                                 accum_out=total[:, n % 2, i:i + 1])
                        ins.then_inc(exp_done, 1)
                    if n >= 1:
                        u = n - 1
                        t, g = units[u]
                        act.wait_ge(transposed, u + 1)
                        if u >= 2:
                            act.wait_ge(mixed, u - 1)
                        act.activation(probs_t[:, u % 2, 4:8, :].rearrange("p a b -> p (a b)"), k.bank(5), ACT.Copy)\
                            .then_inc(copied_high, 1)
                        act.wait_ge(mixed, u + 1)
                        act.activation(o[:, 2 * g:2 * g + 2, P * t:P * (t + 1)],
                                       k.bank(6 + u % 2, 2 * P).rearrange("p (a b) -> p a b", a=2), ACT.Copy).then_inc(out_done, 1)


def gated_ffn(k, xn, w1, b1, w2, b2, z, hidden):
    nc = k.nc
    rows = [min(P, hidden - P * j) for j in range(3)]
    units = [(c, j) for c in range(NC) for j in range(3)]
    with phase(nc, "gate_done value_done acted gated out_done added",
               [("gelu", [P, 2, CH], F32), ("h", [P, 3, T], F32)]) as (
            gate_done, value_done, acted, gated, out_done, added, gelu, h):
        with nc.Block() as block:
            @block.tensor
            def _(pe):
                for n, (c, j) in enumerate(units):
                    r = rows[j]
                    if n >= 2:
                        pe.wait_ge(acted, n - 1)
                    pe.matmul(k.bank(n % 2, CH, r), w1[:, hidden + P * j:hidden + P * j + r], xn(c), start=True, stop=True)\
                        .then_inc(gate_done, 1)
                    if n >= 2:
                        pe.wait_ge(gated, n - 1)
                    pe.matmul(k.bank(2 + n % 2, CH, r), w1[:, P * j:P * j + r], xn(c), start=True, stop=True)\
                        .then_inc(value_done, 1)
                for c in range(NC):
                    pe.wait_ge(gated, 3 * c + 3)
                    for j in range(3):
                        mm = pe.matmul(k.bank(4 + c), w2[0:rows[j], j, :], h[0:rows[j], j, CH * c:CH * (c + 1)],
                                       start=(j == 0), stop=(j == 2))
                    mm.then_inc(out_done, 1)

            @block.scalar
            def _(act):
                for n, (c, j) in enumerate(units):
                    r = rows[j]
                    act.wait_ge(gate_done, n + 1)
                    if n >= 2:
                        act.wait_ge(gated, n - 1)
                    act.activation(gelu[0:r, n % 2, :], k.bank(n % 2, CH, r), ACT.Gelu, bias=b1[0:r, 3 + j:4 + j]).then_inc(acted, 1)

            @block.vector
            def _(dve):
                for n, (c, j) in enumerate(units):
                    r = rows[j]
                    dve.wait_ge(value_done, n + 1)
                    dve.wait_ge(acted, n + 1)
                    dve.scalar_tensor_tensor(out=h[0:r, j, CH * c:CH * (c + 1)], in0=k.bank(2 + n % 2, CH, r),
                                             scalar=b1[0:r, j:j + 1], in1=gelu[0:r, n % 2, :], op0=ALU.add, op1=ALU.mult)\
                        .then_inc(gated, 1)
                for c in range(NC):
                    dve.wait_ge(out_done, c + 1)
                    zc = z[:, 1 + CH * c:1 + CH * (c + 1)]
                    dve.scalar_tensor_tensor(out=zc, in0=k.bank(4 + c), scalar=b2, in1=zc, op0=ALU.add, op1=ALU.add)\
                        .then_inc(added, 1)


def layer1_ffn(k, A):
    nc = k.nc
    HID = 341
    with ExitStack() as ctx:
        def sb(name, shape):
            return ctx.enter_context(nc.sbuf_tensor(name + "_l1f", shape, F32))

        z, h = sb("z", [P, T + 1]), k.s4
        wqkv, wo, w1, w2 = sb("wqkv", [P, 1536]), sb("wo", [P, 4, P]), sb("w1", [P, 2 * HID]), sb("w2", [P, 3, P])
        vec, b1, bands = sb("vec", [P, 5]), sb("b1", [P, 6]), sb("bands", [P, 2, 2 * P])

        def z_part(c):
            return z[:, 1 + CH * c:1 + CH * (c + 1)]

        def h_part(c):
            return part(h, c)

        load(k, [(bands[:, :, :], A["const_bands"])], zero=[z[:, 0:1]])
        layernorm(k, k.x, z_part, 1e-5)
        for layer in range(2):
            b1_src = A["L1_ffn_b1"][layer]
            loads = [(wqkv[:, :], A["L1_ffn_wqkv"][layer]), (w1[:, :], A["L1_ffn_w1"][layer]),
                     (wo[:, :, :], A["L1_ffn_wo"][layer].rearrange("(j p) d -> p j d", p=P)),
                     (w2[:, 0:2, :], A["L1_ffn_w2"][layer, 0:2 * P].rearrange("(j p) d -> p j d", p=P)),
                     (w2[0:HID - 2 * P, 2, :], A["L1_ffn_w2"][layer, 2 * P:HID])]
            for part_ in range(2):
                for j in range(3):
                    r = min(P, HID - P * j)
                    loads.append((b1[0:r, 3 * part_ + j:3 * part_ + j + 1],
                                  b1_src[HID * part_ + P * j:HID * part_ + P * j + r].rearrange("(p a) -> p a", a=1)))
            for r in range(2):
                for n, name in enumerate(("q_scale", "k_scale")):
                    loads.append((vec[64 * r:64 * r + 64, n:n + 1], A["L1_ffn_" + name][layer].rearrange("(p a) -> p a", a=1)))
            for n, name in enumerate(("ln_g", "ln_b", "b2")):
                loads.append((vec[:, 2 + n:3 + n], A["L1_ffn_" + name][layer].rearrange("(p a) -> p a", a=1)))
            load(k, loads)
            with ExitStack() as att:
                qk = att.enter_context(nc.sbuf_tensor(f"qk_{layer}", [P, 8, P + T], F32))
                shifted_tokens(k, z, h)
                with nc.sbuf_tensor(f"xpos_{layer}", [P, 4, T], F32) as xpos:
                    load(k, [(xpos[:, :, :], A["const_xpos"])], zero=[qk[:, 4:8, 0:P]])
                    window_qk(k, h, wqkv, vec, xpos, qk)
                v = att.enter_context(nc.sbuf_tensor(f"v_{layer}", [P, NT + 1, 512], F32))
                load(k, [(bands[:, :, :], A["const_bands"])], zero=[v[:, 0, :]])
                project(k, [("vector" if t % 2 else "scalar", [(h[:, P * t:P * (t + 1)], wqkv[:, 1024:1536])], P, CH,
                             copy_any(v[:, 1 + t, :])) for t in range(NT)])
                o = k.scratch
                window_attention(k, qk, v, bands, o)
                project(k, [("vector", [(wo[:, j, :], o[:, j, CH * c:CH * (c + 1)]) for j in range(4)], P, CH,
                             lambda dve, ps, c=c: dve.tensor_tensor(z_part(c), z_part(c), ps, ALU.add)) for c in range(NC)])
            shifted_tokens(k, z, h)
            layernorm(k, h_part, k.xn, 1e-5, vec[:, 2:3], vec[:, 3:4])
            gated_ffn(k, k.xn, w1, b1, w2, vec[:, 4:5], z, HID)
        add_tile(k, z[:, 1:1 + T])


def layer2_ffn(k, A):
    nc = k.nc
    E, CAP, F = 16, 32, 256
    SLOT = E * CAP
    G = SLOT // P
    with ExitStack() as ctx:
        def sb(name, shape, dt=F32):
            return ctx.enter_context(nc.sbuf_tensor(name + "_l2f", shape, dt))

        r1, r2 = sb("r1", [P, P]), sb("r2", [P, E])
        w1, w2, w3 = sb("w1", [P, E, F]), sb("w2", [P, E, F]), sb("w3", [P, E, 2, P])
        logits, left = sb("logits", [E, T]), sb("left", [E, T])
        best, place, place_f = sb("best", [E, CAP]), sb("place", [E, CAP], U32), sb("place_f", [E, CAP])
        st, share = sb("st", [E, 6]), sb("share", [E, CAP])
        places, place_col, share_col = sb("places", [P, SLOT]), sb("place_col", [P, G]), sb("share_col", [P, G])
        token, iota = sb("token", [P, NT]), sb("iota", [P, T])
        x_tok, x_slot = sb("x_tok", [P, NT, P]), sb("x_slot", [P, SLOT])
        gate, h, h_t, result = sb("gate", [P, G, F]), sb("h", [P, G, F]), sb("h_t", [P, G, 2, P]), sb("result", [P, G, P])
        place_dram = nc.dram_tensor("place_dram", (E, CAP), F32).ap()
        share_dram = nc.dram_tensor("share_dram", (E, CAP), F32).ap()
        load(k, [(r1[:, :], A["L2_ffn_router_w1"]), (r2[:, :], A["L2_ffn_router_w2"]),
                 (w1[:, :, :], A["L2_ffn_w1"].rearrange("e p f -> p e f")),
                 (w2[:, :, :], A["L2_ffn_w2"].rearrange("e p f -> p e f")),
                 (w3[:, :, :, :], A["L2_ffn_w3"].rearrange("e (j p) d -> p e j d", p=P)),
                 (token[:, :], A["const_token"]), (iota[:, :], A["const_iota"])])
        layernorm(k, k.x, k.xn, 1e-5)
        project(k, [("scalar", [(r1[:, :], k.xn(c))], P, CH,
                     lambda act, ps, c=c: act.activation(part(k.s1, c), ps, ACT.Silu)) for c in range(NC)])
        project(k, [("scalar", [(r2[:, :], part(k.s1, c))], E, CH, copy_out(part(logits, c))) for c in range(NC)])

        names = "step exp_done weighed written row_read turned copied marked gathered"
        with phase(nc, names, []) as (step, exp_done, weighed, written, row_read, turned, copied, marked, gathered):
            rounds = CAP // 8
            with nc.Block() as block:
                @block.vector
                def _(dve):
                    for r in range(rounds):
                        src = logits if r == 0 else left
                        dve.max(best[:, 8 * r:8 * r + 8], src[:, :]).then_inc(step, 1)
                        dve.wait_ge(step, 3 * r + 1)
                        dve.max_index(place[:, 8 * r:8 * r + 8], best[:, 8 * r:8 * r + 8], src[:, :]).then_inc(step, 1)
                        dve.wait_ge(step, 3 * r + 2)
                        dve.match_replace(left[:, :], best[:, 8 * r:8 * r + 8], src[:, :], MASKED).then_inc(step, 1)
                        dve.wait_ge(step, 3 * r + 3)
                    n = 3 * rounds
                    dve.tensor_copy(place_f[:, :], place[:, :]).then_inc(step, 1)
                    dve.tensor_scalar(st[:, 0:1], best[:, 0:1], -1.0, None, ALU.mult).then_inc(step, 1)
                    dve.wait_ge(exp_done, 2)
                    dve.reciprocal(st[:, 2:3], st[:, 1:2]).then_inc(step, 1)
                    dve.wait_ge(step, n + 3)
                    dve.tensor_scalar(share[:, :], share[:, :], st[:, 2:3], None, ALU.mult).then_inc(step, 1)
                    dve.wait_ge(step, n + 4)
                    dve.tensor_reduce(st[:, 3:4], share[:, :], AX.X, ALU.add).then_inc(step, 1)
                    dve.wait_ge(step, n + 5)
                    dve.tensor_scalar(st[:, 4:5], st[:, 3:4], 1e-9, None, ALU.add).then_inc(step, 1)
                    dve.wait_ge(step, n + 6)
                    dve.reciprocal(st[:, 5:6], st[:, 4:5]).then_inc(step, 1)
                    dve.wait_ge(step, n + 7)
                    dve.tensor_scalar(share[:, :], share[:, :], st[:, 5:6], None, ALU.mult).then_inc(weighed, 1)
                    dve.wait_ge(row_read, 48)
                    for t in range(NT):
                        mark = k.scratch[:, t // 4, CH * (t % 4):CH * (t % 4 + 1)]
                        dve.tensor_scalar(mark, places[:, :], token[:, t:t + 1], None, ALU.is_equal).then_inc(marked, 1)
                    dve.wait_ge(gathered, 1)
                    dve.tensor_copy(x_slot[:, :], k.bank(4)).then_inc(step, 1)

                @block.scalar
                def _(act):
                    act.wait_ge(step, 3 * rounds + 2)
                    act.activation(left[:, :], logits[:, :], ACT.Exp, bias=st[:, 0:1], accum_out=st[:, 1:2]).then_inc(exp_done, 1)
                    act.activation(share[:, :], best[:, :], ACT.Exp, bias=st[:, 0:1]).then_inc(exp_done, 1)
                    for b in range(4):
                        act.wait_ge(turned, b + 1)
                        act.activation(x_tok[:, 4 * b:4 * b + 4, :].rearrange("p a b -> p (a b)"), k.bank(b), ACT.Copy)\
                            .then_inc(copied, 1)

                @block.sync
                def _(sp):
                    sp.wait_ge(step, 3 * rounds + 1)
                    sp.dma_start(place_dram, place_f[:, :]).then_inc(written, 16)
                    sp.wait_ge(weighed, 1)
                    sp.dma_start(share_dram, share[:, :]).then_inc(written, 16)
                    sp.wait_ge(written, 32)
                    row = place_dram.rearrange("e c -> (e c)")
                    sp.dma_start(places[:, :], row.rearrange("(a n) -> a n", a=1).to_broadcast([P, SLOT])).then_inc(row_read, 16)
                    sp.dma_start(place_col[:, :], row.rearrange("(g p) -> p g", p=P), allow_slow_non_contiguous=True).then_inc(row_read, 16)
                    sp.dma_start(share_col[:, :], share_dram.rearrange("e c -> (e c)").rearrange("(g p) -> p g", p=P),
                                 allow_slow_non_contiguous=True)\
                        .then_inc(row_read, 16)

                @block.tensor
                def _(pe):
                    for b in range(4):
                        for a in range(4):
                            mm = pe.transpose(k.bank(b)[:, P * a:P * (a + 1)], k.xn_tile(4 * b + a), k.mat("ident"))
                        mm.then_inc(turned, 1)
                    for t in range(NT):
                        pe.wait_ge(copied, t // 4 + 1)
                        pe.wait_ge(marked, t + 1)
                        mm = pe.matmul(k.bank(4), x_tok[:, t, :], k.scratch[:, t // 4, CH * (t % 4):CH * (t % 4 + 1)],
                                       start=(t == 0), stop=(t == NT - 1))
                    mm.then_inc(gathered, 1)

        names = "raised acted gated turned copied lowered weighed marked out_done added"
        with phase(nc, names, []) as (raised, acted, gated, turned, copied, lowered, weighed, marked, out_done, added):
            with nc.Block() as block:
                @block.tensor
                def _(pe):
                    for g in range(G):
                        for base, w in ((0, w1), (2, w2)):
                            for j in range(4):
                                e = 4 * g + j
                                mm = pe.matmul(k.bank(base + g // 2)[32 * j:32 * j + 32, F * (g % 2):F * (g % 2 + 1)],
                                               x_slot[:, CAP * e:CAP * (e + 1)], w[:, e, :], start=True, stop=True)
                    mm.then_inc(raised, 1)
                    for g in range(G):
                        pe.wait_ge(gated, g + 1)
                        for j in range(2):
                            mm = pe.transpose(k.bank(4 + g // 2)[:, F * (g % 2) + P * j:F * (g % 2) + P * (j + 1)],
                                              h[:, g, P * j:P * (j + 1)], k.mat("ident"))
                        mm.then_inc(turned, 1)
                    for g in range(G):
                        pe.wait_ge(copied, g // 2 + 1)
                        for e in range(4 * g, 4 * g + 4):
                            j = e % 4
                            for f in range(2):
                                mm = pe.matmul(k.bank(6)[32 * j:32 * j + 32, P * g:P * (g + 1)],
                                               h_t[:, g, f, CAP * j:CAP * (j + 1)], w3[:, e, f, :], start=(f == 0), stop=(f == 1))
                    mm.then_inc(lowered, 1)
                    pe.wait_ge(weighed, G)
                    for c in range(NC):
                        for g in range(G):
                            pe.wait_ge(marked, g + 1)
                            mm = pe.matmul(k.bank(c), result[:, g, :], k.scratch[:, g, CH * c:CH * (c + 1)],
                                           start=(g == 0), stop=(g == G - 1))
                        mm.then_inc(out_done, 1)

                @block.scalar
                def _(act):
                    act.wait_ge(raised, 1)
                    for b in range(2):
                        act.activation(gate[:, 2 * b:2 * b + 2, :].rearrange("p a b -> p (a b)"), k.bank(b), ACT.Silu)\
                            .then_inc(acted, 1)
                    for b in range(2):
                        act.wait_ge(turned, 2 * b + 2)
                        act.activation(h_t[:, 2 * b:2 * b + 2, :, :].rearrange("p a j b -> p (a j b)"), k.bank(4 + b), ACT.Copy)\
                            .then_inc(copied, 1)

                @block.vector
                def _(dve):
                    for g in range(G):
                        dve.tensor_scalar(k.scratch[:, g, :], iota[:, :], place_col[:, g:g + 1], None, ALU.is_equal)\
                            .then_inc(marked, 1)
                    for g in range(G):
                        dve.wait_ge(acted, g // 2 + 1)
                        dve.tensor_tensor(h[:, g, :], k.bank(2 + g // 2)[:, F * (g % 2):F * (g % 2 + 1)], gate[:, g, :], ALU.mult)\
                            .then_inc(gated, 1)
                    dve.wait_ge(lowered, 1)
                    for g in range(G):
                        dve.tensor_scalar(result[:, g, :], k.bank(6)[:, P * g:P * (g + 1)], share_col[:, g:g + 1], None, ALU.mult)\
                            .then_inc(weighed, 1)
                    for c in range(NC):
                        dve.wait_ge(out_done, c + 1)
                        dve.tensor_tensor(k.x(c), k.x(c), k.bank(c), ALU.add).then_inc(added, 1)


def causal_schedule():
    blocks = [(p, q, s) for p in range(8) for q in range(NC) for s in range(2)]
    order = []
    for tile in range(12):
        order.append(("fill", 0, tile))
    for b in range(len(blocks) + 1):
        for i in range(4):
            side = []
            if b >= 1:
                p, q, s = blocks[b - 1]
                keys = range(i * (q + 1), (i + 1) * (q + 1))
                for kt in keys:
                    side.append(("turn", b - 1, kt))
                if i == 3 and s == 1:
                    side.append(("close", b - 1, 0))
                    if p >= 1 and q == 0 or b == len(blocks):
                        side.append(("project", p - 1 if q == 0 else p, 0))
            if b < len(blocks):
                p, q, s = blocks[b]
                n = 4 * b + i
                local = 4 * (2 * q + s) + i
                if p < 7 and 12 <= local < 24:
                    side.append(("fill", p + 1, local - 12))
                for j in range(q + 1):
                    order.append(("score", n, j))
                exps = [("exp", n, j) for j in range(q + 1)]
                total = len(side) + len(exps)
                done_e = done_s = 0
                for m in range(total):
                    if done_e < len(exps) and (done_s >= len(side) or done_e * len(side) <= done_s * len(exps)):
                        order.append(exps[done_e])
                        done_e += 1
                    else:
                        order.append(side[done_s])
                        done_s += 1
            else:
                order.extend(side)
    return blocks, order


def causal_attention(k, wq, wk, wv, proj, bq8, bk, bv, eighth):
    nc = k.nc
    blocks, order = causal_schedule()
    S_BANKS = 5
    names = ("scored masked part_max maxed exped turned copied_v copied_s mixed totalled inverted spread shared_done "
             "shared_copied weighted laid_out out_done added zeroed")
    tiles = [("q_pad", [P, 2, 2, T], F32), ("probs", [P, 2, 4, T], F32), ("probs_t", [P, 3, CH], F32),
             ("tops", [P, 2, 4], F32), ("neg_max", [P, 2], F32), ("total", [P, 16, 4], F32), ("sums", [P, 8], F32),
             ("inv", [P, 8], F32), ("diag", [P, 8, P], F32), ("shares", [P, CH], F32), ("z", [P, T], F32), ("z_dup", [P, 2, T], F32)]
    with phase(nc, names, tiles) as (scored, masked, part_max, maxed, exped, turned, copied_v, copied_s, mixed, totalled,
                                     inverted, spread, shared_done, shared_copied, weighted, laid_out, out_done, added, zeroed,
                                     q_pad, probs, probs_t, tops, neg_max, total, sums, inv, diag, shares, z, z_dup):
        side = [e for e in order if e[0] in ("fill", "turn")]
        engine_of, count_of = [], []
        n_v = n_s = 0
        for m, e in enumerate(side):
            by_s = e[2] < 4 if e[0] == "fill" else m % 5 in (0, 2)
            n_s, n_v = n_s + by_s, n_v + (not by_s)
            engine_of.append("s" if by_s else "v")
            count_of.append(n_s if by_s else n_v)
        side_index = {e: m for m, e in enumerate(side)}
        turns = [e for e in side if e[0] == "turn"]
        turn_index = {e: m for m, e in enumerate(turns)}
        chunk_index = {e[1:]: m for m, e in enumerate([e for e in order if e[0] == "score"])}
        fills = {e[1:]: side_index[e] for e in side if e[0] == "fill"}

        def wait_copied(eng, m):
            eng.wait_ge(copied_s if engine_of[m] == "s" else copied_v, count_of[m])

        def chunks_through(b):
            return chunk_index[(4 * b + 3, blocks[b][1])] + 1

        def turns_through(b):
            return turn_index[("turn", b, 4 * blocks[b][1] + 3)] + 1

        def width(n, j):
            q = blocks[n // 4][1]
            return CH if j < q else P * (n % 4 + 1)

        def first_query(b, kt):
            return max(0, kt - 4 * blocks[b][1])

        def last_side_before(close):
            at = order.index(close)
            return max(side_index[e] for e in order[:at] if e[0] in ("fill", "turn"))

        with nc.Block() as block:
            @block.tensor
            def _(pe):
                pending = []

                def mix():
                    e = pending.pop(0)
                    _, b, kt = e
                    p, q, s = blocks[b]
                    a = first_query(b, kt)
                    wait_copied(pe, side_index[e])
                    if kt == 0 and s == 0 and b >= 2:
                        pe.wait_ge(weighted, b // 2)
                    if kt == 0:
                        wait_copied(pe, fills[(p, 11)])
                    pe.matmul(k.bank(7)[64 * s:64 * s + 64, P * a:CH],
                              k.scratch[:, 2 + p % 2, P * kt + 64 * s:P * kt + 64 * s + 64],
                              probs_t[:, turn_index[e] % 3, P * a:CH],
                              start=(kt == 0), stop=(kt == 4 * q + 3)).then_inc(mixed, 1)

                pe.wait_ge(zeroed, 4)
                for e in order:
                    kind = e[0]
                    if kind == "score":
                        n, j = e[1:]
                        p, q, s = blocks[n // 4]
                        c = chunk_index[(n, j)]
                        if c >= S_BANKS:
                            pe.wait_ge(exped, c - S_BANKS + 1)
                        if j == 0 and q == 0 and s == 0 and n % 4 == 0:
                            wait_copied(pe, fills[(p, 3)])
                            wait_copied(pe, fills[(p, 7)])
                        w = width(n, j)
                        t = 4 * q + n % 4
                        pe.matmul(k.bank(c % S_BANKS, w), q_pad[:, p % 2, s, P * t:P * (t + 1)],
                                  k.scratch[:, p % 2, CH * j:CH * j + w], start=True, stop=True).then_inc(scored, 1)
                    elif kind in ("fill", "turn"):
                        m = side_index[e]
                        if m >= 2:
                            wait_copied(pe, m - 2)
                        bank = k.bank(5 + m % 2)
                        if kind == "fill":
                            p, tile = e[1:]
                            if tile < 8:
                                w = (wq if tile < 4 else wk)[:, P * p:P * (p + 1)]
                                mm = pe.matmul(bank, w, k.xn(tile % 4), start=True, stop=True)
                            else:
                                for a in range(4):
                                    mm = pe.matmul(bank[:, P * a:P * (a + 1)], k.xn_tile(4 * (tile - 8) + a),
                                                   wv[:, P * p:P * (p + 1)], start=True, stop=True)
                        else:
                            b, kt = e[1:]
                            if kt == 0:
                                pe.wait_ge(exped, chunks_through(b))
                            for a in range(first_query(b, kt), 4):
                                mm = pe.transpose(bank[:, P * a:P * (a + 1)], probs[:, b % 2, a, P * kt:P * (kt + 1)],
                                                  k.mat("ident"))
                            pending.append(e)
                        mm.then_inc(turned, 1)
                        if len(pending) > 1:
                            mix()
                    elif kind == "close":
                        while pending:
                            mix()
                        b = e[1]
                        p, q, _ = blocks[b]
                        pe.wait_ge(spread, 8 * (b // 2 + 1))
                        for m in range(2):
                            wait_copied(pe, last_side_before(e) - m)
                        for s in range(2):
                            for a in range(4):
                                mm = pe.matmul(k.bank(5)[64 * s:64 * s + 64, P * a:P * (a + 1)], eighth[:, :],
                                               diag[:, 4 * s + a, :], start=True, stop=True)
                        mm.then_inc(shared_done, 1)
                        pe.wait_ge(shared_copied, b // 2 + 1)
                    elif kind == "project":
                        p = e[1]
                        pe.wait_ge(laid_out, 64 * (p + 1))
                        for m in range(2):
                            wait_copied(pe, last_side_before(e) - m)
                        for m in range(8):
                            rows = z_dup[:, :, :].rearrange("p s (r j) -> p s r j", j=16)[:, :, :, 2 * m]
                            mm = pe.matmul(k.bank(6, 2 * P), proj[:, m, :], rows, start=(m == 0), stop=(m == 7))
                        mm.then_inc(out_done, 1)
                        pe.wait_ge(added, p + 1)

            @block.gpsimd
            def _(pool):
                for parity in range(2):
                    pool.memset(q_pad[64:P, parity, 0, :], 0.0).then_inc(zeroed, 1)
                    pool.memset(q_pad[0:64, parity, 1, :], 0.0).then_inc(zeroed, 1)

            def before_fill(eng, p, tile):
                if p >= 2:
                    last = 8 * (p - 1) - 1
                    eng.wait_ge(scored, chunks_through(last))
                    if tile >= 8:
                        eng.wait_ge(mixed, turns_through(last))

            @block.scalar
            def _(act):
                for e in order:
                    if e[0] == "exp":
                        n, j = e[1:]
                        b = n // 4
                        act.wait_ge(maxed, n + 1)
                        if b >= 2 and n % 4 == 0 and j == 0:
                            act.wait_ge(turned, side_index[turns[turns_through(b - 2) - 1]] + 1)
                        if b >= 4 and n % 8 == 0 and j == 0:
                            act.wait_ge(totalled, b // 2 - 1)
                        c, w = chunk_index[(n, j)], width(n, j)
                        act.activation(probs[:, b % 2, n % 4, CH * j:CH * j + w], k.bank(c % S_BANKS, w), ACT.Exp,
                                       bias=neg_max[:, n % 2:n % 2 + 1], accum_out=total[:, n % 16, j:j + 1]).then_inc(exped, 1)
                    elif e[0] in ("fill", "turn") and engine_of[side_index[e]] == "s":
                        m = side_index[e]
                        act.wait_ge(turned, m + 1)
                        bank = k.bank(5 + m % 2)
                        if e[0] == "fill":
                            p, c = e[1:]
                            before_fill(act, p, c)
                            for s in range(2):
                                r = slice(64 * s, 64 * s + 64)
                                ins = act.activation(q_pad[r, p % 2, s, CH * c:CH * (c + 1)], bank[r, :], ACT.Identity,
                                                     scale=0.125, bias=bq8[r, p:p + 1])
                        else:
                            t = turn_index[e]
                            if t >= 3:
                                act.wait_ge(mixed, t - 2)
                            a = first_query(*e[1:])
                            ins = act.activation(probs_t[:, t % 3, P * a:CH], bank[:, P * a:CH], ACT.Copy)
                        ins.then_inc(copied_s, 1)
                    elif e[0] == "close":
                        act.wait_ge(shared_done, e[1] // 2 + 1)
                        act.activation(shares[:, :], k.bank(5), ACT.Copy).then_inc(shared_copied, 1)

            @block.vector
            def _(dve):
                n_mask = n_part = 0
                for e in order:
                    if e[0] == "score":
                        n, j = e[1:]
                        q = blocks[n // 4][1]
                        c, w = chunk_index[(n, j)], width(n, j)
                        dve.wait_ge(scored, c + 1)
                        bank = k.bank(c % S_BANKS, w)
                        if j == q:
                            edge = bank[:, w - P:w]
                            dve.tensor_tensor(edge, edge, k.mat("causal"), ALU.add).then_inc(masked, 1)
                            n_mask += 1
                            dve.wait_ge(masked, n_mask)
                        if q == 0:
                            if n >= 2:
                                dve.wait_ge(exped, chunk_index[(n - 2, blocks[(n - 2) // 4][1])] + 1)
                            dve.tensor_reduce(neg_max[:, n % 2:n % 2 + 1], bank, AX.X, ALU.max, negate=True).then_inc(maxed, 1)
                        else:
                            dve.tensor_reduce(tops[:, n % 2, j:j + 1], bank, AX.X, ALU.max).then_inc(part_max, 1)
                            n_part += 1
                            if j == q:
                                dve.wait_ge(part_max, n_part)
                                if n >= 2:
                                    dve.wait_ge(exped, chunk_index[(n - 2, blocks[(n - 2) // 4][1])] + 1)
                                dve.tensor_reduce(neg_max[:, n % 2:n % 2 + 1], tops[:, n % 2, 0:q + 1], AX.X, ALU.max,
                                                  negate=True).then_inc(maxed, 1)
                    elif e[0] in ("fill", "turn") and engine_of[side_index[e]] == "v":
                        m = side_index[e]
                        dve.wait_ge(turned, m + 1)
                        bank = k.bank(5 + m % 2)
                        if e[0] == "fill":
                            p, tile = e[1:]
                            before_fill(dve, p, tile)
                            if tile < 8:
                                ins = dve.tensor_scalar(k.scratch[:, p % 2, CH * (tile - 4):CH * (tile - 3)], bank, bk[:, p:p + 1],
                                                        None, ALU.add)
                            else:
                                ins = dve.tensor_tensor(
                                    k.scratch[:, 2 + p % 2, CH * (tile - 8):CH * (tile - 7)].rearrange("p (t d) -> p t d", t=4),
                                    bank.rearrange("p (t d) -> p t d", t=4),
                                    bv[:, P * p:P * (p + 1)].unsqueeze(1).to_broadcast([P, 4, P]), ALU.add)
                        else:
                            t = turn_index[e]
                            if t >= 3:
                                dve.wait_ge(mixed, t - 2)
                            a = first_query(*e[1:])
                            ins = dve.tensor_copy(probs_t[:, t % 3, P * a:CH], bank[:, P * a:CH])
                        ins.then_inc(copied_v, 1)
                    elif e[0] == "close":
                        b = e[1]
                        _, q, _ = blocks[b]
                        r = b // 2
                        dve.wait_ge(exped, chunks_through(b))
                        at = 4 * (b - 1) % 16
                        dve.tensor_reduce(sums[:, :], total[:, at:at + 8, 0:q + 1], AX.X, ALU.add).then_inc(totalled, 1)
                        dve.wait_ge(totalled, r + 1)
                        dve.reciprocal(inv[:, :], sums[:, :]).then_inc(inverted, 1)
                        dve.wait_ge(inverted, r + 1)
                        for u in range(8):
                            dve.tensor_scalar(diag[:, u, :], k.mat("ident"), inv[:, u:u + 1], None, ALU.mult).then_inc(spread, 1)
                        dve.wait_ge(shared_copied, r + 1)
                        dve.wait_ge(mixed, turns_through(b))
                        p = blocks[b][0]
                        if p >= 1 and q == 0:
                            dve.wait_ge(laid_out, 64 * p)
                        dve.tensor_tensor(part(z, q), k.bank(7), shares[:, :], ALU.mult).then_inc(weighted, 1)
                    elif e[0] == "project":
                        p = e[1]
                        dve.wait_ge(out_done, p + 1)
                        xs = k.xpad[:, 1 + 2 * P * p:1 + 2 * P * (p + 1)]
                        dve.tensor_tensor(xs, xs, k.bank(6, 2 * P), ALU.add).then_inc(added, 1)

            @block.sync
            def _(sp):
                for p in range(8):
                    sp.wait_ge(weighted, 4 * (p + 1))
                    if p >= 1:
                        sp.wait_ge(out_done, p)
                    for s in range(2):
                        src = z[64 * s:64 * s + 64, :]
                        sp.dma_start(z_dup[0:64, s, :], src).then_inc(laid_out, 16)
                        sp.dma_start(z_dup[64:P, s, 0:T - 1], src[:, 1:T]).then_inc(laid_out, 16)
                sp.wait_ge(laid_out, 64 * 8)


def layer3_attention(k, A):
    nc = k.nc
    with ExitStack() as ctx:
        def sb(name, shape):
            return ctx.enter_context(nc.sbuf_tensor(name + "_l3a", shape, F32))

        wq, wk, wv, proj = sb("wq", [P, 1024]), sb("wk", [P, 1024]), sb("wv", [P, 1024]), sb("proj", [P, 8, P])
        bq, bq8, bk, bv, eighth = sb("bq", [P, 8]), sb("bq8", [P, 8]), sb("bk", [P, 8]), sb("bv", [P, 1024]), sb("eighth", [P, 64])
        pairs = [(wq[:, :], A["L3_attn_WqT"]), (wk[:, :], A["L3_attn_WkT"]), (wv[:, :], A["L3_attn_WvT"]),
                 (proj[:, :, :], A["L3_attn_proj"].rearrange("(j p) d -> p j d", p=P)),
                 (bv[:, :], A["L3_attn_bv"].rearrange("h d -> (h d)").rearrange("(a n) -> a n", a=1).to_broadcast([P, 1024]))]
        for p in range(8):
            for tile, name in ((bq, "bq"), (bk, "bk")):
                pairs.append((tile[:, p:p + 1], A["L3_attn_" + name][2 * p:2 * p + 2].rearrange("h (d a) -> (h d) a", a=1)))
        load(k, pairs)
        layernorm(k, k.x, k.xn, 1e-5)
        with phase(nc, "made", []) as (made,):
            with nc.Block() as block:
                @block.vector
                def _(dve):
                    dve.tensor_scalar(bq8[:, :], bq[:, :], 0.125, None, ALU.mult).then_inc(made, 1)
                    dve.memset(eighth[:, :], 0.125).then_inc(made, 1)
        causal_attention(k, wq, wk, wv, proj, bq8, bk, bv, eighth)


def layer3_ffn(k, A):
    nc = k.nc
    E, F = 8, 512
    FT = F // P
    with ExitStack() as ctx:
        def sb(name, shape, dt=F32):
            return ctx.enter_context(nc.sbuf_tensor(name + "_l3f", shape, dt))

        gate_w, up, down = sb("gate_w", [P, E]), sb("up", [P, E, 2 * F]), sb("down", [P, E, FT, P])
        logits, best, place = sb("logits", [P, NT, E]), sb("best", [P, NT, 8]), sb("place", [P, NT, 8], U32)
        place_f, iota8 = sb("place_f", [P, NT, 2]), sb("iota8", [P, E])
        gap, second, inv, share = sb("gap", [P, NT]), sb("second", [P, NT]), sb("inv", [P, NT]), sb("share", [P, 2, NT])
        pick, combine, rows = sb("pick", [P, 2, E, NT]), sb("combine", [P, E, NT]), sb("rows", [P, P])
        xe = sb("xe", [P, E, T])
        combine_dram = nc.dram_tensor("combine_dram", (E, T), F32).ap()
        load(k, [(gate_w[:, :], A["L3_ffn_gateT"]), (up[:, :, :], A["L3_ffn_gate_upT"].rearrange("e p f -> p e f")),
                 (down[:, :, :, :], A["L3_ffn_downT"].rearrange("e (j p) d -> p e j d", p=P)),
                 (iota8[:, :], A["const_iota"][:, 0:E])])
        layernorm(k, k.x, k.xn, 1e-5)

        names = "scored copied found placed gap_done exp_done step turned rows_done written read scaled"
        with phase(nc, names, []) as (scored, copied, found, placed, gap_done, exp_done, step, turned, rows_done, written,
                                      read, scaled):
            with nc.Block() as block:
                @block.tensor
                def _(pe):
                    for t in range(NT):
                        mm = pe.matmul(k.bank(0)[:, E * t:E * (t + 1)], k.xn_tile(t), gate_w[:, :], start=True, stop=True)
                    mm.then_inc(scored, 1)
                    pe.wait_ge(step, 7)
                    pe.transpose(k.bank(1, P), combine[:, :, :].rearrange("p e t -> p (e t)"), k.mat("ident")).then_inc(turned, 1)

                @block.vector
                def _(dve):
                    dve.wait_ge(scored, 1)
                    dve.tensor_copy(logits[:, :, :].rearrange("p t e -> p (t e)"), k.bank(0, NT * E)).then_inc(copied, 1)
                    dve.wait_ge(copied, 1)
                    for t in range(NT):
                        dve.max(best[:, t, :], logits[:, t, :]).then_inc(found, 1)
                    for t in range(NT):
                        dve.wait_ge(found, t + 1)
                        dve.max_index(place[:, t, :], best[:, t, :], logits[:, t, :]).then_inc(placed, 1)
                    dve.tensor_tensor(gap[:, :], best[:, :, 1], best[:, :, 0], ALU.subtract).then_inc(gap_done, 1)
                    dve.wait_ge(placed, NT)
                    dve.tensor_copy(place_f[:, :, :], place[:, :, 0:2]).then_inc(step, 1)
                    dve.wait_ge(exp_done, 1)
                    dve.tensor_scalar(inv[:, :], second[:, :], 1.0, None, ALU.add).then_inc(step, 1)
                    dve.wait_ge(step, 2)
                    dve.reciprocal(share[:, 0, :], inv[:, :]).then_inc(step, 1)
                    dve.wait_ge(step, 3)
                    dve.tensor_tensor(share[:, 1, :], share[:, 0, :], second[:, :], ALU.mult).then_inc(step, 1)
                    for b in range(2):
                        dve.tensor_tensor(pick[:, b, :, :], iota8[:, :].unsqueeze(2).to_broadcast([P, E, NT]),
                                          place_f[:, :, b].unsqueeze(1).to_broadcast([P, E, NT]), ALU.is_equal).then_inc(step, 1)
                    dve.wait_ge(step, 6)
                    for b in range(2):
                        dve.tensor_tensor(pick[:, b, :, :], pick[:, b, :, :],
                                          share[:, b, :].unsqueeze(1).to_broadcast([P, E, NT]), ALU.mult).then_inc(rows_done, 1)
                    dve.wait_ge(rows_done, 2)
                    dve.tensor_tensor(combine[:, :, :], pick[:, 0, :, :], pick[:, 1, :, :], ALU.add).then_inc(step, 1)
                    dve.wait_ge(turned, 1)
                    dve.tensor_copy(rows[:, :], k.bank(1, P)).then_inc(rows_done, 1)
                    for e in range(0, E, 2):
                        dve.wait_ge(read, 16 * (e + 1))
                        dve.tensor_tensor(xe[:, e, :], xe[:, e, :], k.xnpad[:, 1:1 + T], ALU.mult).then_inc(scaled, 1)

                @block.scalar
                def _(act):
                    act.wait_ge(gap_done, 1)
                    act.activation(second[:, :], gap[:, :], ACT.Exp).then_inc(exp_done, 1)

                @block.gpsimd
                def _(pool):
                    for e in range(1, E, 2):
                        pool.wait_ge(read, 16 * (e + 1))
                        pool.tensor_tensor(xe[:, e, :], xe[:, e, :], k.xnpad[:, 1:1 + T], ALU.mult).then_inc(scaled, 1)

                @block.sync
                def _(sp):
                    sp.wait_ge(rows_done, 3)
                    sp.dma_start(combine_dram.rearrange("e (t p) -> (e t) p", p=P), rows[:, :]).then_inc(written, 16)
                    sp.wait_ge(written, 16)
                    for e in range(E):
                        if e >= 1:
                            sp.wait_ge(read, 16 * e)
                        sp.dma_start(xe[:, e, :], combine_dram[e:e + 1, :].to_broadcast([P, T])).then_inc(read, 16)

        units = [(c, e, f) for c in range(NC) for e in range(E) for f in range(FT)]
        LAG = 2
        with phase(nc, "gate_done value_done acted gated out_done added",
                   [("silu", [P, 2, CH], F32), ("h", [P, 4, CH], F32)]) as (
                gate_done, value_done, acted, gated, out_done, added, silu, h):
            with nc.Block() as block:
                @block.tensor
                def _(pe):
                    for n in range(len(units) + LAG):
                        if n < len(units):
                            c, e, f = units[n]
                            if n >= 3:
                                pe.wait_ge(acted, n - 2)
                                pe.wait_ge(gated, n - 2)
                            pe.matmul(k.bank(n % 3), up[:, e, P * f:P * (f + 1)], k.xn(c), start=True, stop=True)\
                                .then_inc(gate_done, 1)
                            pe.matmul(k.bank(3 + n % 3), up[:, e, F + P * f:F + P * (f + 1)], xe[:, e, CH * c:CH * (c + 1)],
                                      start=True, stop=True).then_inc(value_done, 1)
                        if n >= LAG:
                            u = n - LAG
                            c, e, f = units[u]
                            first, last = (e, f) == (0, 0), (e, f) == (E - 1, FT - 1)
                            if first and c >= 2:
                                pe.wait_ge(added, c - 1)
                            pe.wait_ge(gated, u + 1)
                            mm = pe.matmul(k.bank(6 + c % 2), down[:, e, f, :], h[:, u % 4, :], start=first, stop=last)
                            mm.then_inc(out_done, 1)

                @block.scalar
                def _(act):
                    for n in range(len(units)):
                        act.wait_ge(gate_done, n + 1)
                        if n >= 2:
                            act.wait_ge(gated, n - 1)
                        act.activation(silu[:, n % 2, :], k.bank(n % 3), ACT.Silu).then_inc(acted, 1)

                @block.vector
                def _(dve):
                    for n, (c, e, f) in enumerate(units):
                        dve.wait_ge(value_done, n + 1)
                        dve.wait_ge(acted, n + 1)
                        if n >= 4:
                            dve.wait_ge(out_done, n - 3)
                        dve.tensor_tensor(h[:, n % 4, :], k.bank(3 + n % 3), silu[:, n % 2, :], ALU.mult).then_inc(gated, 1)
                        if n >= 8 and n % (E * FT) == 7 and c >= 1:
                            dve.wait_ge(out_done, E * FT * c)
                            dve.tensor_tensor(k.x(c - 1), k.x(c - 1), k.bank(6 + (c - 1) % 2), ALU.add).then_inc(added, 1)
                    dve.wait_ge(out_done, len(units))
                    dve.tensor_tensor(k.x(NC - 1), k.x(NC - 1), k.bank(6 + (NC - 1) % 2), ALU.add).then_inc(added, 1)
STEPS = [layer0_attention, layer0_ffn, layer1_attention, layer1_ffn, layer2_attention, layer2_ffn,
         layer3_attention, layer3_ffn]


def build(nc, A, out, steps=STEPS):
    with ExitStack() as ctx:
        k = Core(nc, ctx)
        setup(k, A["x_t"], A["const_mats"])
        for step in steps:
            step(k, A)
        store(k, out)


def host_constants(np):
    i = np.arange(P)
    mats = np.zeros((P, N_MATS, P), np.float32)
    mats[:, 0] = np.eye(P)
    mats[:, 1] = i[:, None] // 8 == i[None, :] // 8
    mats[:, 2] = i[:, None] // 64 == i[None, :] // 64
    for m in range(P):
        if m % 64 < 32:
            mats[m + 32, 3, m] = -1.0
        else:
            mats[m - 32, 3, m] = 1.0
    for m in range(P):
        mats[32 * (m // 32) + 8, 4, m] = 1.0
    mats[:, 5] = np.where(i[None, :] > i[:, None], MASKED, 0.0)

    t = np.arange(T, dtype=np.float32)
    f32 = np.float32
    inv = (f32(1.0) / f32(10000.0) ** (np.arange(0, 8, 2, dtype=f32) / f32(8))).astype(f32)
    ang = np.outer(inv, t).astype(f32)
    d8 = i % 8
    rope = np.stack([np.cos(ang)[d8 % 4], np.where(d8[:, None] < 4, -1.0, 1.0) * np.sin(ang)[d8 % 4]], 1).astype(f32)

    half = np.arange(0, 64, 2, dtype=f32)
    inv = (f32(1.0) / f32(10000.0) ** (half / f32(64))).astype(f32)
    ang = np.outer(inv, t).astype(f32).astype(np.float64)
    base = ((half + f32(0.4 * 64)) / f32(1.4 * 64)).astype(f32)
    power = ((t - T // 2) / f32(32)).astype(f32)
    scale = (base[:, None].astype(np.float64) ** power[None, :].astype(np.float64))
    d64 = i % 32
    cos, sin, sc = np.cos(ang)[d64], np.sin(ang)[d64], scale[d64]
    xpos = np.stack([8 * cos * sc, 8 * sin * sc, cos / sc, sin / sc], 1).astype(f32)

    kk = np.arange(2 * P)[None, :] - P
    q = i[:, None]
    band = np.where((kk <= q) & (q - kk <= 64), 0.0, MASKED)
    first = np.where(kk < 0, MASKED, band)
    bands = np.stack([first, band], 1).astype(f32)
    return {"const_mats": mats, "const_rope": rope, "const_xpos": xpos, "const_bands": bands,
            "const_iota": np.broadcast_to(np.arange(T, dtype=f32), (P, T)).copy(),
            "const_token": (np.arange(NT)[None, :] * P + i[:, None]).astype(f32)}


def arrange(np, inputs):
    a = {n: np.asarray(v) for n, v in inputs.items()}
    out = {}
    for n, v in a.items():
        out[n] = v.reshape(-1, 1) if v.ndim == 1 else v
    out["x_t"] = a["L0_attn_x"][0].T
    del out["L0_attn_x"]
    for n in ("Wq", "Wk", "Wv", "Wp"):
        out[f"L0_attn_{n}T"] = a[f"L0_attn_{n}"].T
        del out[f"L0_attn_{n}"]
    w = a["L1_attn_w_qkv"]
    even = np.arange(D).reshape(16, 4, 2).transpose(0, 2, 1).reshape(-1)
    odd = np.arange(D).reshape(16, 4, 2)[:, :, ::-1].transpose(0, 2, 1).reshape(-1)
    out["L1_attn_qkT"] = np.stack([w[:D][even].T, w[:D][odd].T, w[D:2 * D][even].T, w[D:2 * D][odd].T], 1)
    out["L1_attn_vT"] = w[2 * D:].T
    out["L1_attn_outT"] = a["L1_attn_w_out"].T
    del out["L1_attn_w_qkv"], out["L1_attn_w_out"]
    for n in ("q", "k", "v"):
        out[f"L3_attn_W{n}T"] = a[f"L3_attn_W{n}"].reshape(16 * 64, D).T
        del out[f"L3_attn_W{n}"]
    out["L3_ffn_gateT"] = a["L3_ffn_gate_w"].T
    out["L3_ffn_gate_upT"] = a["L3_ffn_gate_up_proj"].transpose(0, 2, 1)
    out["L3_ffn_downT"] = a["L3_ffn_down_proj"].transpose(0, 2, 1)
    del out["L3_ffn_gate_w"], out["L3_ffn_gate_up_proj"], out["L3_ffn_down_proj"]
    out.update(host_constants(np))
    return {n: np.ascontiguousarray(v) for n, v in out.items()}


def kernel(**inputs):
    import numpy as np
    import concourse.bacc as bacc
    from concourse.bass_utils import run_bass_kernel_spmd

    nc = bacc.Bacc("TRN2", target_bir_lowering=False, num_devices=1)
    arrays, args = {}, {}
    for name, a in arrange(np, inputs).items():
        arrays[f"in_{name}"] = a
        args[name] = nc.dram_tensor(f"in_{name}", a.shape, mybir.dt.from_np(a.dtype), kind="ExternalInput").ap()
    out = nc.dram_tensor("out_t", (D, T), F32, kind="ExternalOutput").ap()
    build(nc, args, out)
    r = run_bass_kernel_spmd(nc, [arrays], core_ids=[0])
    return np.ascontiguousarray(r.results[0]["out_t"].T).reshape(1, T, D)
```

```python
from contextlib import ExitStack, contextmanager

import concourse.bass as bass
from concourse import mybir

ALU = mybir.AluOpType
ACT = mybir.ActivationFunctionType
AX = mybir.AxisListType
F32 = mybir.dt.float32
BF16 = mybir.dt.bfloat16
U32 = mybir.dt.uint32

P = 128
D = 128
T = 2048
CH = 512
NC = T // CH
NT = T // P
LEAD = 64
ROUND = 12582912.0
MASKED = -3.0e38


@contextmanager
def phase(nc, sems, tiles):
    with ExitStack() as ctx:
        tag = nc.next_id()
        got_tiles = [ctx.enter_context(nc.sbuf_tensor(f"{n}_{tag}", s, d)) for n, s, d in tiles]
        got_sems = [nc.alloc_semaphore(name=f"{n}_{tag}") for n in sems.split()]
        yield (*got_sems, *got_tiles)
        nc.clear_and_free_semaphores(got_sems)
        nc.all_engine_barrier()


class Core:

    def __init__(self, nc, ctx):
        self.nc = nc

        def sb(name, shape, dt=F32):
            return ctx.enter_context(nc.sbuf_tensor(name, shape, dt))

        self.xpad = sb("xpad", [P, T + 1])
        self.xnpad = sb("xnpad", [P, LEAD + T + 1])
        self.scratch = sb("scratch", [P, 4, T])
        self.s1, self.s2, self.s3, self.s4 = (self.scratch[:, n, :] for n in range(4))
        self.mats = sb("mats", [P, N_MATS, P])
        self.mean_mat = sb("mean_mat", [P, P])
        self.cols = sb("cols", [P, 4])
        self.out_stored = ctx.enter_context(nc.semaphore("out_stored"))
        self.psum = ctx.enter_context(nc.psum_tensor("psum", [P, 8 * CH], F32))

    def mat(self, name):
        return self.mats[:, MATS.index(name), :]

    def bank(self, b, n=CH, rows=P):
        return self.psum[0:rows, CH * b:CH * b + n]

    def x(self, c, rows=slice(0, P)):
        return self.xpad[rows, 1 + CH * c:1 + CH * (c + 1)]

    def xn(self, c, shift=0):
        return self.xnpad[:, LEAD + shift + CH * c:LEAD + shift + CH * (c + 1)]

    def xn_tile(self, t):
        return self.xnpad[:, LEAD + P * t:LEAD + P * (t + 1)]

    def eps(self, value):
        return self.cols[:, EPS.index(value):EPS.index(value) + 1]


MATS = ["ident", "heads8", "heads64", "den", "causal", "centre"]
N_MATS = len(MATS)
EPS = [1e-5, 1e-3, 1e-30]


def part(tile, c):
    return tile[:, CH * c:CH * (c + 1)]


def load(k, pairs, zero=()):
    nc = k.nc
    with phase(nc, "landed cleared", []) as (landed, cleared):
        with nc.Block() as block:
            @block.gpsimd
            def _(pool):
                for z in zero:
                    pool.memset(z, 0.0).then_inc(cleared, 1)

            @block.sync
            def _(sp):
                if zero:
                    sp.wait_ge(cleared, len(zero))
                for dst, src in pairs:
                    sp.dma_start(dst, src).then_inc(landed, 16)
                sp.wait_ge(landed, 16 * len(pairs))


def setup(k, x_t, const_mats):
    nc = k.nc
    with phase(nc, "landed cleared", []) as (landed, cleared):
        with nc.Block() as block:
            @block.sync
            def _(sp):
                sp.dma_start(k.xpad[:, 1:1 + T], x_t).then_inc(landed, 16)
                sp.dma_start(k.mats[:, :, :], const_mats).then_inc(landed, 16)
                sp.wait_ge(landed, 32)

            @block.vector
            def _(dve):
                dve.memset(k.mean_mat[:, :], 1.0 / D).then_inc(cleared, 1)
                dve.memset(k.xpad[:, 0:1], 0.0).then_inc(cleared, 1)
                dve.memset(k.xnpad[:, 0:LEAD], 0.0).then_inc(cleared, 1)
                dve.memset(k.xnpad[:, LEAD + T:LEAD + T + 1], 0.0).then_inc(cleared, 1)
                for n, e in enumerate(EPS):
                    dve.memset(k.cols[:, n:n + 1], e).then_inc(cleared, 1)
                dve.wait_ge(cleared, 4 + len(EPS))


def layernorm(k, src, dst, eps, gain=None, bias=None, loads=()):
    nc = k.nc
    names = "centred squared var_done log_done inverted scaled normed landed"
    with phase(nc, names, []) as (centred, squared, var_done, log_done, inverted, scaled, normed, landed):
        with nc.Block() as block:
            @block.sync
            def _(sp):
                for tile, dram in loads:
                    sp.dma_start(tile, dram).then_inc(landed, 16)
                if loads:
                    sp.wait_ge(landed, 16 * len(loads))

            @block.tensor
            def _(pe):
                for c in range(NC):
                    pe.matmul(k.bank(c), k.mat("centre"), src(c), start=True, stop=True).then_inc(centred, 1)
                for c in range(NC):
                    pe.wait_ge(squared, c + 1)
                    pe.matmul(k.bank(4 + c), k.mean_mat[:, :], part(k.s2, c), start=True, stop=True)\
                        .then_inc(var_done, 1)

            @block.scalar
            def _(act):
                act.preload_act_table_set("natural_log_exp_and_others")
                for c in range(NC):
                    act.wait_ge(centred, c + 1)
                    act.activation(part(k.s2, c), k.bank(c), ACT.Square).then_inc(squared, 1)
                for c in range(NC):
                    act.wait_ge(var_done, c + 1)
                    act.activation(part(k.s3, c), k.bank(4 + c), ACT.Ln, bias=k.eps(eps)).then_inc(log_done, 1)
                    act.wait_ge(log_done, c + 1)
                    act.activation(part(k.s1, c), part(k.s3, c), ACT.Exp, scale=-0.5).then_inc(inverted, 1)

            @block.vector
            def _(dve):
                for c in range(NC):
                    dve.wait_ge(inverted, c + 1)
                    dve.tensor_tensor(dst(c), k.bank(c), part(k.s1, c), ALU.mult).then_inc(scaled, 1)
                    if gain is not None:
                        dve.wait_ge(scaled, c + 1)
                        dve.tensor_scalar(dst(c), dst(c), gain, bias, ALU.mult, ALU.add).then_inc(normed, 1)


def project(k, jobs):
    nc = k.nc
    by = {e: [n for n, job in enumerate(jobs) if job[0] == e] for e in ("vector", "scalar")}
    with phase(nc, "product_done left_by_vector left_by_scalar", []) as (product_done, by_vector, by_scalar):
        left = {"vector": by_vector, "scalar": by_scalar}
        with nc.Block() as block:
            @block.tensor
            def _(pe):
                for n, (_, pairs, rows, cols, _) in enumerate(jobs):
                    if n >= 8:
                        e = jobs[n - 8][0]
                        pe.wait_ge(left[e], by[e].index(n - 8) + 1)
                    for i, (lhs, rhs) in enumerate(pairs):
                        mm = pe.matmul(k.bank(n % 8, cols, rows), lhs, rhs,
                                       start=(i == 0), stop=(i == len(pairs) - 1))
                    mm.then_inc(product_done, 1)

            @block.vector
            def _(dve):
                for n in by["vector"]:
                    dve.wait_ge(product_done, n + 1)
                    jobs[n][4](dve, k.bank(n % 8, jobs[n][3], jobs[n][2])).then_inc(by_vector, 1)

            @block.scalar
            def _(act):
                for n in by["scalar"]:
                    act.wait_ge(product_done, n + 1)
                    jobs[n][4](act, k.bank(n % 8, jobs[n][3], jobs[n][2])).then_inc(by_scalar, 1)


def add_to_x(k, c, bias=None):
    def leave(dve, ps):
        if bias is None:
            return dve.tensor_tensor(k.x(c), k.x(c), ps, ALU.add)
        return dve.scalar_tensor_tensor(out=k.x(c), in0=ps, scalar=bias, in1=k.x(c), op0=ALU.add, op1=ALU.add)
    return leave


def copy_out(dst):
    def leave(eng, ps):
        return eng.activation(dst, ps, ACT.Copy)
    return leave


def copy_any(dst):
    def leave(eng, ps):
        if eng.engine == mybir.EngineType.Activation:
            return eng.activation(dst, ps, ACT.Copy)
        return eng.tensor_copy(dst, ps)
    return leave


def linear_attention(k, wq, wkv, y, floor, guard):
    nc = k.nc
    units = 12
    names = "product_done low_done exp_done phi_done v_done ones_done kv_done state_done out_done den_done log_done inverse_done y_done"
    tiles = [("phi_q", [P, T], F32), ("phi_k", [P, NT, P], F32), ("v1", [P, NT, P + 1], F32),
             ("kv_state", [P, P], F32), ("z_state", [P, P], F32), ("z_col", [P, 1], F32)]
    with phase(nc, names, tiles) as (product_done, low_done, exp_done, phi_done, v_done, ones_done, kv_done,
                                     state_done, out_done, den_done, log_done, inverse_done, y_done,
                                     phi_q, phi_k, v1, kv_state, z_state, z_col):
        def views(n):
            if n < 4:
                return k.bank(n), part(k.s1, n), part(k.s2, n), part(phi_q, n)
            m = n - 4
            ps = k.bank(n % 6).rearrange("p (a b) -> p a b", a=2)[:, :, 0:P]
            lo = k.s3[:, 256 * m:256 * m + 256].rearrange("p (a b) -> p a b", a=2)
            ex = y[:, 256 * m:256 * m + 256].rearrange("p (a b) -> p a b", a=2)
            return ps, lo, ex, phi_k[:, 2 * m:2 * m + 2, :]

        with nc.Block() as block:
            @block.tensor
            def _(pe):
                for n in range(units):
                    if n >= 6:
                        pe.wait_ge(phi_done, n - 5)
                        if n - 6 >= 4:
                            pe.wait_ge(v_done, n - 6 - 3)
                    if n < 4:
                        mm = pe.matmul(k.bank(n), wq, k.xn(n), start=True, stop=True)
                    else:
                        for a in range(2):
                            mm = pe.matmul(k.bank(n % 6)[:, 256 * a:256 * a + 256], k.xn_tile(2 * (n - 4) + a), wkv,
                                           start=True, stop=True)
                    mm.then_inc(product_done, 1)
                pe.wait_ge(ones_done, 1)
                for t in range(NT):
                    pe.wait_ge(phi_done, 4 + t // 2 + 1)
                    pe.wait_ge(v_done, t // 2 + 1)
                    mm = pe.matmul(k.bank(6, P + 1), phi_k[:, t, :], v1[:, t, :], start=(t == 0), stop=(t == NT - 1))
                mm.then_inc(kv_done, 1)
                pe.wait_ge(state_done, 3)
                for c in range(NC):
                    if c >= 3:
                        pe.wait_ge(y_done, c - 2)
                    pe.matmul(k.bank(c % 3), kv_state[:, :], part(phi_q, c), start=True, stop=True)
                    pe.matmul(k.bank(3 + c % 3), z_state[:, :], part(phi_q, c), start=True, stop=True).then_inc(out_done, 1)

            @block.scalar
            def _(act):
                act.preload_act_table_set("natural_log_exp_and_others")
                for n in range(units):
                    act.wait_ge(low_done, n + 1)
                    _, lo, ex, _ = views(n)
                    act.activation(ex, lo, ACT.Exp).then_inc(exp_done, 1)
                    if n >= 4:
                        v_ps = k.bank(n % 6).rearrange("p (a b) -> p a b", a=2)[:, :, P:2 * P]
                        act.activation(v1[:, 2 * (n - 4):2 * (n - 4) + 2, 0:P], v_ps, ACT.Copy).then_inc(v_done, 1)
                for c in range(NC):
                    act.wait_ge(den_done, c + 1)
                    act.activation(part(k.s3, c), part(k.s1, c), ACT.Ln).then_inc(log_done, 1)
                    act.wait_ge(log_done, c + 1)
                    act.activation(part(k.s2, c), part(k.s3, c), ACT.Exp, scale=-1.0).then_inc(inverse_done, 1)

            @block.vector
            def _(dve):
                dve.memset(v1[:, :, P:P + 1], 1.0).then_inc(ones_done, 1)
                for n in range(units + 1):
                    if n < units:
                        dve.wait_ge(product_done, n + 1)
                        ps, lo, _, _ = views(n)
                        dve.tensor_scalar(lo, ps, 0.0, None, ALU.min).then_inc(low_done, 1)
                    if n >= 1:
                        dve.wait_ge(exp_done, n)
                        if n - 1 >= 4:
                            dve.wait_ge(v_done, n - 4)
                        ps, _, ex, phi = views(n - 1)
                        dve.scalar_tensor_tensor(out=phi, in0=ps, scalar=0.0, in1=ex, op0=ALU.max, op1=ALU.add)\
                            .then_inc(phi_done, 1)
                dve.wait_ge(kv_done, 1)
                dve.tensor_tensor(kv_state[:, :], k.bank(6, P), k.mat("heads8"), ALU.mult).then_inc(state_done, 1)
                dve.tensor_copy(z_col[:, :], k.bank(6, P + 1)[:, P:P + 1]).then_inc(state_done, 1)
                dve.wait_ge(state_done, 2)
                dve.tensor_scalar(z_state[:, :], k.mat("heads8"), z_col[:, 0:1], None, ALU.mult).then_inc(state_done, 1)
                for c in range(NC + 1):
                    if c < NC:
                        dve.wait_ge(out_done, c + 1)
                        op, bound = (ALU.max, floor) if guard is None else (ALU.add, guard)
                        dve.tensor_scalar(part(k.s1, c), k.bank(3 + c % 3), bound, None, op).then_inc(den_done, 1)
                    if c >= 1:
                        dve.wait_ge(inverse_done, c)
                        dve.tensor_tensor(part(y, c - 1), k.bank((c - 1) % 3), part(k.s2, c - 1), ALU.mult)\
                            .then_inc(y_done, 1)


def layer0_attention(k, A):
    nc = k.nc
    with ExitStack() as ctx:
        w = ctx.enter_context(nc.sbuf_tensor("w_l0a", [P, 4, P], F32))
        vec = ctx.enter_context(nc.sbuf_tensor("vec_l0a", [P, 5], F32))
        y = ctx.enter_context(nc.sbuf_tensor("y_l0a", [P, T], F32))
        layernorm(k, k.x, k.xn, 1e-5, loads=[(w[:, n, :], A[name]) for n, name in enumerate(
            ("L0_attn_WqT", "L0_attn_WkT", "L0_attn_WvT", "L0_attn_WpT"))]
            + [(vec[:, 0:3], A["L0_attn_conv_w"]), (vec[:, 3:4], A["L0_attn_conv_b"]), (vec[:, 4:5], A["L0_attn_bp"])])
        linear_attention(k, w[:, 0, :], w[:, 1:3, :].rearrange("p a b -> p (a b)"), y, 1e-6, None)
        with phase(nc, "middle_done step_done", []) as (middle_done, step_done):
            with nc.Block() as block:
                @block.scalar
                def _(act):
                    for c in range(NC):
                        act.activation(part(k.s1, c), k.xn(c), ACT.Identity, scale=vec[:, 1:2], bias=vec[:, 3:4])\
                            .then_inc(middle_done, 1)

                @block.vector
                def _(dve):
                    for c in range(NC):
                        dve.scalar_tensor_tensor(out=part(y, c), in0=k.xn(c, -1), scalar=vec[:, 0:1], in1=part(y, c),
                                                 op0=ALU.mult, op1=ALU.add).then_inc(step_done, 1)
                        dve.wait_ge(step_done, 3 * c + 1)
                        dve.scalar_tensor_tensor(out=part(y, c), in0=k.xn(c, 1), scalar=vec[:, 2:3], in1=part(y, c),
                                                 op0=ALU.mult, op1=ALU.add).then_inc(step_done, 1)
                        dve.wait_ge(step_done, 3 * c + 2)
                        dve.wait_ge(middle_done, c + 1)
                        dve.tensor_tensor(part(y, c), part(y, c), part(k.s1, c), ALU.add).then_inc(step_done, 1)
        project(k, [("vector", [(w[:, 3, :], part(y, c))], P, CH, add_to_x(k, c, vec[:, 4:5])) for c in range(NC)])


def layer0_ffn(k, A):
    nc = k.nc
    QB, QEPS = 128.0, 1e-5
    with ExitStack() as ctx:
        w = ctx.enter_context(nc.sbuf_tensor("w_l0f", [P, P], F32))
        wq = ctx.enter_context(nc.sbuf_tensor("wq_l0f", [P, P], F32))
        vec = ctx.enter_context(nc.sbuf_tensor("vec_l0f", [P, 2], F32))
        st = ctx.enter_context(nc.sbuf_tensor("st_l0f", [P, 8], F32))
        layernorm(k, k.x, k.xn, 1e-5, loads=[
            (w[:, :], A["L0_ffn_weight"]), (vec[:, 0:1], A["L0_ffn_ln_gamma"]), (vec[:, 1:2], A["L0_ffn_ln_beta"])])
        layernorm(k, k.xn, k.xn, 1e-3, vec[:, 0:1], vec[:, 1:2])
        with phase(nc, "step all_max beta_done", []) as (step, all_max, beta_done):
            with nc.Block() as block:
                @block.tensor
                def _(pe):
                    pe.wait_ge(step, 2)
                    pe.matmul(k.bank(0, 1), k.mean_mat[:, :], st[:, 0:1], start=True, stop=True).then_inc(beta_done, 1)

                @block.gpsimd
                def _(pool):
                    pool.wait_ge(step, 1)
                    pool.partition_all_reduce(st[:, 2:3], st[:, 1:2], P, bass.bass_isa.ReduceOp.max).then_inc(all_max, 1)

                @block.vector
                def _(dve):
                    n = 0

                    def then(ins):
                        ins.then_inc(step, 1)

                    then(dve.tensor_reduce(st[:, 1:2], k.xnpad[:, LEAD:LEAD + T], AX.X, ALU.max, apply_absolute_value=True))
                    then(dve.tensor_reduce(st[:, 0:1], w[:, :], AX.X, ALU.add, apply_absolute_value=True))
                    dve.wait_ge(beta_done, 1)
                    then(dve.tensor_scalar(st[:, 3:4], k.bank(0, 1), 1.0 / D, None, ALU.mult))
                    dve.wait_ge(step, 3)
                    then(dve.tensor_scalar(st[:, 4:5], st[:, 3:4], QEPS, None, ALU.add))
                    dve.wait_ge(step, 4)
                    then(dve.reciprocal(st[:, 5:6], st[:, 4:5]))
                    dve.wait_ge(step, 5)
                    then(dve.tensor_scalar(wq[:, :], w[:, :], st[:, 5:6], ROUND, ALU.mult, ALU.add))
                    dve.wait_ge(step, 6)
                    then(dve.tensor_scalar(wq[:, :], wq[:, :], ROUND, 1.0, ALU.subtract, ALU.min))
                    dve.wait_ge(step, 7)
                    then(dve.tensor_scalar(wq[:, :], wq[:, :], -1.0, None, ALU.max))
                    dve.wait_ge(all_max, 1)
                    then(dve.reciprocal(st[:, 6:7], st[:, 2:3]))
                    dve.wait_ge(step, 9)
                    then(dve.tensor_scalar(st[:, 6:7], st[:, 6:7], QB, None, ALU.mult))
                    then(dve.tensor_scalar(st[:, 7:8], st[:, 3:4], st[:, 2:3], 1.0 / QB, ALU.mult, ALU.mult))
                    dve.wait_ge(step, 11)
                    xn = k.xnpad[:, LEAD:LEAD + T]
                    then(dve.tensor_scalar(xn, xn, st[:, 6:7], QB - QEPS, ALU.mult, ALU.min))
                    dve.wait_ge(step, 12)
                    then(dve.tensor_scalar(xn, xn, QEPS - QB, None, ALU.max))

        def scaled(c):
            def leave(dve, ps):
                return dve.scalar_tensor_tensor(out=k.x(c), in0=ps, scalar=st[:, 7:8], in1=k.x(c),
                                                op0=ALU.mult, op1=ALU.add)
            return leave
        project(k, [("vector", [(wq[:, :], k.xn(c))], P, CH, scaled(c)) for c in range(NC)])


def lookup_ffn(k, w1, w2, hidden):
    nc = k.nc
    tiles = [("raw", [P, 2, CH], F32), ("low", [P, 2, CH], F32), ("grid", [P, 2, CH], F32), ("h", [P, NC, hidden, CH], F32)]
    with phase(nc, "product_done rounded lowered gridded acted out_done added", tiles) as (
            product_done, rounded, lowered, gridded, acted, out_done, added, raw, low, grid, h):
        units = [(c, j) for c in range(NC) for j in range(hidden)]
        with nc.Block() as block:
            @block.tensor
            def _(pe):
                for n, (c, j) in enumerate(units):
                    if n >= 4:
                        pe.wait_ge(rounded, n - 3)
                    pe.matmul(k.bank(n % 4), w1[:, P * j:P * (j + 1)], k.xn(c), start=True, stop=True).then_inc(product_done, 1)
                for c in range(NC):
                    for j in range(hidden):
                        pe.wait_ge(acted, hidden * c + j + 1)
                        mm = pe.matmul(k.bank(4 + c), w2[:, j, :], h[:, c, j, :], start=(j == 0), stop=(j == hidden - 1))
                    mm.then_inc(out_done, 1)

            @block.vector
            def _(dve):
                for n in range(len(units)):
                    dve.wait_ge(product_done, n + 1)
                    dve.tensor_scalar(raw[:, n % 2, :], k.bank(n % 4), 10.0, ROUND, ALU.mult, ALU.add).then_inc(rounded, 1)
                    dve.wait_ge(rounded, n + 1)
                    dve.tensor_scalar(low[:, n % 2, :], raw[:, n % 2, :], ROUND, -128.0, ALU.subtract, ALU.max).then_inc(lowered, 1)
                    dve.wait_ge(lowered, n + 1)
                    if n >= 2:
                        dve.wait_ge(acted, n - 1)
                    dve.tensor_scalar(grid[:, n % 2, :], low[:, n % 2, :], 127.0, 0.1, ALU.min, ALU.mult).then_inc(gridded, 1)
                for c in range(NC):
                    dve.wait_ge(out_done, c + 1)
                    dve.tensor_tensor(k.x(c), k.x(c), k.bank(4 + c), ALU.add).then_inc(added, 1)

            @block.scalar
            def _(act):
                for n, (c, j) in enumerate(units):
                    act.wait_ge(gridded, n + 1)
                    act.activation(h[:, c, j, :], grid[:, n % 2, :], ACT.Gelu_apprx_tanh).then_inc(acted, 1)


def layer2_attention(k, A):
    nc = k.nc
    with ExitStack() as ctx:
        w = ctx.enter_context(nc.sbuf_tensor("w_l2a", [P, 4, P], F32))
        w1 = ctx.enter_context(nc.sbuf_tensor("w1_l2a", [P, 512], F32))
        w2 = ctx.enter_context(nc.sbuf_tensor("w2_l2a", [P, 4, P], F32))
        vec = ctx.enter_context(nc.sbuf_tensor("vec_l2a", [P, 4], F32))
        y = ctx.enter_context(nc.sbuf_tensor("y_l2a", [P, T], F32))
        weights = ([(vec[:, n:n + 1], A["L2_attn_" + name]) for n, name in enumerate(("ln1_g", "ln1_b", "ln2_g", "ln2_b"))]
                   + [(w[:, n, :], A["L2_attn_" + name]) for n, name in enumerate(("wq", "wk", "wv", "wo"))]
                   + [(w1[:, :], A["L2_attn_w1"]), (w2[:, :, :], A["L2_attn_w2"].rearrange("(j p) d -> p j d", p=P))])
        z = ctx.enter_context(nc.sbuf_tensor("z_l2a", [P, T], F32))

        def z_part(c):
            return part(z, c)

        layernorm(k, k.x, z_part, 1e-5, loads=weights)
        layernorm(k, z_part, k.xn, 1e-5, vec[:, 0:1], vec[:, 1:2])
        linear_attention(k, w[:, 0, :], w[:, 1:3, :].rearrange("p a b -> p (a b)"), y, None, 1e-6)
        project(k, [("vector", [(w[:, 3, :], part(y, c))], P, CH, lambda dve, ps, c=c: dve.tensor_tensor(
            z_part(c), z_part(c), ps, ALU.add)) for c in range(NC)])
        layernorm(k, z_part, k.xn, 1e-5, vec[:, 2:3], vec[:, 3:4])
        add_tile(k, z[:, :])
        lookup_ffn(k, w1, w2, 4)


def add_tile(k, tile):
    nc = k.nc
    with phase(nc, "added", []) as (added,):
        with nc.Block() as block:
            @block.vector
            def _(dve):
                dve.tensor_tensor(k.xpad[:, 1:1 + T], k.xpad[:, 1:1 + T], tile, ALU.add).then_inc(added, 1)


def store(k, out):
    with k.nc.Block() as block:
        @block.sync
        def _(sp):
            sp.dma_start(out, k.xpad[:, 1:1 + T]).then_inc(k.out_stored, 16)
            sp.wait_ge(k.out_stored, 16)


def split_into_bf16(k, qk_w, rope, pieces, pieces_dram):
    nc = k.nc
    units = [(m, c) for m in range(2) for c in range(NC)]
    names = "straight_done turned_done by_cos by_sin rotated high_done rest_done middle_done low_done cleared stored"
    tiles = [("cos_part", [P, 2, CH], F32), ("sin_part", [P, 2, CH], F32), ("value", [P, 2, CH], F32), ("rest", [P, 2, CH], F32)]
    with phase(nc, names, tiles) as (straight_done, turned_done, by_cos, by_sin, rotated, high_done, rest_done, middle_done,
                                     low_done, cleared, stored, cos_part, sin_part, value, rest):
        with nc.Block() as block:
            @block.gpsimd
            def _(pool):
                for n in range(4):
                    pool.memset(k.scratch[:, n, :], 0.0).then_inc(cleared, 1)

            @block.sync
            def _(sp):
                for n, (m, c) in enumerate(units):
                    sp.wait_ge(high_done, n + 1)
                    sp.wait_ge(middle_done, n + 1)
                    sp.wait_ge(low_done, n + 1)
                    there = pieces_dram[m, :, :, CH * c:CH * (c + 1)].rearrange("a p t -> p a t")
                    sp.dma_start(there, pieces[:, m, :, CH * c:CH * (c + 1)]).then_inc(stored, 16)
                sp.wait_ge(stored, 16 * len(units))

            @block.tensor
            def _(pe):
                for n, (m, c) in enumerate(units):
                    if n >= 2:
                        pe.wait_ge(by_cos, n - 1)
                        pe.wait_ge(by_sin, n - 1)
                    pe.matmul(k.bank(n % 2), qk_w[:, 2 * m, :], k.xn(c), start=True, stop=True).then_inc(straight_done, 1)
                    pe.matmul(k.bank(2 + n % 2), qk_w[:, 2 * m + 1, :], k.xn(c), start=True, stop=True).then_inc(turned_done, 1)

            @block.vector
            def _(dve):
                for n, (m, c) in enumerate(units):
                    dve.wait_ge(straight_done, n + 1)
                    dve.tensor_tensor(cos_part[:, n % 2, :], k.bank(n % 2), part(rope[:, 0, :], c), ALU.mult).then_inc(by_cos, 1)
                    dve.wait_ge(turned_done, n + 1)
                    dve.tensor_tensor(sin_part[:, n % 2, :], k.bank(2 + n % 2), part(rope[:, 1, :], c), ALU.mult)\
                        .then_inc(by_sin, 1)
                    dve.wait_ge(by_cos, n + 1)
                    dve.wait_ge(by_sin, n + 1)
                    if n >= 2:
                        dve.wait_ge(high_done, n - 1)
                    dve.tensor_tensor(value[:, n % 2, :], cos_part[:, n % 2, :], sin_part[:, n % 2, :], ALU.add).then_inc(rotated, 1)
                    dve.wait_ge(high_done, n + 1)
                    if n >= 2:
                        dve.wait_ge(middle_done, n - 1)
                    dve.tensor_tensor(rest[:, n % 2, :], value[:, n % 2, :], pieces[:, m, 0, CH * c:CH * (c + 1)], ALU.subtract)\
                        .then_inc(rest_done, 1)
                    dve.wait_ge(middle_done, n + 1)
                    dve.tensor_tensor(pieces[:, m, 2, CH * c:CH * (c + 1)], rest[:, n % 2, :],
                                      pieces[:, m, 1, CH * c:CH * (c + 1)], ALU.subtract).then_inc(low_done, 1)

            @block.scalar
            def _(act):
                for n, (m, c) in enumerate(units):
                    act.wait_ge(rotated, n + 1)
                    act.activation(pieces[:, m, 0, CH * c:CH * (c + 1)], value[:, n % 2, :], ACT.Copy).then_inc(high_done, 1)
                    act.wait_ge(rest_done, n + 1)
                    act.activation(pieces[:, m, 1, CH * c:CH * (c + 1)], rest[:, n % 2, :], ACT.Copy).then_inc(middle_done, 1)


def softmax_schedule():
    order = []
    units = 4 * NT * NC
    steps = NC * NT * 2
    order += [("tops", 0, u) for u in range(0, units, NC)] + [("close", 0, 0)]
    for g in range(4):
        done = 0
        for m in range(steps):
            order.append(("step", g, m))
            upto = min(units, (m + 1) * units // (steps - 14)) if g < 3 else 0
            tops = [("top", g + 1, u) for u in range(done, upto)]
            if m % 2 and m >= 3:
                order += tops[:1] + [("mix", g, m - 3)] + tops[1:]
            else:
                order += tops
            if upto == units and done < units:
                order.append(("close", g + 1, 0))
            done = upto
        order.append(("mix", g, steps - 2))
    return order


def grouped_attention(k, pieces_dram, v_w, v_pad, mixed_heads):
    nc = k.nc
    order = softmax_schedule()
    R = 96
    BUFS = 3
    units, steps = 4 * NT * NC, NC * NT * 2
    names = ("ones_set zeros_set v_done v_copied loaded_0 loaded_1 loaded_2 top_scored top_found closed turned high_done rest_done middle_done low_done laid_out scored "
             "exped mixed emptied")
    tiles = [("qs", [P, BUFS, 4, T], BF16), ("ks", [P, BUFS, 4, T], BF16), ("probs_t", [P, 4, 2 * CH], F32),
             ("tops", [P, 4 * NT, NC], F32), ("neg_max", [P, 4 * NT], F32), ("max_pieces", [4 * NT, 3, P], BF16),
             ("rest", [4 * NT, P], F32)]
    with phase(nc, names, tiles) as (ones_set, zeros_set, v_done, v_copied, loaded_0, loaded_1, loaded_2, top_scored, top_found, closed, turned, high_done, rest_done, middle_done,
                                     low_done, laid_out, scored, exped, mixed, emptied, qs, ks, probs_t, tops, neg_max,
                                     max_pieces, rest):
        loaded = (loaded_0, loaded_1, loaded_2)

        def found(g, u):
            return (u + 1) // NC if g == 0 else units // NC + units * (g - 1) + u + 1

        def top_bank(u):
            return k.bank(4 + u % 3)

        with nc.Block() as block:
            @block.gpsimd
            def _(pool):
                for b in range(BUFS):
                    pool.memset(qs[64:96, b, :, :], 0.0).then_inc(zeros_set, 1)
                    if b:
                        pool.wait_ge(zeros_set, 2 * b)
                        pool.memset(ks[64:P, b, :, :], 1.0).then_inc(zeros_set, 1)
                        pool.wait_ge(zeros_set, 2 * b + 1)

            @block.sync
            def _(sp):
                def load_group(g):
                    if g >= BUFS:
                        sp.wait_ge(scored, steps * (g - BUFS + 1))
                    for a in range(3):
                        q_src = pieces_dram[0, a, 32 * g:32 * g + 32, :].rearrange("(j d) t -> d j t", d=8)
                        k_src = pieces_dram[1, :, 32 * g:32 * g + 32, :].rearrange("b (j d) t -> b d j t", d=8)
                        for b in range(3):
                            r = 24 * a + 8 * b
                            sp.dma_start(qs[r:r + 8, g % BUFS, :, :], q_src).then_inc(loaded[g % BUFS], 16)
                            sp.dma_start(ks[r:r + 8, g % BUFS, :, :], k_src[b]).then_inc(loaded[g % BUFS], 16)

                def lay_out(g):
                    sp.wait_ge(low_done, g + 1)
                    for a in range(3):
                        dst = qs[R + a:R + a + 1, g % BUFS, :, :].rearrange("p j (t q) -> p (j t) q", q=P)
                        sp.dma_start(dst, max_pieces[:, a, :]).then_inc(laid_out, 16)

                for g in range(BUFS):
                    if g == 0:
                        sp.wait_ge(ones_set, 1)
                    sp.wait_ge(zeros_set, 2 * g + 1)
                    load_group(g)
                lay_out(0)
                for g in range(1, 4):
                    lay_out(g)
                    if g + BUFS - 1 < 4:
                        load_group(g + BUFS - 1)
                sp.wait_ge(laid_out, 48 * 4)

            @block.tensor
            def _(pe):
                def mix(g, m):
                    qc, kt, pair = m // (2 * NT), m // 2 % NT, m % 2
                    pe.wait_ge(exped, steps * g + m + 1)
                    if kt == 0 and pair == 0 and NC * g + qc >= 1:
                        pe.wait_ge(emptied, NC * g + qc)
                    for i in range(2):
                        j = 2 * pair + i
                        mm = pe.matmul(k.bank(7)[32 * j:32 * j + 32, :],
                                       v_pad[:, kt, 4 * g + j, :], probs_t[:, m % 4, CH * i:CH * (i + 1)],
                                       start=(kt == 0), stop=(kt == NT - 1))
                    mm.then_inc(mixed, 1)

                for t in range(NT):
                    mm = pe.matmul(k.bank(t // 4)[:, P * (t % 4):P * (t % 4 + 1)], k.xn_tile(t), v_w[:, :], start=True, stop=True)
                    if t % 4 == 3:
                        mm.then_inc(v_done, 1)
                for kind, g, m in order:
                    if kind == "tops":
                        j, t = m // (NT * NC), m // NC % NT
                        if m == 0:
                            pe.wait_ge(loaded[0], 16 * 18)
                            pe.wait_ge(v_copied, 4)
                            pe.wait_ge(ones_set, 2)
                        if m >= 2 * NC:
                            pe.wait_ge(top_found, m // NC - 1)
                        for c in range(NC):
                            mm = pe.matmul(k.bank(4 * (m // NC % 2) + c), qs[0:R, 0, j, P * t:P * (t + 1)],
                                           ks[0:R, 0, j, CH * c:CH * (c + 1)], start=True, stop=True)
                        mm.then_inc(top_scored, 1)
                    elif kind == "top":
                        j, t, c = m // (NT * NC), m // NC % NT, m % NC
                        if m == 0:
                            pe.wait_ge(loaded[g % BUFS], 16 * 18 * (g // BUFS + 1))
                            pe.wait_ge(low_done, g)
                        if g >= 2 or m >= 3:
                            pe.wait_ge(top_found, found(g, m) - 3)
                        pe.matmul(top_bank(m), qs[0:R, g % BUFS, j, P * t:P * (t + 1)], ks[0:R, g % BUFS, j, CH * c:CH * (c + 1)],
                                  start=True, stop=True).then_inc(top_scored, 1)
                    elif kind == "close":
                        pe.wait_ge(closed, g + 1)
                        pe.transpose(k.bank(4, P, 4 * NT), neg_max[:, :], k.mat("ident")).then_inc(turned, 1)
                    elif kind == "mix":
                        mix(g, m)
                        mix(g, m + 1)
                    else:
                        qc, kt, pair = m // (2 * NT), m // 2 % NT, m % 2
                        if m == 0:
                            pe.wait_ge(laid_out, 48 * (g + 1))
                        if steps * g + m >= 2:
                            pe.wait_ge(exped, steps * g + m - 1)
                        if g == 0 and m == 0:
                            pe.wait_ge(closed, 1)
                        for i in range(2):
                            j = 2 * pair + i
                            mm = pe.matmul(k.bank(2 * (m % 2) + i), ks[0:R + 3, g % BUFS, j, P * kt:P * (kt + 1)],
                                           qs[0:R + 3, g % BUFS, j, CH * qc:CH * (qc + 1)], start=True, stop=True)
                        mm.then_inc(scored, 1)

            @block.scalar
            def _(act):
                for b in range(4):
                    act.wait_ge(v_done, b + 1)
                    act.activation(v_pad[:, 4 * b:4 * b + 4, :, 0:8], k.bank(b).rearrange("p (t h e) -> p t h e", t=4, e=8),
                                   ACT.Copy).then_inc(v_copied, 1)
                for kind, g, m in order:
                    if kind != "step":
                        continue
                    n = steps * g + m
                    act.wait_ge(scored, n + 1)
                    if n >= 4:
                        act.wait_ge(mixed, n - 3)
                    act.activation(probs_t[:, m % 4, :], k.psum[:, 2 * CH * (m % 2):2 * CH * (m % 2) + 2 * CH], ACT.Exp,
                                   scale=8.0 ** -0.5).then_inc(exped, 1)

            @block.vector
            def _(dve):
                def empty(g, qc):
                    dve.wait_ge(mixed, steps * g + 2 * NT * (qc + 1))
                    dve.tensor_copy(mixed_heads[:, g, CH * qc:CH * (qc + 1)], k.bank(7)).then_inc(emptied, 1)

                dve.memset(ks[64:P, 0, :, :], 1.0).then_inc(ones_set, 1)
                dve.memset(v_pad[:, :, :, 8:9].rearrange("p t h e -> p t (h e)"), 1.0).then_inc(ones_set, 1)
                for kind, g, m in order:
                    if kind == "tops":
                        dve.wait_ge(top_scored, m // NC + 1)
                        four = k.psum[:, 4 * CH * (m // NC % 2):4 * CH * (m // NC % 2) + 4 * CH].rearrange("p (c n) -> p c n", c=4)
                        dve.tensor_reduce(tops[:, m // NC, :], four, AX.X, ALU.max).then_inc(top_found, 1)
                    elif kind == "top":
                        dve.wait_ge(top_scored, found(g, m))
                        dve.tensor_reduce(tops[:, m // NC, m % NC:m % NC + 1], top_bank(m), AX.X, ALU.max)\
                            .then_inc(top_found, 1)
                    elif kind == "close":
                        dve.wait_ge(top_found, found(g, units - 1))
                        dve.tensor_reduce(neg_max[:, :], tops[:, :, :], AX.X, ALU.max, negate=True).then_inc(closed, 1)
                        dve.wait_ge(turned, g + 1)
                        if g >= 1:
                            dve.wait_ge(laid_out, 48 * g)
                        row = k.bank(4, P, 4 * NT)
                        dve.tensor_copy(max_pieces[:, 0, :], row).then_inc(high_done, 1)
                        dve.wait_ge(high_done, g + 1)
                        dve.tensor_tensor(rest[:, :], row, max_pieces[:, 0, :], ALU.subtract).then_inc(rest_done, 1)
                        dve.wait_ge(rest_done, g + 1)
                        dve.tensor_copy(max_pieces[:, 1, :], rest[:, :]).then_inc(middle_done, 1)
                        dve.wait_ge(middle_done, g + 1)
                        dve.tensor_tensor(max_pieces[:, 2, :], rest[:, :], max_pieces[:, 1, :], ALU.subtract).then_inc(low_done, 1)
                    elif kind == "mix" and m % (2 * NT) == 2 * NT - 2:
                        empty(g, m // (2 * NT))


def layer1_attention(k, A):
    nc = k.nc
    with ExitStack() as ctx:
        def sb(name, shape, dt=F32):
            return ctx.enter_context(nc.sbuf_tensor(name + "_l1a", shape, dt))

        qk_w, v_w, out_w, bias = sb("qk_w", [P, 4, P]), sb("v_w", [P, P]), sb("out_w", [P, 4, P]), sb("bias", [P, 1])
        mixed_heads = sb("mixed_heads", [P, 4, T])
        v_pad = k.scratch[:, :, :].rearrange("p a b -> p (a b)").rearrange("p (t h e) -> p t h e", t=NT, h=16)
        pieces_dram = nc.dram_tensor("pieces_dram", (2, 3, P, T), BF16).ap()
        out_rows = [(out_w[32 * j:32 * j + 8, g, :], A["L1_attn_outT"][8 * (4 * g + j):8 * (4 * g + j) + 8, :])
                    for g in range(4) for j in range(4)]
        with nc.sbuf_tensor("rope_l1a", [P, 2, T], F32) as rope, nc.sbuf_tensor("pieces_l1a", [P, 2, 3, T], BF16) as pieces:
            with phase(nc, "cleared", []) as (cleared,):
                with nc.Block() as block:
                    @block.vector
                    def _(dve):
                        dve.memset(out_w[:, :, :], 0.0).then_inc(cleared, 1)
            layernorm(k, k.x, k.xn, 1e-5, loads=[
                (qk_w[:, :, :], A["L1_attn_qkT"]), (rope[:, :, :], A["const_rope"]), (v_w[:, :], A["L1_attn_vT"]),
                (bias[:, :], A["L1_attn_b_out"])] + out_rows)
            split_into_bf16(k, qk_w, rope, pieces, pieces_dram)
        grouped_attention(k, pieces_dram, v_w, v_pad, mixed_heads)

        with phase(nc, "spread log_done inverted divided", [("log", [P, 2, CH], F32), ("inv", [P, 2, CH], F32)]) as (
                spread, log_done, inverted, divided, log, inv):
            units = [(g, c) for g in range(4) for c in range(NC)]
            with nc.Block() as block:
                @block.tensor
                def _(pe):
                    for n, (g, c) in enumerate(units):
                        if n >= 4:
                            pe.wait_ge(log_done, n - 3)
                        pe.matmul(k.bank(n % 4), k.mat("den"), part(mixed_heads[:, g, :], c), start=True, stop=True)\
                            .then_inc(spread, 1)

                @block.scalar
                def _(act):
                    act.preload_act_table_set("natural_log_exp_and_others")
                    for n in range(len(units)):
                        act.wait_ge(spread, n + 1)
                        if n >= 2:
                            act.wait_ge(inverted, n - 1)
                        act.activation(log[:, n % 2, :], k.bank(n % 4), ACT.Ln).then_inc(log_done, 1)
                        act.wait_ge(log_done, n + 1)
                        if n >= 2:
                            act.wait_ge(divided, n - 1)
                        act.activation(inv[:, n % 2, :], log[:, n % 2, :], ACT.Exp, scale=-1.0).then_inc(inverted, 1)

                @block.vector
                def _(dve):
                    for n, (g, c) in enumerate(units):
                        dve.wait_ge(inverted, n + 1)
                        u = part(mixed_heads[:, g, :], c)
                        dve.tensor_tensor(u, u, inv[:, n % 2, :], ALU.mult).then_inc(divided, 1)
        project(k, [("vector", [(out_w[:, g, :], part(mixed_heads[:, g, :], c)) for g in range(4)], P, CH,
                     add_to_x(k, c, bias[:, 0:1])) for c in range(NC)])


def shifted_tokens(k, src_pad, h, n_chunks=NC):
    nc = k.nc
    with phase(nc, "low_copied high_copied", []) as (low_copied, high_copied):
        with nc.Block() as block:
            @block.vector
            def _(dve):
                dve.tensor_copy(h[0:64, :], src_pad[0:64, 1:1 + T]).then_inc(low_copied, 1)

            @block.scalar
            def _(act):
                act.activation(h[64:P, :], src_pad[64:P, 0:T], ACT.Copy).then_inc(high_copied, 1)


def window_qk(k, w_qk, w_turned, columns, xpos_dram, q_pad, keys):
    nc = k.nc
    units = [(c, m) for c in range(NC) for m in range(8)]
    names = "landed_even landed_odd projected turned squared summed log_done inverted by_cos by_sin added rotated cleared"
    tiles = [("xpos", [P, 2, 4, CH], F32)]
    with phase(nc, names, tiles) as (landed_even, landed_odd, projected, turned, squared, summed, log_done, inverted, by_cos,
                                     by_sin, added, rotated, cleared, xpos):
        landed = (landed_even, landed_odd)
        buffers = k.scratch[:, :, :].rearrange("p a (b t) -> p a b t", t=CH)
        sq, log, inv = buffers[:, 0, 0:2, :], buffers[:, 0, 2:4, :], buffers[:, 1, 0:2, :]
        cos_part, sin_part, both = buffers[:, 1, 2:4, :], buffers[:, 2, 0:2, :], buffers[:, 2, 2:4, :]
        rotations = [0]
        for _, m in units:
            rotations.append(rotations[-1] + (2 if m < 4 else 1))

        with nc.Block() as block:
            @block.sync
            def _(sp):
                for c in range(NC):
                    if c >= 2:
                        sp.wait_ge(by_cos, 8 * (c - 1))
                        sp.wait_ge(by_sin, 8 * (c - 1))
                    sp.dma_start(xpos[:, c % 2, :, :], xpos_dram[:, :, CH * c:CH * (c + 1)]).then_inc(landed[c % 2], 16)
                for parity in range(2):
                    sp.wait_ge(landed[parity], 16 * NC // 2)

            @block.tensor
            def _(pe):
                for n in range(len(units) + 1):
                    if n < len(units):
                        c, m = units[n]
                        if n >= 3:
                            pe.wait_ge(by_cos, n - 2)
                        pe.matmul(k.bank(n % 3), w_qk[:, P * m:P * (m + 1)], k.xn(c), start=True, stop=True)\
                            .then_inc(projected, 1)
                        if n >= 3:
                            pe.wait_ge(by_sin, n - 2)
                        pe.matmul(k.bank(3 + n % 3), w_turned[:, P * m:P * (m + 1)], k.xn(c), start=True, stop=True)\
                            .then_inc(turned, 1)
                    if n >= 1:
                        u = n - 1
                        pe.wait_ge(squared, u + 1)
                        if u >= 2:
                            pe.wait_ge(log_done, u - 1)
                        pe.matmul(k.bank(6 + u % 2), k.mat("heads64"), sq[:, u % 2, :], start=True, stop=True)\
                            .then_inc(summed, 1)

            @block.scalar
            def _(act):
                act.preload_act_table_set("natural_log_exp_and_others")
                for n in range(len(units) + 1):
                    if n < len(units):
                        act.wait_ge(projected, n + 1)
                        if n >= 2:
                            act.wait_ge(summed, n - 1)
                        act.activation(sq[:, n % 2, :], k.bank(n % 3), ACT.Square).then_inc(squared, 1)
                    if n >= 1:
                        u = n - 1
                        act.wait_ge(summed, u + 1)
                        act.activation(log[:, u % 2, :], k.bank(6 + u % 2), ACT.Ln, bias=k.eps(1e-30)).then_inc(log_done, 1)
                        act.wait_ge(log_done, u + 1)
                        if u >= 2:
                            act.wait_ge(rotated, rotations[u - 1])
                        act.activation(inv[:, u % 2, :], log[:, u % 2, :], ACT.Exp, scale=-0.5).then_inc(inverted, 1)

            @block.gpsimd
            def _(pool):
                pool.memset(q_pad[64:P, :, 0, :], 0.0).then_inc(cleared, 1)
                pool.wait_ge(cleared, 1)
                pool.memset(q_pad[0:64, :, 1, :], 0.0).then_inc(cleared, 1)
                pool.wait_ge(cleared, 2)
                pool.memset(keys[:, :, 0:64], 0.0).then_inc(cleared, 1)
                pool.wait_ge(cleared, 3)
                for n in range(len(units)):
                    pool.wait_ge(by_cos, n + 1)
                    pool.wait_ge(by_sin, n + 1)
                    if n >= 2:
                        pool.wait_ge(rotated, rotations[n - 1])
                    pool.tensor_tensor(both[:, n % 2, :], cos_part[:, n % 2, :], sin_part[:, n % 2, :], ALU.add)\
                        .then_inc(added, 1)

            @block.vector
            def _(dve):
                for n in range(len(units) + 1):
                    if n < len(units):
                        c, m = units[n]
                        table, scale = 2 * (m // 4), 2 * (m // 4)
                        if m == 0:
                            dve.wait_ge(landed[c % 2], 16 * (c // 2 + 1))
                        dve.wait_ge(squared, n + 1)
                        if n >= 2:
                            dve.wait_ge(added, n - 1)
                        dve.scalar_tensor_tensor(out=cos_part[:, n % 2, :], in0=k.bank(n % 3), scalar=columns[:, scale:scale + 1],
                                                 in1=xpos[:, c % 2, table, :], op0=ALU.mult, op1=ALU.mult).then_inc(by_cos, 1)
                        dve.wait_ge(turned, n + 1)
                        dve.scalar_tensor_tensor(out=sin_part[:, n % 2, :], in0=k.bank(3 + n % 3),
                                                 scalar=columns[:, scale + 1:scale + 2], in1=xpos[:, c % 2, table + 1, :],
                                                 op0=ALU.mult, op1=ALU.mult).then_inc(by_sin, 1)
                    if n >= 1:
                        u = n - 1
                        c, m = units[u]
                        dve.wait_ge(added, u + 1)
                        dve.wait_ge(inverted, u + 1)
                        if m < 4:
                            places = [(slice(64 * s, 64 * s + 64), q_pad[64 * s:64 * s + 64, m, s, CH * c:CH * (c + 1)])
                                      for s in range(2)]
                        else:
                            places = [(slice(0, P), keys[:, m - 4, 64 + CH * c:64 + CH * (c + 1)])]
                        for rows, place in places:
                            dve.scalar_tensor_tensor(out=place, in0=inv[rows, u % 2, :], scalar=1e12, in1=both[rows, u % 2, :],
                                                     op0=ALU.min, op1=ALU.mult).then_inc(rotated, 1)


def window_attention(k, q_pad, keys, wv, bands, ident, o):
    nc = k.nc
    names = ("v_done v_copied_low v_copied_high scored max_done exp_done inverted scaled transposed copied_low copied_high "
             "mixed out_done")
    tiles = [("s", [P, 2, 8, P], F32), ("probs_t", [P, 2, 8, P], F32), ("v", [P, 2, 2, CH], F32),
             ("neg_max", [P, 2, 8], F32), ("total", [P, 2, 8], F32), ("inv", [P, 2, 8], F32)]
    with phase(nc, names, tiles) as (v_done, v_copied_low, v_copied_high, scored, max_done, exp_done, inverted, scaled,
                                     transposed, copied_low, copied_high, mixed, out_done, s, probs_t, v, neg_max, total, inv):
        def scores(t):
            return k.psum[:, 2 * CH * (t % 2):2 * CH * (t % 2) + 2 * CH].rearrange("p (h j) -> p h j", h=8)

        with nc.Block() as block:
            @block.tensor
            def _(pe):
                def values(t, r):
                    w = 2 * t + r
                    if w >= 1:
                        if r == 0:
                            pe.wait_ge(v_copied_high, t)
                        else:
                            pe.wait_ge(v_copied_low, t + 1)
                    first = LEAD + 64 * (w - 1)
                    pe.matmul(k.bank(4), k.xnpad[:, first:first + P], wv, start=True, stop=True).then_inc(v_done, 1)

                for t in range(NT + 1):
                    if t < NT:
                        values(t, 0)
                        if t >= 2:
                            pe.wait_ge(exp_done, t - 1)
                        for half in range(2):
                            pe.matmul(k.bank(2 * (t % 2) + half), ident[:, :], bands[:, min(t, 1), :, :], start=True, stop=False)
                            for i in range(4):
                                h = 4 * half + i
                                for r in range(2):
                                    w = 2 * t + r
                                    mm = pe.matmul(scores(t)[64 * r:64 * r + 64, h, :],
                                                   q_pad[:, h // 2, h % 2, 64 * w:64 * w + 64],
                                                   keys[:, h // 2, 64 * w:64 * w + P], start=False, stop=(i == 3))
                        mm.then_inc(scored, 1)
                    if t >= 1:
                        u = t - 1
                        pe.wait_ge(scaled, u + 1)
                        if u >= 1:
                            pe.wait_ge(copied_low, u)
                            pe.wait_ge(copied_high, u)
                        for h in range(8):
                            mm = pe.transpose(k.bank(5 + h // 4)[:, P * (h % 4):P * (h % 4 + 1)], s[:, u % 2, h, :],
                                              k.mat("ident"))
                        mm.then_inc(transposed, 1)
                    if t < NT:
                        values(t, 1)
                    if t >= 1:
                        u = t - 1
                        pe.wait_ge(copied_low, u + 1)
                        pe.wait_ge(copied_high, u + 1)
                        pe.wait_ge(v_copied_low, u + 1)
                        pe.wait_ge(v_copied_high, u + 1)
                        if u >= 1:
                            pe.wait_ge(out_done, u)
                        for m in range(4):
                            for r in range(2):
                                for i in range(2):
                                    h = 2 * m + i
                                    mm = pe.matmul(k.bank(7)[64 * i:64 * i + 64, P * m + 64 * r:P * m + 64 * r + 64],
                                                   v[:, u % 2, r, 64 * h:64 * h + 64], probs_t[:, u % 2, h, 64 * r:64 * r + 64],
                                                   start=True, stop=True)
                        mm.then_inc(mixed, 1)

            @block.vector
            def _(dve):
                for t in range(NT + 1):
                    if t < NT:
                        dve.wait_ge(v_done, 2 * t + 1)
                        if t >= 2:
                            dve.wait_ge(mixed, t - 1)
                        dve.tensor_copy(v[:, t % 2, 0, :], k.bank(4)).then_inc(v_copied_low, 1)
                    if t >= 1:
                        u = t - 1
                        dve.wait_ge(exp_done, u + 1)
                        dve.reciprocal(inv[:, u % 2, :], total[:, u % 2, :]).then_inc(inverted, 1)
                        dve.wait_ge(inverted, u + 1)
                        share = inv[:, u % 2, :].unsqueeze(2).to_broadcast([P, 8, P])
                        dve.tensor_tensor(s[:, u % 2, :, :], s[:, u % 2, :, :], share, ALU.mult).then_inc(scaled, 1)
                    if t < NT:
                        dve.wait_ge(scored, t + 1)
                        dve.tensor_reduce(neg_max[:, t % 2, :], scores(t), AX.X, ALU.max, negate=True).then_inc(max_done, 1)
                    if t >= 1:
                        u = t - 1
                        dve.wait_ge(transposed, u + 1)
                        if u >= 2:
                            dve.wait_ge(mixed, u - 1)
                        dve.tensor_copy(probs_t[:, u % 2, 0:4, :].rearrange("p a b -> p (a b)"), k.bank(5)).then_inc(copied_low, 1)

            @block.scalar
            def _(act):
                act.preload_act_table_set("natural_log_exp_and_others")
                for t in range(NT + 1):
                    if t >= 1:
                        u = t - 1
                        act.wait_ge(transposed, u + 1)
                        if u >= 2:
                            act.wait_ge(mixed, u - 1)
                        act.activation(probs_t[:, u % 2, 4:8, :].rearrange("p a b -> p (a b)"), k.bank(6), ACT.Copy)\
                            .then_inc(copied_high, 1)
                    if t < NT:
                        act.wait_ge(v_done, 2 * t + 2)
                        if t >= 2:
                            act.wait_ge(mixed, t - 1)
                        act.activation(v[:, t % 2, 1, :], k.bank(4), ACT.Copy).then_inc(v_copied_high, 1)
                        act.wait_ge(max_done, t + 1)
                        if t >= 2:
                            act.wait_ge(transposed, t - 1)
                        for h in range(8):
                            ins = act.activation(s[:, t % 2, h, :], scores(t)[:, h, :], ACT.Exp,
                                                 bias=neg_max[:, t % 2, h:h + 1], accum_out=total[:, t % 2, h:h + 1])
                        ins.then_inc(exp_done, 1)
                    if t >= 1:
                        u = t - 1
                        act.wait_ge(mixed, u + 1)
                        act.activation(o[:, :, P * u:P * (u + 1)], k.bank(7).rearrange("p (a b) -> p a b", a=4), ACT.Copy)\
                            .then_inc(out_done, 1)


def gated_ffn(k, xn, w1, b1, w2, b2, z, hidden):
    nc = k.nc
    rows = [min(P, hidden - P * j) for j in range(3)]
    units = [(c, j) for c in range(NC) for j in range(3)]
    with phase(nc, "gate_done value_done acted gated out_done added",
               [("gelu", [P, 2, CH], F32), ("h", [P, 3, T], F32)]) as (
            gate_done, value_done, acted, gated, out_done, added, gelu, h):
        with nc.Block() as block:
            @block.tensor
            def _(pe):
                for n, (c, j) in enumerate(units):
                    r = rows[j]
                    if n >= 2:
                        pe.wait_ge(acted, n - 1)
                    pe.matmul(k.bank(n % 2, CH, r), w1[:, hidden + P * j:hidden + P * j + r], xn(c), start=True, stop=True)\
                        .then_inc(gate_done, 1)
                    if n >= 2:
                        pe.wait_ge(gated, n - 1)
                    pe.matmul(k.bank(2 + n % 2, CH, r), w1[:, P * j:P * j + r], xn(c), start=True, stop=True)\
                        .then_inc(value_done, 1)
                for c in range(NC):
                    pe.wait_ge(gated, 3 * c + 3)
                    for j in range(3):
                        mm = pe.matmul(k.bank(4 + c), w2[0:rows[j], j, :], h[0:rows[j], j, CH * c:CH * (c + 1)],
                                       start=(j == 0), stop=(j == 2))
                    mm.then_inc(out_done, 1)

            @block.scalar
            def _(act):
                for n, (c, j) in enumerate(units):
                    r = rows[j]
                    act.wait_ge(gate_done, n + 1)
                    if n >= 2:
                        act.wait_ge(gated, n - 1)
                    act.activation(gelu[0:r, n % 2, :], k.bank(n % 2, CH, r), ACT.Gelu, bias=b1[0:r, 3 + j:4 + j]).then_inc(acted, 1)

            @block.vector
            def _(dve):
                for n, (c, j) in enumerate(units):
                    r = rows[j]
                    dve.wait_ge(value_done, n + 1)
                    dve.wait_ge(acted, n + 1)
                    dve.scalar_tensor_tensor(out=h[0:r, j, CH * c:CH * (c + 1)], in0=k.bank(2 + n % 2, CH, r),
                                             scalar=b1[0:r, j:j + 1], in1=gelu[0:r, n % 2, :], op0=ALU.add, op1=ALU.mult)\
                        .then_inc(gated, 1)
                for c in range(NC):
                    dve.wait_ge(out_done, c + 1)
                    zc = z[:, 1 + CH * c:1 + CH * (c + 1)]
                    dve.scalar_tensor_tensor(out=zc, in0=k.bank(4 + c), scalar=b2, in1=zc, op0=ALU.add, op1=ALU.add)\
                        .then_inc(added, 1)


def layer1_ffn(k, A):
    nc = k.nc
    hidden = A["L1_ffn_w1"].shape[2] // 2
    with ExitStack() as ctx:
        def sb(name, shape, dt=F32):
            return ctx.enter_context(nc.sbuf_tensor(name + "_l1f", shape, dt))

        z, h = sb("z", [P, T + 1]), k.s4
        wqkv, w_turned, wo = sb("wqkv", [P, 1536]), sb("w_turned", [P, 1024]), sb("wo", [P, 4, P])
        w1, w2, b1, columns = sb("w1", [P, 2 * hidden]), sb("w2", [P, 3, P]), sb("b1", [P, 6]), sb("columns", [P, 7])
        bands, ident = sb("bands", [P, 2, 4, P], BF16), sb("ident_bf16", [P, P], BF16)

        def z_part(c):
            return z[:, 1 + CH * c:1 + CH * (c + 1)]

        def h_part(c):
            return part(h, c)

        def weights(layer):
            return [(wqkv[:, :], A["L1_ffn_wqkv"][layer]), (w_turned[:, :], A["L1_ffn_w_turned"][layer]),
                    (w1[:, :], A["L1_ffn_w1"][layer]), (columns[:, :], A["L1_ffn_columns"][layer]),
                    (wo[:, :, :], A["L1_ffn_wo"][layer].rearrange("(j p) d -> p j d", p=P)),
                    (w2[:, 0:2, :], A["L1_ffn_w2"][layer, 0:2 * P].rearrange("(j p) d -> p j d", p=P)),
                    (w2[0:hidden - 2 * P, 2, :], A["L1_ffn_w2"][layer, 2 * P:hidden]), (b1[:, :], A["L1_ffn_b1"][layer])]

        with nc.sbuf_tensor("bands_f32", [P, 2, P], F32) as bands_f32:
            layernorm(k, k.x, z_part, 1e-5, loads=weights(0) + [(bands_f32[:, :, :], A["const_bands"])])
            with phase(nc, "cleared rounded", []) as (cleared, rounded):
                with nc.Block() as block:
                    @block.vector
                    def _(dve):
                        dve.memset(z[:, 0:1], 0.0).then_inc(cleared, 1)
                        dve.tensor_copy(ident[:, :], k.mat("ident")).then_inc(rounded, 1)
                        for n in range(2):
                            dve.tensor_copy(bands[:, n, :, :], bands_f32[:, n, :].unsqueeze(1).to_broadcast([P, 4, P]))\
                                .then_inc(rounded, 1)
        for layer in range(2):
            if layer:
                load(k, weights(layer))
            shifted_tokens(k, z, k.xnpad[:, LEAD:LEAD + T])
            with nc.sbuf_tensor(f"q_{layer}", [P, 4, 2, T], F32) as q_pad, nc.sbuf_tensor(f"k_{layer}", [P, 4, 64 + T], F32) as keys:
                window_qk(k, wqkv, w_turned, columns, A["const_xpos"], q_pad, keys)
                o = k.scratch
                window_attention(k, q_pad, keys, wqkv[:, 1024:1536], bands, ident, o)
                project(k, [("vector", [(wo[:, j, :], o[:, j, CH * c:CH * (c + 1)]) for j in range(4)], P, CH,
                             lambda dve, ps, c=c: dve.tensor_tensor(z_part(c), z_part(c), ps, ALU.add)) for c in range(NC)])
            shifted_tokens(k, z, h)
            layernorm(k, h_part, k.xn, 1e-5, columns[:, 4:5], columns[:, 5:6])
            gated_ffn(k, k.xn, w1, b1, w2, columns[:, 6:7], z, hidden)
        add_tile(k, z[:, 1:1 + T])


def layer2_ffn(k, A):
    nc = k.nc
    E, CAP, F = 16, 32, 256
    SLOT = E * CAP
    G = SLOT // P
    with ExitStack() as ctx:
        def sb(name, shape, dt=F32):
            return ctx.enter_context(nc.sbuf_tensor(name + "_l2f", shape, dt))

        r1, r2 = sb("r1", [P, P]), sb("r2", [P, E])
        w1, w2, w3 = sb("w1", [P, E, F]), sb("w2", [P, E, F]), sb("w3", [P, E, 2, P])
        logits, left = sb("logits", [E, T]), sb("left", [E, T])
        best, place, place_f = sb("best", [E, CAP]), sb("place", [E, CAP], U32), sb("place_f", [E, CAP])
        st, share = sb("st", [E, 6]), sb("share", [E, CAP])
        places, place_col, share_col = sb("places", [P, SLOT]), sb("place_col", [P, G]), sb("share_col", [P, G])
        token, iota = sb("token", [P, NT]), sb("iota", [P, T])
        x_tok, x_slot = sb("x_tok", [P, NT, P]), sb("x_slot", [P, SLOT])
        gate, h, h_t, result = sb("gate", [P, G, F]), sb("h", [P, G, F]), sb("h_t", [P, G, 2, P]), sb("result", [P, G, P])
        place_dram = nc.dram_tensor("place_dram", (E, CAP), F32).ap()
        share_dram = nc.dram_tensor("share_dram", (E, CAP), F32).ap()
        layernorm(k, k.x, k.xn, 1e-5, loads=[
            (r1[:, :], A["L2_ffn_router_w1"]), (r2[:, :], A["L2_ffn_router_w2"]), (token[:, :], A["const_token"])])
        project(k, [("scalar", [(r1[:, :], k.xn(c))], P, CH,
                     lambda act, ps, c=c: act.activation(part(k.s1, c), ps, ACT.Silu)) for c in range(NC)])
        project(k, [("scalar", [(r2[:, :], part(k.s1, c))], E, CH, copy_out(part(logits, c))) for c in range(NC)])

        names = "step exp_done weighed written row_read turned copied marked gathered landed"
        with phase(nc, names, []) as (step, exp_done, weighed, written, row_read, turned, copied, marked, gathered, landed):
            rounds = CAP // 8
            with nc.Block() as block:
                @block.vector
                def _(dve):
                    for r in range(rounds):
                        src = logits if r == 0 else left
                        dve.max(best[:, 8 * r:8 * r + 8], src[:, :]).then_inc(step, 1)
                        dve.wait_ge(step, 3 * r + 1)
                        dve.max_index(place[:, 8 * r:8 * r + 8], best[:, 8 * r:8 * r + 8], src[:, :]).then_inc(step, 1)
                        dve.wait_ge(step, 3 * r + 2)
                        dve.match_replace(left[:, :], best[:, 8 * r:8 * r + 8], src[:, :], MASKED).then_inc(step, 1)
                        dve.wait_ge(step, 3 * r + 3)
                    n = 3 * rounds
                    dve.tensor_copy(place_f[:, :], place[:, :]).then_inc(step, 1)
                    dve.tensor_scalar(st[:, 0:1], best[:, 0:1], -1.0, None, ALU.mult).then_inc(step, 1)
                    dve.wait_ge(exp_done, 2)
                    dve.reciprocal(st[:, 2:3], st[:, 1:2]).then_inc(step, 1)
                    dve.wait_ge(step, n + 3)
                    dve.tensor_scalar(share[:, :], share[:, :], st[:, 2:3], None, ALU.mult).then_inc(step, 1)
                    dve.wait_ge(step, n + 4)
                    dve.tensor_reduce(st[:, 3:4], share[:, :], AX.X, ALU.add).then_inc(step, 1)
                    dve.wait_ge(step, n + 5)
                    dve.tensor_scalar(st[:, 4:5], st[:, 3:4], 1e-9, None, ALU.add).then_inc(step, 1)
                    dve.wait_ge(step, n + 6)
                    dve.reciprocal(st[:, 5:6], st[:, 4:5]).then_inc(step, 1)
                    dve.wait_ge(step, n + 7)
                    dve.tensor_scalar(share[:, :], share[:, :], st[:, 5:6], None, ALU.mult).then_inc(weighed, 1)
                    dve.wait_ge(row_read, 48)
                    for t in range(NT):
                        mark = k.scratch[:, t // 4, CH * (t % 4):CH * (t % 4 + 1)]
                        dve.tensor_scalar(mark, places[:, :], token[:, t:t + 1], None, ALU.is_equal).then_inc(marked, 1)
                    dve.wait_ge(gathered, 1)
                    dve.tensor_copy(x_slot[:, :], k.bank(4)).then_inc(step, 1)

                @block.scalar
                def _(act):
                    act.dma_start(w1[:, :, :], A["L2_ffn_w1"].rearrange("e p f -> p e f")).then_inc(landed, 16)
                    act.dma_start(w2[:, :, :], A["L2_ffn_w2"].rearrange("e p f -> p e f")).then_inc(landed, 16)
                    act.dma_start(w3[:, :, :, :], A["L2_ffn_w3"].rearrange("e (j p) d -> p e j d", p=P)).then_inc(landed, 16)
                    act.dma_start(iota[:, :], A["const_iota"]).then_inc(landed, 16)
                    act.wait_ge(step, 3 * rounds + 2)
                    act.activation(left[:, :], logits[:, :], ACT.Exp, bias=st[:, 0:1], accum_out=st[:, 1:2]).then_inc(exp_done, 1)
                    act.activation(share[:, :], best[:, :], ACT.Exp, bias=st[:, 0:1]).then_inc(exp_done, 1)
                    for b in range(4):
                        act.wait_ge(turned, b + 1)
                        act.activation(x_tok[:, 4 * b:4 * b + 4, :].rearrange("p a b -> p (a b)"), k.bank(b), ACT.Copy)\
                            .then_inc(copied, 1)
                    act.wait_ge(landed, 64)

                @block.sync
                def _(sp):
                    sp.wait_ge(step, 3 * rounds + 1)
                    sp.dma_start(place_dram, place_f[:, :]).then_inc(written, 16)
                    sp.wait_ge(weighed, 1)
                    sp.dma_start(share_dram, share[:, :]).then_inc(written, 16)
                    sp.wait_ge(written, 32)
                    row = place_dram.rearrange("e c -> (e c)")
                    sp.dma_start(places[:, :], row.rearrange("(a n) -> a n", a=1).to_broadcast([P, SLOT])).then_inc(row_read, 16)
                    sp.dma_start(place_col[:, :], row.rearrange("(g p) -> p g", p=P), allow_slow_non_contiguous=True).then_inc(row_read, 16)
                    sp.dma_start(share_col[:, :], share_dram.rearrange("e c -> (e c)").rearrange("(g p) -> p g", p=P),
                                 allow_slow_non_contiguous=True)\
                        .then_inc(row_read, 16)

                @block.tensor
                def _(pe):
                    for b in range(4):
                        for a in range(4):
                            mm = pe.transpose(k.bank(b)[:, P * a:P * (a + 1)], k.xn_tile(4 * b + a), k.mat("ident"))
                        mm.then_inc(turned, 1)
                    for t in range(NT):
                        pe.wait_ge(copied, t // 4 + 1)
                        pe.wait_ge(marked, t + 1)
                        mm = pe.matmul(k.bank(4), x_tok[:, t, :], k.scratch[:, t // 4, CH * (t % 4):CH * (t % 4 + 1)],
                                       start=(t == 0), stop=(t == NT - 1))
                    mm.then_inc(gathered, 1)

        names = "raised acted gated turned copied lowered weighed marked out_done added"
        with phase(nc, names, []) as (raised, acted, gated, turned, copied, lowered, weighed, marked, out_done, added):
            with nc.Block() as block:
                @block.tensor
                def _(pe):
                    for g in range(G):
                        for base, w in ((0, w1), (2, w2)):
                            for j in range(4):
                                e = 4 * g + j
                                mm = pe.matmul(k.bank(base + g // 2)[32 * j:32 * j + 32, F * (g % 2):F * (g % 2 + 1)],
                                               x_slot[:, CAP * e:CAP * (e + 1)], w[:, e, :], start=True, stop=True)
                    mm.then_inc(raised, 1)
                    for g in range(G):
                        pe.wait_ge(gated, g + 1)
                        for j in range(2):
                            mm = pe.transpose(k.bank(4 + g // 2)[:, F * (g % 2) + P * j:F * (g % 2) + P * (j + 1)],
                                              h[:, g, P * j:P * (j + 1)], k.mat("ident"))
                        mm.then_inc(turned, 1)
                    for g in range(G):
                        pe.wait_ge(copied, g // 2 + 1)
                        for e in range(4 * g, 4 * g + 4):
                            j = e % 4
                            for f in range(2):
                                mm = pe.matmul(k.bank(6)[32 * j:32 * j + 32, P * g:P * (g + 1)],
                                               h_t[:, g, f, CAP * j:CAP * (j + 1)], w3[:, e, f, :], start=(f == 0), stop=(f == 1))
                    mm.then_inc(lowered, 1)
                    pe.wait_ge(weighed, G)
                    for c in range(NC):
                        for g in range(G):
                            pe.wait_ge(marked, g + 1)
                            mm = pe.matmul(k.bank(c), result[:, g, :], k.scratch[:, g, CH * c:CH * (c + 1)],
                                           start=(g == 0), stop=(g == G - 1))
                        mm.then_inc(out_done, 1)

                @block.scalar
                def _(act):
                    act.wait_ge(raised, 1)
                    for b in range(2):
                        act.activation(gate[:, 2 * b:2 * b + 2, :].rearrange("p a b -> p (a b)"), k.bank(b), ACT.Silu)\
                            .then_inc(acted, 1)
                    for b in range(2):
                        act.wait_ge(turned, 2 * b + 2)
                        act.activation(h_t[:, 2 * b:2 * b + 2, :, :].rearrange("p a j b -> p (a j b)"), k.bank(4 + b), ACT.Copy)\
                            .then_inc(copied, 1)

                @block.vector
                def _(dve):
                    for g in range(G):
                        dve.tensor_scalar(k.scratch[:, g, :], iota[:, :], place_col[:, g:g + 1], None, ALU.is_equal)\
                            .then_inc(marked, 1)
                    for g in range(G):
                        dve.wait_ge(acted, g // 2 + 1)
                        dve.tensor_tensor(h[:, g, :], k.bank(2 + g // 2)[:, F * (g % 2):F * (g % 2 + 1)], gate[:, g, :], ALU.mult)\
                            .then_inc(gated, 1)
                    dve.wait_ge(lowered, 1)
                    for g in range(G):
                        dve.tensor_scalar(result[:, g, :], k.bank(6)[:, P * g:P * (g + 1)], share_col[:, g:g + 1], None, ALU.mult)\
                            .then_inc(weighed, 1)
                    for c in range(NC):
                        dve.wait_ge(out_done, c + 1)
                        dve.tensor_tensor(k.x(c), k.x(c), k.bank(c), ALU.add).then_inc(added, 1)


def causal_schedule():
    blocks = [(p, q, s) for p in range(8) for q in range(NC) for s in range(2)]
    n_units = 4 * len(blocks)
    order = [("fill", 0, tile) for tile in range(12)] + [("score", 0, 0)]
    late = []
    for n in range(n_units + 6):
        b, i = n // 4, n % 4
        side, late_now = late, []
        if 1 <= b <= len(blocks):
            q = blocks[b - 1][1]
            keys = 4 * (q + 1)
            pairs = range(2 * (q + 1) * i // 4, 2 * (q + 1) * (i + 1) // 4)
            if i == 2:
                side = [("share", b - 1, 0)] + side
            for m in pairs:
                side += [("turn", b - 1, 2 * m), ("turn", b - 1, 2 * m + 1)]
                side.append(("mix", b - 1, m))
            if i == 3:
                side.append(("weigh", b - 1, 0))
                p, q, s = blocks[b - 1]
                if q == NC - 1 and s == 1:
                    late_now.append(("project", p, 0))
        late = late_now
        if n < n_units:
            p, q, s = blocks[b]
            local = 4 * (2 * q + s) + i
            if p < 7 and 12 <= local < 24:
                side.append(("fill", p + 1, local - 12))
        lists = []
        if n < n_units:
            q = blocks[b][1]
            lists.append([((j + 0.35) / (q + 1), 1, ("exp", n, j)) for j in range(q + 1)])
            if i == 3:
                lists.append([(1.0, 3, ("sum", b, 0))])
        if n + 1 < n_units:
            q = blocks[(n + 1) // 4][1]
            lists.append([((j + 0.5) / (q + 1), 2, ("score", n + 1, j)) for j in range(q + 1)])
        lists.append([(m / max(1, len(side)), 0, e) for m, e in enumerate(side)])
        order += [e for _, _, _, e in sorted((at, kind, m, e) for lst in lists for m, (at, kind, e) in enumerate(lst))]
    return blocks, order


def causal_attention(k, wq, wk, wv, proj, bq8, bk, bv):
    nc = k.nc
    blocks, order = causal_schedule()
    S_BANKS = 5
    RING = 6
    names = ("scored masked part_max maxed exped bank_filled copied_v copied_s mixed totalled inverted weighed "
             "zeroed")
    tiles = [("q_pad", [P, 2, 2, T], F32), ("probs", [P, 2, 4, T], F32), ("probs_t", [P, RING, CH], F32),
             ("tops", [P, 2, 4], F32), ("neg_max", [P, 2], F32), ("total", [P, 16, 4], F32), ("sums", [P, 2, 4], F32),
             ("inv", [P, 2, 4], F32), ("shares", [P, 2, CH], F32), ("z", [P, 2, T], F32)]
    with phase(nc, names, tiles) as (scored, masked, part_max, maxed, exped, bank_filled, copied_v, copied_s, mixed, totalled,
                                     inverted, weighed, zeroed,
                                     q_pad, probs, probs_t, tops, neg_max, total, sums, inv, shares, z):
        side = [e for e in order if e[0] in ("fill", "turn", "share", "project")]
        side_index = {e: m for m, e in enumerate(side)}
        engine_of, count_of = [], []
        n_v = n_s = 0
        for m, e in enumerate(side):
            if e[0] == "turn":
                by_s = m % 2 == 0 and not (blocks[e[1]][1] == 0 and e[2] == 1)
            else:
                by_s = e[0] == "share" or (e[0] == "fill" and e[2] < 4)
            n_s, n_v = n_s + by_s, n_v + (not by_s)
            engine_of.append("s" if by_s else "v")
            count_of.append(n_s if by_s else n_v)
        turn_index = {e[1:]: m for m, e in enumerate([e for e in side if e[0] == "turn"])}
        chunk_index = {e[1:]: m for m, e in enumerate([e for e in order if e[0] == "score"])}

        def wait_copied(eng, e):
            m = side_index[e]
            eng.wait_ge(copied_s if engine_of[m] == "s" else copied_v, count_of[m])

        def wait_side_bank(eng, e):
            if side_index[e] >= 2:
                wait_copied(eng, side[side_index[e] - 2])

        def chunks_through(b):
            return chunk_index[(4 * b + 3, blocks[b][1])] + 1

        def last_turn(b):
            return ("turn", b, 4 * blocks[b][1] + 3)

        def mixes_through(b):
            return turn_index[last_turn(b)[1:]] + 1

        def width(n, j):
            return CH if j < blocks[n // 4][1] else P * (n % 4 + 1)

        def first_query(b, kt):
            return max(0, kt - 4 * blocks[b][1])

        with nc.Block() as block:
            @block.tensor
            def _(pe):
                pending = []

                def mix(b, m):
                    p, q, s = blocks[b]
                    if m == 0 and b >= 1:
                        pe.wait_ge(weighed, b)
                    if m == 0:
                        wait_copied(pe, ("fill", p, 11))
                    wait_copied(pe, ("turn", b, 2 * m))
                    wait_copied(pe, ("turn", b, 2 * m + 1))
                    for half in range(2):
                        kt = 2 * m + half
                        a = 0 if m == 0 else first_query(b, kt)
                        pe.matmul(k.bank(7)[64 * half:64 * half + 64, P * a:CH],
                                  k.scratch[:, 2 + p % 2, P * kt + 64 * s:P * kt + 64 * s + 64],
                                  probs_t[:, turn_index[(b, kt)] % RING, P * a:CH],
                                  start=(m == 0), stop=(m == 2 * q + 1)).then_inc(mixed, 1)

                pe.wait_ge(zeroed, 4)
                for e in order:
                    kind = e[0]
                    if kind == "score":
                        n, j = e[1:]
                        p, q, s = blocks[n // 4]
                        c = chunk_index[(n, j)]
                        if c >= S_BANKS:
                            pe.wait_ge(exped, c - S_BANKS + 1)
                        if j == 0 and q == 0 and s == 0 and n % 4 == 0:
                            wait_copied(pe, ("fill", p, 3))
                            wait_copied(pe, ("fill", p, 7))
                        w = width(n, j)
                        t = 4 * q + n % 4
                        pe.matmul(k.bank(c % S_BANKS, w), q_pad[:, p % 2, s, P * t:P * (t + 1)],
                                  k.scratch[:, p % 2, CH * j:CH * j + w], start=True, stop=True).then_inc(scored, 1)
                    elif kind == "mix":
                        pending.append(e[1:])
                        if len(pending) > 1:
                            mix(*pending.pop(0))
                    elif kind == "weigh":
                        while pending:
                            mix(*pending.pop(0))
                    elif e in side_index:
                        bank = k.bank(5 + side_index[e] % 2)
                        wait_side_bank(pe, e)
                        if kind == "fill":
                            p, tile = e[1:]
                            if tile < 8:
                                w = (wq if tile < 4 else wk)[:, P * p:P * (p + 1)]
                                mm = pe.matmul(bank, w, k.xn(tile % 4), start=True, stop=True)
                            else:
                                for a in range(4):
                                    mm = pe.matmul(bank[:, P * a:P * (a + 1)], k.xn_tile(4 * (tile - 8) + a),
                                                   wv[:, P * p:P * (p + 1)], start=True, stop=True)
                        elif kind == "turn":
                            b, kt = e[1:]
                            if kt == 0:
                                pe.wait_ge(exped, chunks_through(b))
                            for a in range(first_query(b, kt), 4):
                                mm = pe.transpose(bank[:, P * a:P * (a + 1)], probs[:, b % 2, a, P * kt:P * (kt + 1)],
                                                  k.mat("ident"))
                        elif kind == "share":
                            b = e[1]
                            pe.wait_ge(inverted, b + 1)
                            for a in range(4):
                                column = inv[:, b % 2, a:a + 1].to_broadcast([P, P])
                                mm = pe.transpose(bank[:, P * a:P * (a + 1)], column, k.mat("ident"))
                        else:
                            pe.wait_ge(weighed, 8 * (e[1] + 1))
                            for j in range(16):
                                rows = z[:, :, :].rearrange("p s (r j) -> p s r j", j=16)[:, :, :, j]
                                mm = pe.matmul(bank[:, 0:2 * P], proj[:, j, :], rows, start=(j == 0), stop=(j == 15))
                        mm.then_inc(bank_filled, 1)

            @block.gpsimd
            def _(pool):
                for parity in range(2):
                    pool.memset(q_pad[64:P, parity, 0, :], 0.0).then_inc(zeroed, 1)
                    pool.memset(q_pad[0:64, parity, 1, :], 0.0).then_inc(zeroed, 1)

            def before_fill(eng, p, tile):
                if p >= 2:
                    last = 8 * (p - 1) - 1
                    eng.wait_ge(scored, chunks_through(last))
                    if tile >= 8:
                        eng.wait_ge(mixed, mixes_through(last))

            def before_turn_copy(eng, e):
                t = turn_index[e[1:]]
                if t >= RING:
                    eng.wait_ge(mixed, t - RING + 1)

            @block.scalar
            def _(act):
                for e in order:
                    if e[0] == "exp":
                        n, j = e[1:]
                        b = n // 4
                        act.wait_ge(maxed, n + 1)
                        if b >= 2 and n % 4 == 0 and j == 0:
                            act.wait_ge(bank_filled, side_index[last_turn(b - 2)] + 1)
                        if b >= 4 and n % 4 == 0 and j == 0:
                            act.wait_ge(totalled, b - 3)
                        c, w = chunk_index[(n, j)], width(n, j)
                        act.activation(probs[:, b % 2, n % 4, CH * j:CH * j + w], k.bank(c % S_BANKS, w), ACT.Exp,
                                       bias=neg_max[:, n % 2:n % 2 + 1], accum_out=total[:, n % 16, j:j + 1]).then_inc(exped, 1)
                    elif e in side_index and engine_of[side_index[e]] == "s":
                        m = side_index[e]
                        act.wait_ge(bank_filled, m + 1)
                        bank = k.bank(5 + m % 2)
                        if e[0] == "fill":
                            p, c = e[1:]
                            before_fill(act, p, c)
                            for s in range(2):
                                r = slice(64 * s, 64 * s + 64)
                                ins = act.activation(q_pad[r, p % 2, s, CH * c:CH * (c + 1)], bank[r, :], ACT.Identity,
                                                     scale=0.125, bias=bq8[r, p:p + 1])
                        elif e[0] == "turn":
                            before_turn_copy(act, e)
                            a = first_query(*e[1:])
                            ins = act.activation(probs_t[:, turn_index[e[1:]] % RING, P * a:CH], bank[:, P * a:CH], ACT.Copy)
                        else:
                            b = e[1]
                            if b >= 2:
                                act.wait_ge(weighed, b - 1)
                            ins = act.activation(shares[:, b % 2, :], bank, ACT.Copy)
                        ins.then_inc(copied_s, 1)

            @block.vector
            def _(dve):
                n_mask = n_part = 0
                for e in order:
                    if e[0] == "score":
                        n, j = e[1:]
                        q = blocks[n // 4][1]
                        c, w = chunk_index[(n, j)], width(n, j)
                        dve.wait_ge(scored, c + 1)
                        bank = k.bank(c % S_BANKS, w)
                        if j == q:
                            edge = bank[:, w - P:w]
                            dve.tensor_tensor(edge, edge, k.mat("causal"), ALU.add).then_inc(masked, 1)
                            n_mask += 1
                            dve.wait_ge(masked, n_mask)
                            if n >= 2:
                                dve.wait_ge(exped, chunk_index[(n - 2, blocks[(n - 2) // 4][1])] + 1)
                        if q == 0:
                            dve.tensor_reduce(neg_max[:, n % 2:n % 2 + 1], bank, AX.X, ALU.max, negate=True).then_inc(maxed, 1)
                        else:
                            dve.tensor_reduce(tops[:, n % 2, j:j + 1], bank, AX.X, ALU.max).then_inc(part_max, 1)
                            n_part += 1
                            if j == q:
                                dve.wait_ge(part_max, n_part)
                                dve.tensor_reduce(neg_max[:, n % 2:n % 2 + 1], tops[:, n % 2, 0:q + 1], AX.X, ALU.max,
                                                  negate=True).then_inc(maxed, 1)
                    elif e[0] == "sum":
                        b = e[1]
                        q = blocks[b][1]
                        dve.wait_ge(exped, chunks_through(b))
                        at = 4 * b % 16
                        dve.tensor_reduce(sums[:, b % 2, :], total[:, at:at + 4, 0:q + 1], AX.X, ALU.add).then_inc(totalled, 1)
                        dve.wait_ge(totalled, b + 1)
                        if b >= 2:
                            dve.wait_ge(bank_filled, side_index[("share", b - 2, 0)] + 1)
                        dve.reciprocal(inv[:, b % 2, :], sums[:, b % 2, :]).then_inc(inverted, 1)
                    elif e[0] == "weigh":
                        b = e[1]
                        dve.wait_ge(mixed, mixes_through(b))
                        wait_copied(dve, ("share", b, 0))
                        p, q, s = blocks[b]
                        if p >= 1 and q == 0 and s == 0:
                            dve.wait_ge(bank_filled, side_index[("project", p - 1, 0)] + 1)
                        dve.scalar_tensor_tensor(out=z[:, s, CH * q:CH * (q + 1)], in0=k.bank(7), scalar=0.125,
                                                 in1=shares[:, b % 2, :], op0=ALU.mult, op1=ALU.mult).then_inc(weighed, 1)
                    elif e in side_index and engine_of[side_index[e]] == "v":
                        m = side_index[e]
                        dve.wait_ge(bank_filled, m + 1)
                        bank = k.bank(5 + m % 2)
                        if e[0] == "fill":
                            p, tile = e[1:]
                            before_fill(dve, p, tile)
                            if tile < 8:
                                ins = dve.tensor_scalar(k.scratch[:, p % 2, CH * (tile - 4):CH * (tile - 3)], bank, bk[:, p:p + 1],
                                                        None, ALU.add)
                            else:
                                ins = dve.tensor_tensor(
                                    k.scratch[:, 2 + p % 2, CH * (tile - 8):CH * (tile - 7)].rearrange("p (t d) -> p t d", t=4),
                                    bank.rearrange("p (t d) -> p t d", t=4),
                                    bv[:, P * p:P * (p + 1)].unsqueeze(1).to_broadcast([P, 4, P]), ALU.add)
                        elif e[0] == "turn":
                            before_turn_copy(dve, e)
                            b, kt = e[1:]
                            a = first_query(b, kt)
                            slot = probs_t[:, turn_index[(b, kt)] % RING, :]
                            if kt == 1 and a == 1:
                                dve.memset(slot[:, 0:P], 0.0)
                            ins = dve.tensor_copy(slot[:, P * a:CH], bank[:, P * a:CH])
                        else:
                            xs = k.xpad[:, 1 + 2 * P * e[1]:1 + 2 * P * (e[1] + 1)]
                            ins = dve.tensor_tensor(xs, xs, bank[:, 0:2 * P], ALU.add)
                        ins.then_inc(copied_v, 1)


def layer3_attention(k, A):
    nc = k.nc
    with ExitStack() as ctx:
        def sb(name, shape):
            return ctx.enter_context(nc.sbuf_tensor(name + "_l3a", shape, F32))

        wq, wk, wv, proj = sb("wq", [P, 1024]), sb("wk", [P, 1024]), sb("wv", [P, 1024]), sb("proj", [P, 16, P])
        bq, bq8, bk, bv = sb("bq", [P, 8]), sb("bq8", [P, 8]), sb("bk", [P, 8]), sb("bv", [P, 1024])
        pairs = [(wq[:, :], A["L3_attn_WqT"]), (wk[:, :], A["L3_attn_WkT"]), (wv[:, :], A["L3_attn_WvT"]),
                 (proj[0:64, :, :], A["L3_attn_proj"].rearrange("(j p) d -> p j d", p=64)),
                 (proj[64:P, :, :], A["L3_attn_proj"].rearrange("(j p) d -> p j d", p=64)),
                 (bv[:, :], A["L3_attn_bv"].rearrange("h d -> (h d)").rearrange("(a n) -> a n", a=1).to_broadcast([P, 1024]))]
        for p in range(8):
            for tile, name in ((bq, "bq"), (bk, "bk")):
                pairs.append((tile[:, p:p + 1], A["L3_attn_" + name][2 * p:2 * p + 2].rearrange("h (d a) -> (h d) a", a=1)))
        layernorm(k, k.x, k.xn, 1e-5, loads=pairs)
        with phase(nc, "made", []) as (made,):
            with nc.Block() as block:
                @block.vector
                def _(dve):
                    dve.tensor_scalar(bq8[:, :], bq[:, :], 0.125, None, ALU.mult).then_inc(made, 1)
        causal_attention(k, wq, wk, wv, proj, bq8, bk, bv)


def layer3_ffn(k, A):
    nc = k.nc
    E, F = 8, 512
    FT = F // P
    with ExitStack() as ctx:
        def sb(name, shape, dt=F32):
            return ctx.enter_context(nc.sbuf_tensor(name + "_l3f", shape, dt))

        gate_w, up, down = sb("gate_w", [P, E]), sb("up", [P, E, 2 * F]), sb("down", [P, E, FT, P])
        logits, best, place = sb("logits", [P, NT, E]), sb("best", [P, NT, 8]), sb("place", [P, NT, 8], U32)
        place_f, iota8 = sb("place_f", [P, NT, 2]), sb("iota8", [P, E])
        gap, second, inv, share = sb("gap", [P, NT]), sb("second", [P, NT]), sb("inv", [P, NT]), sb("share", [P, 2, NT])
        pick, combine, rows = sb("pick", [P, 2, E, NT]), sb("combine", [P, E, NT]), sb("rows", [P, P])
        xe = sb("xe", [P, E, T])
        combine_dram = nc.dram_tensor("combine_dram", (E, T), F32).ap()
        layernorm(k, k.x, k.xn, 1e-5, loads=[
            (gate_w[:, :], A["L3_ffn_gateT"]), (iota8[:, :], A["const_iota"][:, 0:E]),
            (up[:, :, :], A["L3_ffn_gate_upT"].rearrange("e p f -> p e f")),
            (down[:, :, :, :], A["L3_ffn_downT"].rearrange("e (j p) d -> p e j d", p=P))])

        names = "scored copied found placed gap_done exp_done step turned rows_done written"
        with phase(nc, names, []) as (scored, copied, found, placed, gap_done, exp_done, step, turned, rows_done, written):
            with nc.Block() as block:
                @block.tensor
                def _(pe):
                    for t in range(NT):
                        mm = pe.matmul(k.bank(0)[:, E * t:E * (t + 1)], k.xn_tile(t), gate_w[:, :], start=True, stop=True)
                    mm.then_inc(scored, 1)
                    pe.wait_ge(step, 7)
                    pe.transpose(k.bank(1, P), combine[:, :, :].rearrange("p e t -> p (e t)"), k.mat("ident")).then_inc(turned, 1)

                @block.vector
                def _(dve):
                    dve.wait_ge(scored, 1)
                    dve.tensor_copy(logits[:, :, :].rearrange("p t e -> p (t e)"), k.bank(0, NT * E)).then_inc(copied, 1)
                    dve.wait_ge(copied, 1)
                    for t in range(NT):
                        dve.max(best[:, t, :], logits[:, t, :]).then_inc(found, 1)
                    for t in range(NT):
                        dve.wait_ge(found, t + 1)
                        dve.max_index(place[:, t, :], best[:, t, :], logits[:, t, :]).then_inc(placed, 1)
                    dve.tensor_tensor(gap[:, :], best[:, :, 1], best[:, :, 0], ALU.subtract).then_inc(gap_done, 1)
                    dve.wait_ge(placed, NT)
                    dve.tensor_copy(place_f[:, :, :], place[:, :, 0:2]).then_inc(step, 1)
                    dve.wait_ge(exp_done, 1)
                    dve.tensor_scalar(inv[:, :], second[:, :], 1.0, None, ALU.add).then_inc(step, 1)
                    dve.wait_ge(step, 2)
                    dve.reciprocal(share[:, 0, :], inv[:, :]).then_inc(step, 1)
                    dve.wait_ge(step, 3)
                    dve.tensor_tensor(share[:, 1, :], share[:, 0, :], second[:, :], ALU.mult).then_inc(step, 1)
                    for b in range(2):
                        dve.tensor_tensor(pick[:, b, :, :], iota8[:, :].unsqueeze(2).to_broadcast([P, E, NT]),
                                          place_f[:, :, b].unsqueeze(1).to_broadcast([P, E, NT]), ALU.is_equal).then_inc(step, 1)
                    dve.wait_ge(step, 6)
                    for b in range(2):
                        dve.tensor_tensor(pick[:, b, :, :], pick[:, b, :, :],
                                          share[:, b, :].unsqueeze(1).to_broadcast([P, E, NT]), ALU.mult).then_inc(rows_done, 1)
                    dve.wait_ge(rows_done, 2)
                    dve.tensor_tensor(combine[:, :, :], pick[:, 0, :, :], pick[:, 1, :, :], ALU.add).then_inc(step, 1)
                    dve.wait_ge(turned, 1)
                    dve.tensor_copy(rows[:, :], k.bank(1, P)).then_inc(rows_done, 1)

                @block.scalar
                def _(act):
                    act.wait_ge(gap_done, 1)
                    act.activation(second[:, :], gap[:, :], ACT.Exp).then_inc(exp_done, 1)

                @block.sync
                def _(sp):
                    sp.wait_ge(rows_done, 3)
                    sp.dma_start(combine_dram.rearrange("e (t p) -> (e t) p", p=P), rows[:, :]).then_inc(written, 16)
                    sp.wait_ge(written, 16)

        units = [(c, e, f) for c in range(NC) for e in range(E) for f in range(FT)]
        LAG = 2
        with phase(nc, "read scaled_low scaled_high gate_done value_done acted gated out_done added",
                   [("silu", [P, 2, CH], F32), ("h", [P, 4, CH], F32)]) as (
                read, scaled_low, scaled_high, gate_done, value_done, acted, gated, out_done, added, silu, h):
            def scale(eng, c, e):
                here = xe[:, e, CH * c:CH * (c + 1)]
                return eng.tensor_tensor(here, here, k.xn(c), ALU.mult)

            with nc.Block() as block:
                @block.sync
                def _(sp):
                    for c in range(NC):
                        if c:
                            sp.wait_ge(read, 16 * c)
                        shares = combine_dram[:, CH * c:CH * (c + 1)].unsqueeze(0).to_broadcast([P, E, CH])
                        sp.dma_start(xe[:, :, CH * c:CH * (c + 1)], shares).then_inc(read, 16)
                    sp.wait_ge(read, 16 * NC)

                @block.gpsimd
                def _(pool):
                    for c in range(NC):
                        pool.wait_ge(read, 16 * (c + 1))
                        for e in range(4 if c == 0 else 0, E):
                            scale(pool, c, e).then_inc(scaled_high, 1)

                @block.tensor
                def _(pe):
                    for n in range(len(units) + LAG):
                        if n < len(units):
                            c, e, f = units[n]
                            if n >= 3:
                                pe.wait_ge(acted, n - 2)
                                pe.wait_ge(gated, n - 2)
                            pe.matmul(k.bank(n % 3), up[:, e, P * f:P * (f + 1)], k.xn(c), start=True, stop=True)\
                                .then_inc(gate_done, 1)
                            if f == 0:
                                if c == 0 and e < 4:
                                    pe.wait_ge(scaled_low, e + 1)
                                else:
                                    pe.wait_ge(scaled_high, E * c + e + 1 - 4)
                            pe.matmul(k.bank(3 + n % 3), up[:, e, F + P * f:F + P * (f + 1)], xe[:, e, CH * c:CH * (c + 1)],
                                      start=True, stop=True).then_inc(value_done, 1)
                        if n >= LAG:
                            u = n - LAG
                            c, e, f = units[u]
                            first, last = (e, f) == (0, 0), (e, f) == (E - 1, FT - 1)
                            if first and c >= 2:
                                pe.wait_ge(added, c - 1)
                            pe.wait_ge(gated, u + 1)
                            mm = pe.matmul(k.bank(6 + c % 2), down[:, e, f, :], h[:, u % 4, :], start=first, stop=last)
                            mm.then_inc(out_done, 1)

                @block.scalar
                def _(act):
                    for n in range(len(units)):
                        act.wait_ge(gate_done, n + 1)
                        if n >= 2:
                            act.wait_ge(gated, n - 1)
                        act.activation(silu[:, n % 2, :], k.bank(n % 3), ACT.Silu).then_inc(acted, 1)

                @block.vector
                def _(dve):
                    dve.wait_ge(read, 16)
                    for e in range(4):
                        scale(dve, 0, e).then_inc(scaled_low, 1)
                    for n, (c, e, f) in enumerate(units):
                        dve.wait_ge(value_done, n + 1)
                        dve.wait_ge(acted, n + 1)
                        if n >= 4:
                            dve.wait_ge(out_done, n - 3)
                        dve.tensor_tensor(h[:, n % 4, :], k.bank(3 + n % 3), silu[:, n % 2, :], ALU.mult).then_inc(gated, 1)
                        if n >= 8 and n % (E * FT) == 7 and c >= 1:
                            dve.wait_ge(out_done, E * FT * c)
                            dve.tensor_tensor(k.x(c - 1), k.x(c - 1), k.bank(6 + (c - 1) % 2), ALU.add).then_inc(added, 1)
                    dve.wait_ge(out_done, len(units))
                    dve.tensor_tensor(k.x(NC - 1), k.x(NC - 1), k.bank(6 + (NC - 1) % 2), ALU.add).then_inc(added, 1)
STEPS = [layer0_attention, layer0_ffn, layer1_attention, layer1_ffn, layer2_attention, layer2_ffn,
         layer3_attention, layer3_ffn]


def build(nc, A, out, steps=STEPS):
    with ExitStack() as ctx:
        k = Core(nc, ctx)
        setup(k, A["x_t"], A["const_mats"])
        for step in steps:
            step(k, A)
        store(k, out)


def host_constants(np):
    i = np.arange(P)
    mats = np.zeros((P, N_MATS, P), np.float32)
    mats[:, 0] = np.eye(P)
    mats[:, 1] = i[:, None] // 8 == i[None, :] // 8
    mats[:, 2] = i[:, None] // 64 == i[None, :] // 64
    for m in range(P):
        mats[32 * (m // 32) + 8, 3, m] = 1.0
    mats[:, 4] = np.where(i[None, :] > i[:, None], MASKED, 0.0)

    mats[:, 5] = np.eye(P) - 1.0 / D

    t = np.arange(T, dtype=np.float32)
    f32 = np.float32
    inv = (f32(1.0) / f32(10000.0) ** (np.arange(0, 8, 2, dtype=f32) / f32(8))).astype(f32)
    ang = np.outer(inv, t).astype(f32)
    d8 = i % 8
    rope = np.stack([np.cos(ang)[d8 % 4], np.where(d8[:, None] < 4, -1.0, 1.0) * np.sin(ang)[d8 % 4]], 1).astype(f32)

    half = np.arange(0, 64, 2, dtype=f32)
    inv = (f32(1.0) / f32(10000.0) ** (half / f32(64))).astype(f32)
    ang = np.outer(inv, t).astype(f32).astype(np.float64)
    base = ((half + f32(0.4 * 64)) / f32(1.4 * 64)).astype(f32)
    power = ((t - T // 2) / f32(32)).astype(f32)
    scale = (base[:, None].astype(np.float64) ** power[None, :].astype(np.float64))
    d64 = i % 32
    cos, sin, sc = np.cos(ang)[d64], np.sin(ang)[d64], scale[d64]
    sin = np.where(i[:, None] % 64 < 32, -sin, sin)
    xpos = np.stack([8 * cos * sc, 8 * sin * sc, cos / sc, sin / sc], 1).astype(f32)

    key, query = np.arange(P)[None, :], i[:, None] % 64
    band = np.where((key <= query + 64) & (key >= query), 0.0, MASKED)
    first = np.where((i[:, None] < 64) & (key < 64), MASKED, band)
    bands = np.stack([first, band], 1).astype(f32)
    return {"const_mats": mats, "const_rope": rope, "const_xpos": xpos, "const_bands": bands,
            "const_iota": np.broadcast_to(np.arange(T, dtype=f32), (P, T)).copy(),
            "const_token": (np.arange(NT)[None, :] * P + i[:, None]).astype(f32)}


def arrange(np, inputs):
    a = {n: np.asarray(v) for n, v in inputs.items()}
    out = {}
    for n, v in a.items():
        out[n] = v.reshape(-1, 1) if v.ndim == 1 else v
    out["x_t"] = a["L0_attn_x"][0].T
    del out["L0_attn_x"]
    for n in ("Wq", "Wk", "Wv", "Wp"):
        out[f"L0_attn_{n}T"] = a[f"L0_attn_{n}"].T
        del out[f"L0_attn_{n}"]
    w = a["L1_attn_w_qkv"]
    even = np.arange(D).reshape(16, 4, 2).transpose(0, 2, 1).reshape(-1)
    odd = np.arange(D).reshape(16, 4, 2)[:, :, ::-1].transpose(0, 2, 1).reshape(-1)
    out["L1_attn_qkT"] = np.stack([w[:D][even].T, w[:D][odd].T, w[D:2 * D][even].T, w[D:2 * D][odd].T], 1)
    out["L1_attn_vT"] = w[2 * D:].T
    out["L1_attn_outT"] = a["L1_attn_w_out"].T
    del out["L1_attn_w_qkv"], out["L1_attn_w_out"]
    w = a["L1_ffn_wqkv"]
    depth = w.shape[0]
    turned = w[:, :, :1024].reshape(depth, D, 16, 2, 32)[:, :, :, ::-1].reshape(depth, D, 1024)
    out["L1_ffn_w_turned"] = turned
    twice = {n: np.tile(a["L1_ffn_" + n], (1, 2)) for n in ("q_scale", "k_scale")}
    swapped = {n: v.reshape(depth, 2, 2, 32)[:, :, ::-1].reshape(depth, D) for n, v in twice.items()}
    out["L1_ffn_columns"] = np.stack([twice["q_scale"], swapped["q_scale"], twice["k_scale"], swapped["k_scale"],
                                      a["L1_ffn_ln_g"], a["L1_ffn_ln_b"], a["L1_ffn_b2"]], 2)
    hidden = a["L1_ffn_b1"].shape[1] // 2
    b1 = np.zeros((depth, 2, 3 * P), np.float32)
    b1[:, :, :hidden] = a["L1_ffn_b1"].reshape(depth, 2, hidden)
    out["L1_ffn_b1"] = b1.reshape(depth, 6, P).transpose(0, 2, 1)
    for n in ("q_scale", "k_scale", "ln_g", "ln_b", "b2"):
        del out["L1_ffn_" + n]
    for n in ("q", "k", "v"):
        out[f"L3_attn_W{n}T"] = a[f"L3_attn_W{n}"].reshape(16 * 64, D).T
        del out[f"L3_attn_W{n}"]
    out["L3_ffn_gateT"] = a["L3_ffn_gate_w"].T
    out["L3_ffn_gate_upT"] = a["L3_ffn_gate_up_proj"].transpose(0, 2, 1)
    out["L3_ffn_downT"] = a["L3_ffn_down_proj"].transpose(0, 2, 1)
    del out["L3_ffn_gate_w"], out["L3_ffn_gate_up_proj"], out["L3_ffn_down_proj"]
    out.update(host_constants(np))
    return {n: np.ascontiguousarray(v) for n, v in out.items()}


def kernel(**inputs):
    import numpy as np
    import concourse.bacc as bacc
    from concourse.bass_utils import run_bass_kernel_spmd

    nc = bacc.Bacc("TRN2", target_bir_lowering=False, num_devices=1)
    arrays, args = {}, {}
    for name, a in arrange(np, inputs).items():
        arrays[f"in_{name}"] = a
        args[name] = nc.dram_tensor(f"in_{name}", a.shape, mybir.dt.from_np(a.dtype), kind="ExternalInput").ap()
    out = nc.dram_tensor("out_t", (D, T), F32, kind="ExternalOutput").ap()
    build(nc, args, out)
    r = run_bass_kernel_spmd(nc, [arrays], core_ids=[0])
    return np.ascontiguousarray(r.results[0]["out_t"].T).reshape(1, T, D)
```

```python
from contextlib import ExitStack, contextmanager

import concourse.bass as bass
from concourse import mybir

ALU = mybir.AluOpType
ACT = mybir.ActivationFunctionType
AX = mybir.AxisListType
F32 = mybir.dt.float32
BF16 = mybir.dt.bfloat16
F16 = mybir.dt.float16
U32 = mybir.dt.uint32

P = 128
D = 128
T = 2048
CH = 512
NC = T // CH
NT = T // P
LEAD = 64
ROUND = 12582912.0
MASKED = -3.0e38


@contextmanager
def phase(nc, sems, tiles):
    with ExitStack() as ctx:
        tag = nc.next_id()
        got_tiles = [ctx.enter_context(nc.sbuf_tensor(f"{n}_{tag}", s, d)) for n, s, d in tiles]
        got_sems = [nc.alloc_semaphore(name=f"{n}_{tag}") for n in sems.split()]
        yield (*got_sems, *got_tiles)
        nc.clear_and_free_semaphores(got_sems)
        nc.all_engine_barrier()


class Core:

    def __init__(self, nc, ctx):
        self.nc = nc

        def sb(name, shape, dt=F32):
            return ctx.enter_context(nc.sbuf_tensor(name, shape, dt))

        self.xpad = sb("xpad", [P, T + 1])
        self.xnpad = sb("xnpad", [P, LEAD + T + 1])
        self.scratch = sb("scratch", [P, 4, T])
        self.s1, self.s2, self.s3, self.s4 = (self.scratch[:, n, :] for n in range(4))
        self.mats = sb("mats", [P, N_MATS, P])
        self.mean_mat = sb("mean_mat", [P, P])
        self.cols = sb("cols", [P, 4])
        self.out_stored = ctx.enter_context(nc.semaphore("out_stored"))
        self.psum = ctx.enter_context(nc.psum_tensor("psum", [P, 8 * CH], F32))

    def mat(self, name):
        return self.mats[:, MATS.index(name), :]

    def bank(self, b, n=CH, rows=P):
        return self.psum[0:rows, CH * b:CH * b + n]

    def x(self, c, rows=slice(0, P)):
        return self.xpad[rows, 1 + CH * c:1 + CH * (c + 1)]

    def xn(self, c, shift=0):
        return self.xnpad[:, LEAD + shift + CH * c:LEAD + shift + CH * (c + 1)]

    def xn_tile(self, t):
        return self.xnpad[:, LEAD + P * t:LEAD + P * (t + 1)]

    def eps(self, value):
        return self.cols[:, EPS.index(value):EPS.index(value) + 1]


MATS = ["ident", "heads8", "heads64", "den", "causal", "centre"]
N_MATS = len(MATS)
EPS = [1e-5, 1e-3, 1e-30]


def part(tile, c):
    return tile[:, CH * c:CH * (c + 1)]


def setup(k, x_t, const_mats):
    nc = k.nc
    with phase(nc, "landed cleared", []) as (landed, cleared):
        with nc.Block() as block:
            @block.sync
            def _(sp):
                sp.dma_start(k.xpad[:, 1:1 + T], x_t).then_inc(landed, 16)
                sp.dma_start(k.mats[:, :, :], const_mats).then_inc(landed, 16)
                sp.wait_ge(landed, 32)

            @block.vector
            def _(dve):
                dve.memset(k.mean_mat[:, :], 1.0 / D).then_inc(cleared, 1)
                dve.memset(k.xpad[:, 0:1], 0.0).then_inc(cleared, 1)
                dve.memset(k.xnpad[:, 0:LEAD], 0.0).then_inc(cleared, 1)
                dve.memset(k.xnpad[:, LEAD + T:LEAD + T + 1], 0.0).then_inc(cleared, 1)
                for n, e in enumerate(EPS):
                    dve.memset(k.cols[:, n:n + 1], e).then_inc(cleared, 1)
                dve.wait_ge(cleared, 4 + len(EPS))


def layernorm(k, src, dst, eps, gain=None, bias=None, loads=(), late=(), late_landed=None):
    nc = k.nc
    names = "centred squared var_done log_done inverted scaled normed landed"
    with phase(nc, names, []) as (centred, squared, var_done, log_done, inverted, scaled, normed, landed):
        with nc.Block() as block:
            @block.sync
            def _(sp):
                for tile, dram in loads:
                    sp.dma_start(tile, dram).then_inc(landed, 16)
                for tile, dram in late:
                    sp.dma_start(tile, dram).then_inc(late_landed, 16)
                if loads:
                    sp.wait_ge(landed, 16 * len(loads))

            @block.tensor
            def _(pe):
                for c in range(NC):
                    pe.matmul(k.bank(c), k.mat("centre"), src(c), start=True, stop=True).then_inc(centred, 1)
                for c in range(NC):
                    pe.wait_ge(squared, c + 1)
                    pe.matmul(k.bank(4 + c), k.mean_mat[:, :], part(k.s2, c), start=True, stop=True)\
                        .then_inc(var_done, 1)

            @block.scalar
            def _(act):
                act.preload_act_table_set("natural_log_exp_and_others")
                for c in range(NC):
                    act.wait_ge(centred, c + 1)
                    act.activation(part(k.s2, c), k.bank(c), ACT.Square).then_inc(squared, 1)
                for c in range(NC):
                    act.wait_ge(var_done, c + 1)
                    act.activation(part(k.s3, c), k.bank(4 + c), ACT.Ln, bias=k.eps(eps)).then_inc(log_done, 1)
                    act.wait_ge(log_done, c + 1)
                    act.activation(part(k.s1, c), part(k.s3, c), ACT.Exp, scale=-0.5).then_inc(inverted, 1)

            @block.vector
            def _(dve):
                for c in range(NC):
                    dve.wait_ge(inverted, c + 1)
                    dve.tensor_tensor(dst(c), k.bank(c), part(k.s1, c), ALU.mult).then_inc(scaled, 1)
                    if gain is not None:
                        dve.wait_ge(scaled, c + 1)
                        dve.tensor_scalar(dst(c), dst(c), gain, bias, ALU.mult, ALU.add).then_inc(normed, 1)


def project(k, jobs):
    nc = k.nc
    by = {e: [n for n, job in enumerate(jobs) if job[0] == e] for e in ("vector", "scalar")}
    with phase(nc, "product_done left_by_vector left_by_scalar", []) as (product_done, by_vector, by_scalar):
        left = {"vector": by_vector, "scalar": by_scalar}
        with nc.Block() as block:
            @block.tensor
            def _(pe):
                for n, (_, pairs, rows, cols, _) in enumerate(jobs):
                    if n >= 8:
                        e = jobs[n - 8][0]
                        pe.wait_ge(left[e], by[e].index(n - 8) + 1)
                    for i, (lhs, rhs) in enumerate(pairs):
                        mm = pe.matmul(k.bank(n % 8, cols, rows), lhs, rhs,
                                       start=(i == 0), stop=(i == len(pairs) - 1))
                    mm.then_inc(product_done, 1)

            @block.vector
            def _(dve):
                for n in by["vector"]:
                    dve.wait_ge(product_done, n + 1)
                    jobs[n][4](dve, k.bank(n % 8, jobs[n][3], jobs[n][2])).then_inc(by_vector, 1)

            @block.scalar
            def _(act):
                for n in by["scalar"]:
                    act.wait_ge(product_done, n + 1)
                    jobs[n][4](act, k.bank(n % 8, jobs[n][3], jobs[n][2])).then_inc(by_scalar, 1)


def add_to_x(k, c, bias=None):
    def leave(dve, ps):
        if bias is None:
            return dve.tensor_tensor(k.x(c), k.x(c), ps, ALU.add)
        return dve.scalar_tensor_tensor(out=k.x(c), in0=ps, scalar=bias, in1=k.x(c), op0=ALU.add, op1=ALU.add)
    return leave


def copy_out(dst):
    def leave(eng, ps):
        return eng.activation(dst, ps, ACT.Copy)
    return leave


def linear_attention(k, wq, wkv, y, floor, guard):
    nc = k.nc
    units = 12
    names = "product_done low_done exp_done phi_done v_done ones_done kv_done state_done out_done den_done log_done inverse_done y_done"
    tiles = [("phi_q", [P, T], F32), ("phi_k", [P, NT, P], F32), ("v1", [P, NT, P + 1], F32),
             ("kv_state", [P, P], F32), ("z_state", [P, P], F32), ("z_col", [P, 1], F32)]
    with phase(nc, names, tiles) as (product_done, low_done, exp_done, phi_done, v_done, ones_done, kv_done,
                                     state_done, out_done, den_done, log_done, inverse_done, y_done,
                                     phi_q, phi_k, v1, kv_state, z_state, z_col):
        def views(n):
            if n < 4:
                return k.bank(n), part(k.s1, n), part(k.s2, n), part(phi_q, n)
            m = n - 4
            ps = k.bank(n % 6).rearrange("p (a b) -> p a b", a=2)[:, :, 0:P]
            lo = k.s3[:, 256 * m:256 * m + 256].rearrange("p (a b) -> p a b", a=2)
            ex = y[:, 256 * m:256 * m + 256].rearrange("p (a b) -> p a b", a=2)
            return ps, lo, ex, phi_k[:, 2 * m:2 * m + 2, :]

        with nc.Block() as block:
            @block.tensor
            def _(pe):
                for n in range(units):
                    if n >= 6:
                        pe.wait_ge(phi_done, n - 5)
                        if n - 6 >= 4:
                            pe.wait_ge(v_done, n - 6 - 3)
                    if n < 4:
                        mm = pe.matmul(k.bank(n), wq, k.xn(n), start=True, stop=True)
                    else:
                        for a in range(2):
                            mm = pe.matmul(k.bank(n % 6)[:, 256 * a:256 * a + 256], k.xn_tile(2 * (n - 4) + a), wkv,
                                           start=True, stop=True)
                    mm.then_inc(product_done, 1)
                pe.wait_ge(ones_done, 1)
                for t in range(NT):
                    pe.wait_ge(phi_done, 4 + t // 2 + 1)
                    pe.wait_ge(v_done, t // 2 + 1)
                    mm = pe.matmul(k.bank(6, P + 1), phi_k[:, t, :], v1[:, t, :], start=(t == 0), stop=(t == NT - 1))
                mm.then_inc(kv_done, 1)
                pe.wait_ge(state_done, 3)
                for c in range(NC):
                    if c >= 3:
                        pe.wait_ge(y_done, c - 2)
                    pe.matmul(k.bank(c % 3), kv_state[:, :], part(phi_q, c), start=True, stop=True)
                    pe.matmul(k.bank(3 + c % 3), z_state[:, :], part(phi_q, c), start=True, stop=True).then_inc(out_done, 1)

            @block.scalar
            def _(act):
                act.preload_act_table_set("natural_log_exp_and_others")
                for n in range(units):
                    act.wait_ge(low_done, n + 1)
                    _, lo, ex, _ = views(n)
                    act.activation(ex, lo, ACT.Exp).then_inc(exp_done, 1)
                    if n >= 4:
                        v_ps = k.bank(n % 6).rearrange("p (a b) -> p a b", a=2)[:, :, P:2 * P]
                        act.activation(v1[:, 2 * (n - 4):2 * (n - 4) + 2, 0:P], v_ps, ACT.Copy).then_inc(v_done, 1)
                for c in range(NC):
                    act.wait_ge(den_done, c + 1)
                    act.activation(part(k.s3, c), part(k.s1, c), ACT.Ln).then_inc(log_done, 1)
                    act.wait_ge(log_done, c + 1)
                    act.activation(part(k.s2, c), part(k.s3, c), ACT.Exp, scale=-1.0).then_inc(inverse_done, 1)

            @block.vector
            def _(dve):
                dve.memset(v1[:, :, P:P + 1], 1.0).then_inc(ones_done, 1)
                for n in range(units + 1):
                    if n < units:
                        dve.wait_ge(product_done, n + 1)
                        ps, lo, _, _ = views(n)
                        dve.tensor_scalar(lo, ps, 0.0, None, ALU.min).then_inc(low_done, 1)
                    if n >= 1:
                        dve.wait_ge(exp_done, n)
                        if n - 1 >= 4:
                            dve.wait_ge(v_done, n - 4)
                        ps, _, ex, phi = views(n - 1)
                        dve.scalar_tensor_tensor(out=phi, in0=ps, scalar=0.0, in1=ex, op0=ALU.max, op1=ALU.add)\
                            .then_inc(phi_done, 1)
                dve.wait_ge(kv_done, 1)
                dve.tensor_tensor(kv_state[:, :], k.bank(6, P), k.mat("heads8"), ALU.mult).then_inc(state_done, 1)
                dve.tensor_copy(z_col[:, :], k.bank(6, P + 1)[:, P:P + 1]).then_inc(state_done, 1)
                dve.wait_ge(state_done, 2)
                dve.tensor_scalar(z_state[:, :], k.mat("heads8"), z_col[:, 0:1], None, ALU.mult).then_inc(state_done, 1)
                for c in range(NC + 1):
                    if c < NC:
                        dve.wait_ge(out_done, c + 1)
                        op, bound = (ALU.max, floor) if guard is None else (ALU.add, guard)
                        dve.tensor_scalar(part(k.s1, c), k.bank(3 + c % 3), bound, None, op).then_inc(den_done, 1)
                    if c >= 1:
                        dve.wait_ge(inverse_done, c)
                        dve.tensor_tensor(part(y, c - 1), k.bank((c - 1) % 3), part(k.s2, c - 1), ALU.mult)\
                            .then_inc(y_done, 1)


def layer0_attention(k, A):
    nc = k.nc
    with ExitStack() as ctx:
        w = ctx.enter_context(nc.sbuf_tensor("w_l0a", [P, 4, P], F32))
        vec = ctx.enter_context(nc.sbuf_tensor("vec_l0a", [P, 5], F32))
        y = ctx.enter_context(nc.sbuf_tensor("y_l0a", [P, T], F32))
        layernorm(k, k.x, k.xn, 1e-5, loads=[(w[:, n, :], A[name]) for n, name in enumerate(
            ("L0_attn_WqT", "L0_attn_WkT", "L0_attn_WvT", "L0_attn_WpT"))]
            + [(vec[:, 0:3], A["L0_attn_conv_w"]), (vec[:, 3:4], A["L0_attn_conv_b"]), (vec[:, 4:5], A["L0_attn_bp"])])
        linear_attention(k, w[:, 0, :], w[:, 1:3, :].rearrange("p a b -> p (a b)"), y, 1e-6, None)
        with phase(nc, "middle_done step_done", []) as (middle_done, step_done):
            with nc.Block() as block:
                @block.scalar
                def _(act):
                    for c in range(NC):
                        act.activation(part(k.s1, c), k.xn(c), ACT.Identity, scale=vec[:, 1:2], bias=vec[:, 3:4])\
                            .then_inc(middle_done, 1)

                @block.vector
                def _(dve):
                    for c in range(NC):
                        dve.scalar_tensor_tensor(out=part(y, c), in0=k.xn(c, -1), scalar=vec[:, 0:1], in1=part(y, c),
                                                 op0=ALU.mult, op1=ALU.add).then_inc(step_done, 1)
                        dve.wait_ge(step_done, 3 * c + 1)
                        dve.scalar_tensor_tensor(out=part(y, c), in0=k.xn(c, 1), scalar=vec[:, 2:3], in1=part(y, c),
                                                 op0=ALU.mult, op1=ALU.add).then_inc(step_done, 1)
                        dve.wait_ge(step_done, 3 * c + 2)
                        dve.wait_ge(middle_done, c + 1)
                        dve.tensor_tensor(part(y, c), part(y, c), part(k.s1, c), ALU.add).then_inc(step_done, 1)
        project(k, [("vector", [(w[:, 3, :], part(y, c))], P, CH, add_to_x(k, c, vec[:, 4:5])) for c in range(NC)])


def layer0_ffn(k, A):
    nc = k.nc
    QB, QEPS = 128.0, 1e-5
    with ExitStack() as ctx:
        w = ctx.enter_context(nc.sbuf_tensor("w_l0f", [P, P], F32))
        wq = ctx.enter_context(nc.sbuf_tensor("wq_l0f", [P, P], F32))
        vec = ctx.enter_context(nc.sbuf_tensor("vec_l0f", [P, 2], F32))
        st = ctx.enter_context(nc.sbuf_tensor("st_l0f", [P, 8], F32))
        layernorm(k, k.x, k.xn, 1e-5, loads=[
            (w[:, :], A["L0_ffn_weight"]), (vec[:, 0:1], A["L0_ffn_ln_gamma"]), (vec[:, 1:2], A["L0_ffn_ln_beta"])])
        layernorm(k, k.xn, k.xn, 1e-3, vec[:, 0:1], vec[:, 1:2])
        with phase(nc, "step all_max beta_done", []) as (step, all_max, beta_done):
            with nc.Block() as block:
                @block.tensor
                def _(pe):
                    pe.wait_ge(step, 2)
                    pe.matmul(k.bank(0, 1), k.mean_mat[:, :], st[:, 0:1], start=True, stop=True).then_inc(beta_done, 1)

                @block.gpsimd
                def _(pool):
                    pool.wait_ge(step, 1)
                    pool.partition_all_reduce(st[:, 2:3], st[:, 1:2], P, bass.bass_isa.ReduceOp.max).then_inc(all_max, 1)

                @block.vector
                def _(dve):
                    n = 0

                    def then(ins):
                        ins.then_inc(step, 1)

                    then(dve.tensor_reduce(st[:, 1:2], k.xnpad[:, LEAD:LEAD + T], AX.X, ALU.max, apply_absolute_value=True))
                    then(dve.tensor_reduce(st[:, 0:1], w[:, :], AX.X, ALU.add, apply_absolute_value=True))
                    dve.wait_ge(beta_done, 1)
                    then(dve.tensor_scalar(st[:, 3:4], k.bank(0, 1), 1.0 / D, None, ALU.mult))
                    dve.wait_ge(step, 3)
                    then(dve.tensor_scalar(st[:, 4:5], st[:, 3:4], QEPS, None, ALU.add))
                    dve.wait_ge(step, 4)
                    then(dve.reciprocal(st[:, 5:6], st[:, 4:5]))
                    dve.wait_ge(step, 5)
                    then(dve.tensor_scalar(wq[:, :], w[:, :], st[:, 5:6], ROUND, ALU.mult, ALU.add))
                    dve.wait_ge(step, 6)
                    then(dve.tensor_scalar(wq[:, :], wq[:, :], ROUND, 1.0, ALU.subtract, ALU.min))
                    dve.wait_ge(step, 7)
                    then(dve.tensor_scalar(wq[:, :], wq[:, :], -1.0, None, ALU.max))
                    dve.wait_ge(all_max, 1)
                    then(dve.reciprocal(st[:, 6:7], st[:, 2:3]))
                    dve.wait_ge(step, 9)
                    then(dve.tensor_scalar(st[:, 6:7], st[:, 6:7], QB, None, ALU.mult))
                    then(dve.tensor_scalar(st[:, 7:8], st[:, 3:4], st[:, 2:3], 1.0 / QB, ALU.mult, ALU.mult))
                    dve.wait_ge(step, 11)
                    xn = k.xnpad[:, LEAD:LEAD + T]
                    then(dve.tensor_scalar(xn, xn, st[:, 6:7], QB - QEPS, ALU.mult, ALU.min))
                    dve.wait_ge(step, 12)
                    then(dve.tensor_scalar(xn, xn, QEPS - QB, None, ALU.max))

        def scaled(c):
            def leave(dve, ps):
                return dve.scalar_tensor_tensor(out=k.x(c), in0=ps, scalar=st[:, 7:8], in1=k.x(c),
                                                op0=ALU.mult, op1=ALU.add)
            return leave
        project(k, [("vector", [(wq[:, :], k.xn(c))], P, CH, scaled(c)) for c in range(NC)])


def lookup_ffn(k, w1, w2, hidden):
    nc = k.nc
    tiles = [("raw", [P, 2, CH], F32), ("low", [P, 2, CH], F32), ("grid", [P, 2, CH], F32), ("h", [P, NC, hidden, CH], F32)]
    with phase(nc, "product_done rounded lowered gridded acted out_done added", tiles) as (
            product_done, rounded, lowered, gridded, acted, out_done, added, raw, low, grid, h):
        units = [(c, j) for c in range(NC) for j in range(hidden)]
        with nc.Block() as block:
            @block.tensor
            def _(pe):
                for n, (c, j) in enumerate(units):
                    if n >= 4:
                        pe.wait_ge(rounded, n - 3)
                    pe.matmul(k.bank(n % 4), w1[:, P * j:P * (j + 1)], k.xn(c), start=True, stop=True).then_inc(product_done, 1)
                for c in range(NC):
                    for j in range(hidden):
                        pe.wait_ge(acted, hidden * c + j + 1)
                        mm = pe.matmul(k.bank(4 + c), w2[:, j, :], h[:, c, j, :], start=(j == 0), stop=(j == hidden - 1))
                    mm.then_inc(out_done, 1)

            @block.vector
            def _(dve):
                for n in range(len(units)):
                    dve.wait_ge(product_done, n + 1)
                    dve.tensor_scalar(raw[:, n % 2, :], k.bank(n % 4), 10.0, ROUND, ALU.mult, ALU.add).then_inc(rounded, 1)
                    dve.wait_ge(rounded, n + 1)
                    dve.tensor_scalar(low[:, n % 2, :], raw[:, n % 2, :], ROUND, -128.0, ALU.subtract, ALU.max).then_inc(lowered, 1)
                    dve.wait_ge(lowered, n + 1)
                    if n >= 2:
                        dve.wait_ge(acted, n - 1)
                    dve.tensor_scalar(grid[:, n % 2, :], low[:, n % 2, :], 127.0, 0.1, ALU.min, ALU.mult).then_inc(gridded, 1)
                for c in range(NC):
                    dve.wait_ge(out_done, c + 1)
                    dve.tensor_tensor(k.x(c), k.x(c), k.bank(4 + c), ALU.add).then_inc(added, 1)

            @block.scalar
            def _(act):
                for n, (c, j) in enumerate(units):
                    act.wait_ge(gridded, n + 1)
                    act.activation(h[:, c, j, :], grid[:, n % 2, :], ACT.Gelu_apprx_tanh).then_inc(acted, 1)


def layer2_attention(k, A):
    nc = k.nc
    with ExitStack() as ctx:
        w = ctx.enter_context(nc.sbuf_tensor("w_l2a", [P, 4, P], F32))
        w1 = ctx.enter_context(nc.sbuf_tensor("w1_l2a", [P, 512], F32))
        w2 = ctx.enter_context(nc.sbuf_tensor("w2_l2a", [P, 4, P], F32))
        vec = ctx.enter_context(nc.sbuf_tensor("vec_l2a", [P, 4], F32))
        y = ctx.enter_context(nc.sbuf_tensor("y_l2a", [P, T], F32))
        weights = ([(vec[:, n:n + 1], A["L2_attn_" + name]) for n, name in enumerate(("ln1_g", "ln1_b", "ln2_g", "ln2_b"))]
                   + [(w[:, n, :], A["L2_attn_" + name]) for n, name in enumerate(("wq", "wk", "wv", "wo"))]
                   + [(w1[:, :], A["L2_attn_w1"]), (w2[:, :, :], A["L2_attn_w2"].rearrange("(j p) d -> p j d", p=P))])
        z = ctx.enter_context(nc.sbuf_tensor("z_l2a", [P, T], F32))

        def z_part(c):
            return part(z, c)

        layernorm(k, k.x, z_part, 1e-5, loads=weights)
        layernorm(k, z_part, k.xn, 1e-5, vec[:, 0:1], vec[:, 1:2])
        linear_attention(k, w[:, 0, :], w[:, 1:3, :].rearrange("p a b -> p (a b)"), y, None, 1e-6)
        project(k, [("vector", [(w[:, 3, :], part(y, c))], P, CH, lambda dve, ps, c=c: dve.tensor_tensor(
            z_part(c), z_part(c), ps, ALU.add)) for c in range(NC)])
        layernorm(k, z_part, k.xn, 1e-5, vec[:, 2:3], vec[:, 3:4])
        add_tile(k, z[:, :])
        lookup_ffn(k, w1, w2, 4)


def add_tile(k, tile):
    nc = k.nc
    with phase(nc, "added", []) as (added,):
        with nc.Block() as block:
            @block.vector
            def _(dve):
                dve.tensor_tensor(k.xpad[:, 1:1 + T], k.xpad[:, 1:1 + T], tile, ALU.add).then_inc(added, 1)


def store(k, out):
    with k.nc.Block() as block:
        @block.sync
        def _(sp):
            sp.dma_start(out, k.xpad[:, 1:1 + T]).then_inc(k.out_stored, 16)
            sp.wait_ge(k.out_stored, 16)


def clear_group(pool, qs, ks, b, cleared, before):
    pool.memset(qs[64:96, b, :, :, :], 0.0).then_inc(cleared, 1)
    pool.wait_ge(cleared, before + 1)
    pool.memset(ks[64:P, b, :, :], 1.0).then_inc(cleared, 1)
    pool.wait_ge(cleared, before + 2)


def split_into_bf16(k, qk_w, rope, temps, pieces, pieces_dram, qs, ks):
    nc = k.nc
    units = [(m, c) for m in range(2) for c in range(NC)]
    names = "straight_done turned_done by_cos by_sin rotated high_done rest_done middle_done low_done cleared stored"
    cos_part, sin_part, value, rest = (temps[:, 2 * n:2 * n + 2, :] for n in range(4))
    with phase(nc, names, []) as (straight_done, turned_done, by_cos, by_sin, rotated, high_done, rest_done, middle_done,
                                     low_done, cleared, stored):
        with nc.Block() as block:
            @block.gpsimd
            def _(pool):
                clear_group(pool, qs, ks, 0, cleared, 0)

            @block.sync
            def _(sp):
                for n, (m, c) in enumerate(units):
                    sp.wait_ge(high_done, n + 1)
                    sp.wait_ge(middle_done, n + 1)
                    sp.wait_ge(low_done, n + 1)
                    there = pieces_dram[m, :, :, CH * c:CH * (c + 1)].rearrange("a p t -> p a t")
                    sp.dma_start(there, pieces[:, m, :, CH * c:CH * (c + 1)]).then_inc(stored, 16)
                sp.wait_ge(stored, 16 * len(units))

            @block.tensor
            def _(pe):
                for n, (m, c) in enumerate(units):
                    if n >= 2:
                        pe.wait_ge(by_cos, n - 1)
                        pe.wait_ge(by_sin, n - 1)
                    pe.matmul(k.bank(n % 2), qk_w[:, 2 * m, :], k.xn(c), start=True, stop=True).then_inc(straight_done, 1)
                    pe.matmul(k.bank(2 + n % 2), qk_w[:, 2 * m + 1, :], k.xn(c), start=True, stop=True).then_inc(turned_done, 1)

            @block.vector
            def _(dve):
                for n in range(len(units) + 2):
                    if n < len(units):
                        m, c = units[n]
                        dve.wait_ge(straight_done, n + 1)
                        dve.tensor_tensor(cos_part[:, n % 2, :], k.bank(n % 2), part(rope[:, 0, :], c), ALU.mult).then_inc(by_cos, 1)
                        dve.wait_ge(turned_done, n + 1)
                        dve.tensor_tensor(sin_part[:, n % 2, :], k.bank(2 + n % 2), part(rope[:, 1, :], c), ALU.mult)\
                            .then_inc(by_sin, 1)
                        dve.wait_ge(by_cos, n + 1)
                        dve.wait_ge(by_sin, n + 1)
                        if n >= 2:
                            dve.wait_ge(rest_done, n - 1)
                        dve.tensor_tensor(value[:, n % 2, :], cos_part[:, n % 2, :], sin_part[:, n % 2, :], ALU.add)\
                            .then_inc(rotated, 1)
                    if 1 <= n <= len(units):
                        u = n - 1
                        m, c = units[u]
                        dve.wait_ge(high_done, u + 1)
                        if u >= 2:
                            dve.wait_ge(low_done, u - 1)
                        dve.tensor_tensor(rest[:, u % 2, :], value[:, u % 2, :], pieces[:, m, 0, CH * c:CH * (c + 1)],
                                          ALU.subtract).then_inc(rest_done, 1)
                    if n >= 2:
                        u = n - 2
                        m, c = units[u]
                        dve.wait_ge(middle_done, u + 1)
                        dve.tensor_tensor(pieces[:, m, 2, CH * c:CH * (c + 1)], rest[:, u % 2, :],
                                          pieces[:, m, 1, CH * c:CH * (c + 1)], ALU.subtract).then_inc(low_done, 1)

            @block.scalar
            def _(act):
                for n in range(len(units) + 1):
                    if n < len(units):
                        m, c = units[n]
                        act.wait_ge(rotated, n + 1)
                        act.activation(pieces[:, m, 0, CH * c:CH * (c + 1)], value[:, n % 2, :], ACT.Copy).then_inc(high_done, 1)
                    if n >= 1:
                        u = n - 1
                        m, c = units[u]
                        act.wait_ge(rest_done, u + 1)
                        act.activation(pieces[:, m, 1, CH * c:CH * (c + 1)], rest[:, u % 2, :], ACT.Copy).then_inc(middle_done, 1)


BUFS = 3


def softmax_schedule():
    blocks, units, steps = 4 * NC, 4 * 4 * NC, 2 * NT
    ahead = 10
    order = [("tops", 0, u) for u in range(0, units, NC)] + [("close", 0, 0), ("turn", 0, 0)]
    rest = []
    for b in range(1, blocks):
        rest += [("top", b, u) for u in range(units)] + [("close", b, 0)]
    per_step = units // steps
    order += rest[:ahead * per_step]
    rest = rest[ahead * per_step:]
    turn_at = None
    for n in range(blocks * steps):
        b, m = n // steps, n % steps
        order.append(("step", b, m))
        if turn_at and turn_at[0] == n:
            order.append(("turn", turn_at[1], 0))
        if b and m == 6:
            order.append(("spread", b - 1, 0))
        if b and m == 9:
            order.append(("divide", b - 1, 0))
        tops = rest[:per_step]
        rest = rest[per_step:]
        if tops and rest and rest[0][0] == "close":
            tops.append(rest.pop(0))
            turn_at = (n + 2, tops[-1][1])
        if m % 2 and n >= 3:
            order += tops[:1] + [("mix", (n - 3) // steps, (n - 3) % steps)] + tops[1:]
        else:
            order += tops
    order += [("mix", blocks - 1, steps - 2), ("spread", blocks - 1, 0), ("divide", blocks - 1, 0)]
    return order


def grouped_attention(k, pieces_dram, v_w, v_pad, mixed_heads, qs, ks):
    nc = k.nc
    order = softmax_schedule()
    R = 96
    ROWS = 4 * 4
    blocks, units, steps = 4 * NC, ROWS * NC, 2 * NT
    names = ("ones_set zeros_set v_cleared v_done v_copied loaded_0 loaded_1 loaded_2 top_scored top_found closed turned high_done "
             "rest_done middle_done low_done laid_out scored exped mixed emptied spread log_done inverted divided")
    tiles = [("probs_t", [P, 4, 2 * CH], F32),
             ("tops", [P, 2, ROWS, NC], F32), ("neg_max", [P, ROWS], F32), ("max_pieces", [ROWS, 3, P], BF16),
             ("rest", [ROWS, P], F32), ("log", [P, CH], F32), ("inv", [P, CH], F32)]
    with phase(nc, names, tiles) as (ones_set, zeros_set, v_cleared, v_done, v_copied, loaded_0, loaded_1, loaded_2, top_scored, top_found,
                                     closed, turned, high_done, rest_done, middle_done, low_done, laid_out, scored, exped,
                                     mixed, emptied, spread, log_done, inverted, divided, probs_t, tops, neg_max,
                                     max_pieces, rest, log, inv):
        loaded = (loaded_0, loaded_1, loaded_2)
        ring = [e for e in order if e[0] in ("top", "turn", "spread")]
        slot = {e: n for n, e in enumerate(ring)}

        def ring_bank(e, cols=CH, rows=P):
            return k.bank(4 + slot[e] % 3, cols, rows)

        def found(b, u):
            return (u + 1) // NC if b == 0 else ROWS + units * (b - 1) + u + 1

        def wait_ring(eng, e):
            before = ring[slot[e] - 3] if slot[e] >= 3 else ("top", 0, units - 1)
            if before[0] == "turn":
                eng.wait_ge(rest_done, before[1] + 1)
            elif before[0] == "spread":
                eng.wait_ge(log_done, before[1] + 1)
            else:
                eng.wait_ge(top_found, found(before[1], before[2]))

        def finished(b):
            return mixed_heads[:, b // NC, CH * (b % NC):CH * (b % NC + 1)]

        def queries(rows, b):
            return qs[rows, b // NC % BUFS, b % NC, :, :]

        with nc.Block() as block:
            @block.gpsimd
            def _(pool):
                for n in range(4):
                    pool.memset(k.scratch[:, n, :], 0.0).then_inc(v_cleared, 1)
                pool.wait_ge(v_cleared, 4)
                for b in range(1, BUFS):
                    clear_group(pool, qs, ks, b, zeros_set, 2 * (b - 1))

            @block.sync
            def _(sp):
                def load_group(g):
                    if g >= BUFS:
                        sp.wait_ge(scored, steps * NC * (g - BUFS + 1))
                    for a in range(3):
                        q_src = pieces_dram[0, a, 32 * g:32 * g + 32, :].rearrange("(j d) (c t) -> d c j t", d=8, t=CH)
                        k_src = pieces_dram[1, :, 32 * g:32 * g + 32, :].rearrange("b (j d) t -> b d j t", d=8)
                        for b in range(3):
                            r = 24 * a + 8 * b
                            sp.dma_start(qs[r:r + 8, g % BUFS, :, :, :], q_src).then_inc(loaded[g % BUFS], 16)
                            sp.dma_start(ks[r:r + 8, g % BUFS, :, :], k_src[b]).then_inc(loaded[g % BUFS], 16)

                for g in range(BUFS):
                    if g:
                        sp.wait_ge(zeros_set, 2 * g)
                    load_group(g)
                for b in range(blocks):
                    sp.wait_ge(low_done, b + 1)
                    for a in range(3):
                        dst = queries(slice(R + a, R + a + 1), b).rearrange("p j (t q) -> p (j t) q", q=P)
                        sp.dma_start(dst, max_pieces[:, a, :]).then_inc(laid_out, 16)
                    sp.wait_ge(laid_out, 48 * (b + 1))
                    if b == NC:
                        load_group(BUFS)

            @block.tensor
            def _(pe):
                for t in range(NT):
                    mm = pe.matmul(k.bank(t // 4)[:, P * (t % 4):P * (t % 4 + 1)], k.xn_tile(t), v_w[:, :], start=True, stop=True)
                    if t % 4 == 3:
                        mm.then_inc(v_done, 1)
                for e in order:
                    kind, b, m = e
                    g = b // NC
                    if kind == "tops":
                        if m == 0:
                            pe.wait_ge(loaded[0], 16 * 18)
                            pe.wait_ge(v_copied, 4)
                            pe.wait_ge(ones_set, 1)
                        if m >= 2 * NC:
                            pe.wait_ge(top_found, m // NC - 1)
                        j, t = m // ROWS, m // NC % 4
                        for c in range(NC):
                            mm = pe.matmul(k.bank(4 * (m // NC % 2) + c), queries(slice(0, R), b)[:, j, P * t:P * (t + 1)],
                                           ks[0:R, 0, j, CH * c:CH * (c + 1)], start=True, stop=True)
                        mm.then_inc(top_scored, 1)
                    elif kind == "top":
                        if m == 0 and b % NC == 0:
                            pe.wait_ge(loaded[g % BUFS], 16 * 18 * (g // BUFS + 1))
                        wait_ring(pe, e)
                        j, t, c = m // ROWS, m // NC % 4, m % NC
                        pe.matmul(ring_bank(e), queries(slice(0, R), b)[:, j, P * t:P * (t + 1)],
                                  ks[0:R, g % BUFS, j, CH * c:CH * (c + 1)], start=True, stop=True).then_inc(top_scored, 1)
                    elif kind == "turn":
                        pe.wait_ge(closed, b + 1)
                        wait_ring(pe, e)
                        pe.transpose(ring_bank(e, P, ROWS), neg_max[:, :], k.mat("ident")).then_inc(turned, 1)
                    elif kind == "spread":
                        pe.wait_ge(emptied, b + 1)
                        wait_ring(pe, e)
                        pe.matmul(ring_bank(e), k.mat("den"), finished(b), start=True, stop=True).then_inc(spread, 1)
                    elif kind == "mix":
                        pe.wait_ge(exped, steps * b + m + 2)
                        if m == 0 and b >= 1:
                            pe.wait_ge(emptied, b)
                        for j in range(4):
                            mm = pe.matmul(k.bank(7)[32 * j:32 * j + 32, :], v_pad[:, m // 2, 4 * g + j, :],
                                           probs_t[:, (m + j // 2) % 4, CH * (j % 2):CH * (j % 2 + 1)],
                                           start=(m == 0), stop=(m == steps - 2))
                        mm.then_inc(mixed, 2)
                    elif kind == "step":
                        if m == 0:
                            pe.wait_ge(laid_out, 48 * (b + 1))
                        if steps * b + m >= 2:
                            pe.wait_ge(exped, steps * b + m - 1)
                        for i in range(2):
                            j = 2 * (m % 2) + i
                            mm = pe.matmul(k.bank(2 * (m % 2) + i), ks[0:R + 3, g % BUFS, j, P * (m // 2):P * (m // 2 + 1)],
                                           queries(slice(0, R + 3), b)[:, j, :], start=True, stop=True)
                        mm.then_inc(scored, 1)

            @block.scalar
            def _(act):
                act.preload_act_table_set("natural_log_exp_and_others")
                for b in range(4):
                    act.wait_ge(v_done, b + 1)
                    act.wait_ge(v_cleared, b + 1)
                    act.activation(v_pad[:, 4 * b:4 * b + 4, :, 0:8], k.bank(b).rearrange("p (t h e) -> p t h e", t=4, e=8),
                                   ACT.Copy).then_inc(v_copied, 1)
                for e in order:
                    kind, b, m = e
                    if kind == "step":
                        n = steps * b + m
                        act.wait_ge(scored, n + 1)
                        if n >= 4:
                            act.wait_ge(mixed, n - 3)
                        act.activation(probs_t[:, n % 4, :], k.psum[:, 2 * CH * (n % 2):2 * CH * (n % 2) + 2 * CH], ACT.Exp,
                                       scale=8.0 ** -0.5).then_inc(exped, 1)
                    elif kind == "spread":
                        act.wait_ge(spread, b + 1)
                        act.activation(log[:, :], ring_bank(e), ACT.Ln).then_inc(log_done, 1)
                        act.wait_ge(log_done, b + 1)
                        if b >= 1:
                            act.wait_ge(divided, b)
                        act.activation(inv[:, :], log[:, :], ACT.Exp, scale=-1.0).then_inc(inverted, 1)

            @block.vector
            def _(dve):
                dve.wait_ge(v_cleared, 4)
                dve.memset(v_pad[:, :, :, 8:9].rearrange("p t h e -> p t (h e)"), 1.0).then_inc(ones_set, 1)
                for e in order:
                    kind, b, m = e
                    if kind == "tops":
                        dve.wait_ge(top_scored, m // NC + 1)
                        four = k.psum[:, 4 * CH * (m // NC % 2):4 * CH * (m // NC % 2) + 4 * CH].rearrange("p (c n) -> p c n", c=4)
                        dve.tensor_reduce(tops[:, 0, m // NC, :], four, AX.X, ALU.max).then_inc(top_found, 1)
                    elif kind == "top":
                        dve.wait_ge(top_scored, found(b, m))
                        dve.tensor_reduce(tops[:, b % 2, m // NC, m % NC:m % NC + 1], ring_bank(e), AX.X, ALU.max)\
                            .then_inc(top_found, 1)
                    elif kind == "close":
                        dve.wait_ge(top_found, found(b, units - 1))
                        if b >= 1:
                            dve.wait_ge(turned, b)
                        dve.tensor_reduce(neg_max[:, :], tops[:, b % 2, :, :], AX.X, ALU.max, negate=True).then_inc(closed, 1)
                    elif kind == "turn":
                        dve.wait_ge(turned, b + 1)
                        if b >= 1:
                            dve.wait_ge(laid_out, 48 * b)
                        row = ring_bank(e, P, ROWS)
                        dve.tensor_copy(max_pieces[:, 0, :], row).then_inc(high_done, 1)
                        dve.wait_ge(high_done, b + 1)
                        dve.tensor_tensor(rest[:, :], row, max_pieces[:, 0, :], ALU.subtract).then_inc(rest_done, 1)
                        dve.wait_ge(rest_done, b + 1)
                        dve.tensor_copy(max_pieces[:, 1, :], rest[:, :]).then_inc(middle_done, 1)
                        dve.wait_ge(middle_done, b + 1)
                        dve.tensor_tensor(max_pieces[:, 2, :], rest[:, :], max_pieces[:, 1, :], ALU.subtract).then_inc(low_done, 1)
                    elif kind == "mix" and m == steps - 2:
                        dve.wait_ge(mixed, steps * (b + 1))
                        dve.tensor_copy(finished(b), k.bank(7)).then_inc(emptied, 1)
                    elif kind == "divide":
                        dve.wait_ge(inverted, b + 1)
                        dve.tensor_tensor(finished(b), finished(b), inv[:, :], ALU.mult).then_inc(divided, 1)


def layer1_attention(k, A):
    nc = k.nc
    with ExitStack() as ctx:
        def sb(name, shape, dt=F32):
            return ctx.enter_context(nc.sbuf_tensor(name + "_l1a", shape, dt))

        qk_w, v_w, out_w, bias = sb("qk_w", [P, 4, P]), sb("v_w", [P, P]), sb("out_w", [P, 4, P]), sb("bias", [P, 1])
        mixed_heads = sb("mixed_heads", [P, 4, T])
        v_pad = k.scratch[:, :, :].rearrange("p a b -> p (a b)").rearrange("p (t h e) -> p t h e", t=NT, h=16)
        pieces_dram = nc.dram_tensor("pieces_dram", (2, 3, P, T), BF16).ap()
        out_rows = [(out_w[32 * j:32 * j + 8, g, :], A["L1_attn_outT"][8 * (4 * g + j):8 * (4 * g + j) + 8, :])
                    for g in range(4) for j in range(4)]
        qs, ks = sb("qs", [P, BUFS, NC, 4, CH], BF16), sb("ks", [P, BUFS, 4, T], BF16)
        rope, temps = mixed_heads[:, 0:2, :], mixed_heads[:, 2:4, :].rearrange("p a (b t) -> p (a b) t", t=CH)
        pieces = k.scratch[:, 0:3, :].rearrange("p a t -> p (a t)").bitcast(BF16).rearrange("p (m a t) -> p m a t", m=2, a=3)
        with phase(nc, "cleared", []) as (cleared,):
            with nc.Block() as block:
                @block.vector
                def _(dve):
                    dve.memset(out_w[:, :, :], 0.0).then_inc(cleared, 1)
        layernorm(k, k.x, k.xn, 1e-5, loads=[
            (qk_w[:, :, :], A["L1_attn_qkT"]), (rope, A["const_rope"]), (v_w[:, :], A["L1_attn_vT"]),
            (bias[:, :], A["L1_attn_b_out"])] + out_rows)
        split_into_bf16(k, qk_w, rope, temps, pieces, pieces_dram, qs, ks)
        grouped_attention(k, pieces_dram, v_w, v_pad, mixed_heads, qs, ks)

        project(k, [("vector", [(out_w[:, g, :], part(mixed_heads[:, g, :], c)) for g in range(4)], P, CH,
                     add_to_x(k, c, bias[:, 0:1])) for c in range(NC)])


def shifted_tokens(k, src_pad, h):
    nc = k.nc
    with phase(nc, "low_copied high_copied", []) as (low_copied, high_copied):
        with nc.Block() as block:
            @block.vector
            def _(dve):
                dve.tensor_copy(h[0:64, :], src_pad[0:64, 1:1 + T]).then_inc(low_copied, 1)

            @block.scalar
            def _(act):
                act.activation(h[64:P, :], src_pad[64:P, 0:T], ACT.Copy).then_inc(high_copied, 1)


def window_qk(k, w_qk, w_turned, columns, xpos_dram, q_pad, keys):
    nc = k.nc
    units = [(c, m) for c in range(NC) for m in range(8)]
    names = "landed_even landed_odd projected turned squared summed log_done inverted by_cos by_sin added rotated cleared"
    tiles = [("xpos", [P, 2, 4, CH], F32)]
    with phase(nc, names, tiles) as (landed_even, landed_odd, projected, turned, squared, summed, log_done, inverted, by_cos,
                                     by_sin, added, rotated, cleared, xpos):
        landed = (landed_even, landed_odd)
        buffers = k.scratch[:, :, :].rearrange("p a (b t) -> p a b t", t=CH)
        sq, log, inv = buffers[:, 0, 0:2, :], buffers[:, 0, 2:4, :], buffers[:, 1, 0:2, :]
        cos_part, sin_part, both = buffers[:, 1, 2:4, :], buffers[:, 2, 0:2, :], buffers[:, 2, 2:4, :]
        rotations = [0]
        for _, m in units:
            rotations.append(rotations[-1] + (2 if m < 4 else 1))

        with nc.Block() as block:
            @block.sync
            def _(sp):
                for c in range(NC):
                    if c >= 2:
                        sp.wait_ge(by_cos, 8 * (c - 1))
                        sp.wait_ge(by_sin, 8 * (c - 1))
                    sp.dma_start(xpos[:, c % 2, :, :], xpos_dram[:, :, CH * c:CH * (c + 1)]).then_inc(landed[c % 2], 16)
                for parity in range(2):
                    sp.wait_ge(landed[parity], 16 * NC // 2)

            @block.tensor
            def _(pe):
                for n in range(len(units) + 1):
                    if n < len(units):
                        c, m = units[n]
                        if n >= 3:
                            pe.wait_ge(by_cos, n - 2)
                        pe.matmul(k.bank(n % 3), w_qk[:, P * m:P * (m + 1)], k.xn(c), start=True, stop=True)\
                            .then_inc(projected, 1)
                        if n >= 3:
                            pe.wait_ge(by_sin, n - 2)
                        pe.matmul(k.bank(3 + n % 3), w_turned[:, P * m:P * (m + 1)], k.xn(c), start=True, stop=True)\
                            .then_inc(turned, 1)
                    if n >= 1:
                        u = n - 1
                        pe.wait_ge(squared, u + 1)
                        if u >= 2:
                            pe.wait_ge(log_done, u - 1)
                        pe.matmul(k.bank(6 + u % 2), k.mat("heads64"), sq[:, u % 2, :], start=True, stop=True)\
                            .then_inc(summed, 1)

            @block.scalar
            def _(act):
                act.preload_act_table_set("natural_log_exp_and_others")
                for n in range(len(units) + 1):
                    if n < len(units):
                        act.wait_ge(projected, n + 1)
                        if n >= 2:
                            act.wait_ge(summed, n - 1)
                        act.activation(sq[:, n % 2, :], k.bank(n % 3), ACT.Square).then_inc(squared, 1)
                    if n >= 1:
                        u = n - 1
                        act.wait_ge(summed, u + 1)
                        act.activation(log[:, u % 2, :], k.bank(6 + u % 2), ACT.Ln, bias=k.eps(1e-30)).then_inc(log_done, 1)
                        act.wait_ge(log_done, u + 1)
                        if u >= 2:
                            act.wait_ge(rotated, rotations[u - 1])
                        act.activation(inv[:, u % 2, :], log[:, u % 2, :], ACT.Exp, scale=-0.5).then_inc(inverted, 1)

            @block.gpsimd
            def _(pool):
                pool.memset(q_pad[64:P, :, 0, :], 0.0).then_inc(cleared, 1)
                pool.wait_ge(cleared, 1)
                pool.memset(q_pad[0:64, :, 1, :], 0.0).then_inc(cleared, 1)
                pool.wait_ge(cleared, 2)
                pool.memset(keys[:, :, 0:64], 0.0).then_inc(cleared, 1)
                pool.wait_ge(cleared, 3)
                for n in range(len(units)):
                    pool.wait_ge(by_cos, n + 1)
                    pool.wait_ge(by_sin, n + 1)
                    if n >= 2:
                        pool.wait_ge(rotated, rotations[n - 1])
                    pool.tensor_tensor(both[:, n % 2, :], cos_part[:, n % 2, :], sin_part[:, n % 2, :], ALU.add)\
                        .then_inc(added, 1)

            @block.vector
            def _(dve):
                for n in range(len(units) + 1):
                    if n < len(units):
                        c, m = units[n]
                        table, scale = 2 * (m // 4), 2 * (m // 4)
                        if m == 0:
                            dve.wait_ge(landed[c % 2], 16 * (c // 2 + 1))
                        dve.wait_ge(squared, n + 1)
                        if n >= 2:
                            dve.wait_ge(added, n - 1)
                        dve.scalar_tensor_tensor(out=cos_part[:, n % 2, :], in0=k.bank(n % 3), scalar=columns[:, scale:scale + 1],
                                                 in1=xpos[:, c % 2, table, :], op0=ALU.mult, op1=ALU.mult).then_inc(by_cos, 1)
                        dve.wait_ge(turned, n + 1)
                        dve.scalar_tensor_tensor(out=sin_part[:, n % 2, :], in0=k.bank(3 + n % 3),
                                                 scalar=columns[:, scale + 1:scale + 2], in1=xpos[:, c % 2, table + 1, :],
                                                 op0=ALU.mult, op1=ALU.mult).then_inc(by_sin, 1)
                    if n >= 1:
                        u = n - 1
                        c, m = units[u]
                        dve.wait_ge(added, u + 1)
                        dve.wait_ge(inverted, u + 1)
                        if m < 4:
                            places = [(slice(64 * s, 64 * s + 64), q_pad[64 * s:64 * s + 64, m, s, CH * c:CH * (c + 1)])
                                      for s in range(2)]
                        else:
                            places = [(slice(0, P), keys[:, m - 4, 64 + CH * c:64 + CH * (c + 1)])]
                        for rows, place in places:
                            dve.scalar_tensor_tensor(out=place, in0=inv[rows, u % 2, :], scalar=1e12, in1=both[rows, u % 2, :],
                                                     op0=ALU.min, op1=ALU.mult).then_inc(rotated, 1)


def window_attention(k, q_pad, keys, wv, bands, ident, o):
    nc = k.nc
    names = ("v_done v_copied even_zeroed even_low even_high scored max_done exp_done inverted scaled transposed copied_low copied_high "
             "mixed out_done")
    tiles = [("s", [P, 2, 8, P], F32), ("probs_t", [P, 2, 8, P], F32), ("v_odd", [P, 2, CH], F32), ("v_even", [P, 3, CH], F32),
             ("neg_max", [P, 2, 8], F32), ("total", [P, 2, 8], F32), ("inv", [P, 2, 8], F32)]
    with phase(nc, names, tiles) as (v_done, v_copied, even_zeroed, even_low, even_high, scored, max_done, exp_done, inverted, scaled,
                                     transposed, copied_low, copied_high, mixed, out_done, s, probs_t, v_odd, v_even,
                                     neg_max, total, inv):
        def scores(t):
            return k.psum[:, 2 * CH * (t % 2):2 * CH * (t % 2) + 2 * CH].rearrange("p (h j) -> p h j", h=8)

        with nc.Block() as block:
            @block.gpsimd
            def _(pool):
                pool.memset(v_even[64:P, 0, :], 0.0).then_inc(even_zeroed, 1)
                pool.wait_ge(even_zeroed, 1)
                for t in range(NT):
                    pool.wait_ge(v_copied, t + 1)
                    if t >= 3:
                        pool.wait_ge(mixed, t - 2)
                    pool.tensor_copy(v_even[0:64, t % 3, :], v_odd[0:64, t % 2, :]).then_inc(even_low, 1)
                    pool.wait_ge(even_low, t + 1)
                    if t >= 2:
                        pool.wait_ge(mixed, t - 1)
                    pool.tensor_copy(v_even[64:P, (t + 1) % 3, :], v_odd[64:P, t % 2, :]).then_inc(even_high, 1)
                    pool.wait_ge(even_high, t + 1)

            @block.tensor
            def _(pe):
                def values(t):
                    if t >= 1:
                        pe.wait_ge(v_copied, t)
                    pe.matmul(k.bank(4), k.xn_tile(t), wv, start=True, stop=True).then_inc(v_done, 1)

                for t in range(NT + 1):
                    if t < NT:
                        if t >= 2:
                            pe.wait_ge(exp_done, t - 1)
                        for half in range(2):
                            pe.matmul(k.bank(2 * (t % 2) + half), ident[:, :], bands[:, min(t, 1), :, :], start=True, stop=False)
                            for i in range(4):
                                h = 4 * half + i
                                own = keys[:, h // 2, 64 + P * t:64 + P * (t + 1)]
                                before = keys[:, h // 2, P * t:P * t + 64]
                                q_first, q_second = (q_pad[:, h // 2, h % 2, P * t + 64 * r:P * t + 64 * r + 64] for r in range(2))
                                pe.matmul(scores(t)[0:64, h, 0:64], q_first, own[:, 0:64], start=False, stop=False)
                                pe.matmul(scores(t)[0:64, h, 64:P], q_first, before, start=False, stop=(i == 3))
                                mm = pe.matmul(scores(t)[64:P, h, :], q_second, own, start=False, stop=(i == 3))
                        mm.then_inc(scored, 1)
                    if t >= 1:
                        u = t - 1
                        pe.wait_ge(scaled, u + 1)
                        if u >= 1:
                            pe.wait_ge(copied_low, u)
                            pe.wait_ge(copied_high, u)
                        for h in range(8):
                            mm = pe.transpose(k.bank(5 + h // 4)[:, P * (h % 4):P * (h % 4 + 1)], s[:, u % 2, h, :],
                                              k.mat("ident"))
                        mm.then_inc(transposed, 1)
                    if t < NT:
                        values(t)
                    if t >= 1:
                        u = t - 1
                        pe.wait_ge(copied_low, u + 1)
                        pe.wait_ge(copied_high, u + 1)
                        pe.wait_ge(v_copied, u + 1)
                        pe.wait_ge(even_low, u + 1)
                        if u >= 1:
                            pe.wait_ge(even_high, u)
                        else:
                            pe.wait_ge(even_zeroed, 1)
                        if u >= 1:
                            pe.wait_ge(out_done, u)
                        for m in range(4):
                            for r in range(2):
                                for i in range(2):
                                    h = 2 * m + i
                                    mm = pe.matmul(k.bank(7)[64 * i:64 * i + 64, P * m + 64 * r:P * m + 64 * r + 64],
                                                   (v_odd[:, u % 2, :] if r else v_even[:, u % 3, :])[:, 64 * h:64 * h + 64],
                                                   probs_t[:, u % 2, h, 64 * r:64 * r + 64],
                                                   start=True, stop=True)
                        mm.then_inc(mixed, 1)

            @block.vector
            def _(dve):
                for t in range(NT + 1):
                    if t >= 1:
                        u = t - 1
                        dve.wait_ge(exp_done, u + 1)
                        dve.reciprocal(inv[:, u % 2, :], total[:, u % 2, :]).then_inc(inverted, 1)
                        dve.wait_ge(inverted, u + 1)
                        share = inv[:, u % 2, :].unsqueeze(2).to_broadcast([P, 8, P])
                        dve.tensor_tensor(s[:, u % 2, :, :], s[:, u % 2, :, :], share, ALU.mult).then_inc(scaled, 1)
                    if t < NT:
                        dve.wait_ge(scored, t + 1)
                        dve.tensor_reduce(neg_max[:, t % 2, :], scores(t), AX.X, ALU.max, negate=True).then_inc(max_done, 1)
                    if t >= 1:
                        u = t - 1
                        dve.wait_ge(transposed, u + 1)
                        if u >= 2:
                            dve.wait_ge(mixed, u - 1)
                        dve.tensor_copy(probs_t[:, u % 2, 0:4, :].rearrange("p a b -> p (a b)"), k.bank(5)).then_inc(copied_low, 1)
                    if t < NT:
                        dve.wait_ge(v_done, t + 1)
                        if t >= 2:
                            dve.wait_ge(mixed, t - 1)
                            dve.wait_ge(even_low, t - 1)
                            dve.wait_ge(even_high, t - 1)
                        dve.tensor_copy(v_odd[:, t % 2, :], k.bank(4)).then_inc(v_copied, 1)

            @block.scalar
            def _(act):
                act.preload_act_table_set("natural_log_exp_and_others")
                for t in range(NT + 1):
                    if t >= 1:
                        u = t - 1
                        act.wait_ge(transposed, u + 1)
                        if u >= 2:
                            act.wait_ge(mixed, u - 1)
                        act.activation(probs_t[:, u % 2, 4:8, :].rearrange("p a b -> p (a b)"), k.bank(6), ACT.Copy)\
                            .then_inc(copied_high, 1)
                    if t < NT:
                        act.wait_ge(max_done, t + 1)
                        if t >= 2:
                            act.wait_ge(transposed, t - 1)
                        for h in range(8):
                            ins = act.activation(s[:, t % 2, h, :], scores(t)[:, h, :], ACT.Exp,
                                                 bias=neg_max[:, t % 2, h:h + 1], accum_out=total[:, t % 2, h:h + 1])
                        ins.then_inc(exp_done, 1)
                    if t >= 1:
                        u = t - 1
                        act.wait_ge(mixed, u + 1)
                        act.activation(o[:, :, P * u:P * (u + 1)], k.bank(7).rearrange("p (a b) -> p a b", a=4), ACT.Copy)\
                            .then_inc(out_done, 1)


def gated_ffn(k, xn, w1, b1, w2, b2, z, hidden, loads):
    nc = k.nc
    rows = [min(P, hidden - P * j) for j in range(3)]
    units = [(c, j) for c in range(NC) for j in range(3)]
    with phase(nc, "gate_done value_done acted gated out_done added landed",
               [("gelu", [P, 2, CH], F32), ("h", [P, 3, T], F32)]) as (
            gate_done, value_done, acted, gated, out_done, added, landed, gelu, h):
        with nc.Block() as block:
            @block.sync
            def _(sp):
                for tile, dram in loads:
                    sp.dma_start(tile, dram).then_inc(landed, 16)
                if loads:
                    sp.wait_ge(landed, 16 * len(loads))

            @block.tensor
            def _(pe):
                for n, (c, j) in enumerate(units):
                    r = rows[j]
                    if n >= 2:
                        pe.wait_ge(acted, n - 1)
                    pe.matmul(k.bank(n % 2, CH, r), w1[:, hidden + P * j:hidden + P * j + r], xn(c), start=True, stop=True)\
                        .then_inc(gate_done, 1)
                    if n >= 2:
                        pe.wait_ge(gated, n - 1)
                    pe.matmul(k.bank(2 + n % 2, CH, r), w1[:, P * j:P * j + r], xn(c), start=True, stop=True)\
                        .then_inc(value_done, 1)
                for c in range(NC):
                    pe.wait_ge(gated, 3 * c + 3)
                    for j in range(3):
                        mm = pe.matmul(k.bank(4 + c), w2[0:rows[j], j, :], h[0:rows[j], j, CH * c:CH * (c + 1)],
                                       start=(j == 0), stop=(j == 2))
                    mm.then_inc(out_done, 1)

            @block.scalar
            def _(act):
                for n, (c, j) in enumerate(units):
                    r = rows[j]
                    act.wait_ge(gate_done, n + 1)
                    if n >= 2:
                        act.wait_ge(gated, n - 1)
                    act.activation(gelu[0:r, n % 2, :], k.bank(n % 2, CH, r), ACT.Gelu, bias=b1[0:r, 3 + j:4 + j]).then_inc(acted, 1)

            @block.vector
            def _(dve):
                for n, (c, j) in enumerate(units):
                    r = rows[j]
                    dve.wait_ge(value_done, n + 1)
                    dve.wait_ge(acted, n + 1)
                    dve.scalar_tensor_tensor(out=h[0:r, j, CH * c:CH * (c + 1)], in0=k.bank(2 + n % 2, CH, r),
                                             scalar=b1[0:r, j:j + 1], in1=gelu[0:r, n % 2, :], op0=ALU.add, op1=ALU.mult)\
                        .then_inc(gated, 1)
                for c in range(NC):
                    dve.wait_ge(out_done, c + 1)
                    zc = z[:, 1 + CH * c:1 + CH * (c + 1)]
                    dve.scalar_tensor_tensor(out=zc, in0=k.bank(4 + c), scalar=b2, in1=zc, op0=ALU.add, op1=ALU.add)\
                        .then_inc(added, 1)


def layer1_ffn(k, A):
    nc = k.nc
    hidden = A["L1_ffn_w1"].shape[2] // 2
    with ExitStack() as ctx:
        def sb(name, shape, dt=F32):
            return ctx.enter_context(nc.sbuf_tensor(name + "_l1f", shape, dt))

        z, h = sb("z", [P, T + 1]), k.s4
        wqkv, w_turned, wo = sb("wqkv", [P, 1536]), sb("w_turned", [P, 1024]), sb("wo", [P, 4, P])
        w1, w2, b1, all_columns = sb("w1", [P, 2 * hidden]), sb("w2", [P, 3, P]), sb("b1", [P, 2, 6]), sb("columns", [P, 2, 7])
        bands, ident = sb("bands", [P, 2, 4, P], BF16), sb("ident_bf16", [P, P], BF16)

        def z_part(c):
            return z[:, 1 + CH * c:1 + CH * (c + 1)]

        def h_part(c):
            return part(h, c)

        def attention_weights(layer):
            return [(wqkv[:, :], A["L1_ffn_wqkv"][layer]), (w_turned[:, :], A["L1_ffn_w_turned"][layer]),
                    (wo[:, :, :], A["L1_ffn_wo"][layer].rearrange("(j p) d -> p j d", p=P))]

        def ffn_weights(layer):
            return [(w1[:, :], A["L1_ffn_w1"][layer]),
                    (w2[:, 0:2, :], A["L1_ffn_w2"][layer, 0:2 * P].rearrange("(j p) d -> p j d", p=P)),
                    (w2[0:hidden - 2 * P, 2, :], A["L1_ffn_w2"][layer, 2 * P:hidden])]

        with nc.sbuf_tensor("bands_f32", [P, 2, P], F32) as bands_f32:
            layernorm(k, k.x, z_part, 1e-5, loads=attention_weights(0) + [
                (bands_f32[:, :, :], A["const_bands"]), (all_columns[:, :, :], A["L1_ffn_columns"].rearrange("a p n -> p a n")),
                (b1[:, :, :], A["L1_ffn_b1"].rearrange("a p n -> p a n"))])
            with phase(nc, "cleared rounded", []) as (cleared, rounded):
                with nc.Block() as block:
                    @block.vector
                    def _(dve):
                        dve.memset(z[:, 0:1], 0.0).then_inc(cleared, 1)
                        dve.tensor_copy(ident[:, :], k.mat("ident")).then_inc(rounded, 1)
                        for n in range(2):
                            dve.tensor_copy(bands[:, n, :, :], bands_f32[:, n, :].unsqueeze(1).to_broadcast([P, 4, P]))\
                                .then_inc(rounded, 1)
        for layer in range(2):
            columns = all_columns[:, layer, :]
            shifted_tokens(k, z, k.xnpad[:, LEAD:LEAD + T])
            with nc.sbuf_tensor(f"q_{layer}", [P, 4, 2, T], F32) as q_pad, nc.sbuf_tensor(f"k_{layer}", [P, 4, 64 + T], F32) as keys:
                window_qk(k, wqkv, w_turned, columns, A["const_xpos"], q_pad, keys)
                o = k.scratch
                window_attention(k, q_pad, keys, wqkv[:, 1024:1536], bands, ident, o)
                project(k, [("vector", [(wo[:, j, :], o[:, j, CH * c:CH * (c + 1)]) for j in range(4)], P, CH,
                             lambda dve, ps, c=c: dve.tensor_tensor(z_part(c), z_part(c), ps, ALU.add)) for c in range(NC)])
            shifted_tokens(k, z, h)
            layernorm(k, h_part, k.xn, 1e-5, columns[:, 4:5], columns[:, 5:6], loads=ffn_weights(layer))
            gated_ffn(k, k.xn, w1, b1[:, layer, :], w2, columns[:, 6:7], z, hidden,
                      attention_weights(layer + 1) if layer == 0 else [])
        add_tile(k, z[:, 1:1 + T])


def layer2_ffn(k, A):
    nc = k.nc
    E, CAP, F = 16, 32, 256
    SLOT = E * CAP
    G = SLOT // P
    with ExitStack() as ctx:
        def sb(name, shape, dt=F32):
            return ctx.enter_context(nc.sbuf_tensor(name + "_l2f", shape, dt))

        r1, r2 = sb("r1", [P, P]), sb("r2", [P, E])
        w1, w2, w3 = sb("w1", [P, E, F]), sb("w2", [P, E, F]), sb("w3", [P, E, 2, P])
        logits, left = sb("logits", [E, T]), sb("left", [E, T])
        best, place, place_f = sb("best", [E, CAP]), sb("place", [E, CAP], U32), sb("place_f", [E, CAP])
        st, share = sb("st", [E, 6]), sb("share", [E, CAP])
        places, place_col, share_col = sb("places", [P, SLOT]), sb("place_col", [P, G]), sb("share_col", [P, G])
        token, iota = sb("token", [P, NT]), sb("iota", [P, T])
        x_tok, x_slot = sb("x_tok", [P, NT, P]), sb("x_slot", [P, SLOT])
        gate, h, h_t, result = sb("gate", [P, G, F]), sb("h", [P, G, F]), sb("h_t", [P, G, 2, P]), sb("result", [P, G, P])
        place_dram = nc.dram_tensor("place_dram", (E, CAP), F32).ap()
        share_dram = nc.dram_tensor("share_dram", (E, CAP), F32).ap()
        layernorm(k, k.x, k.xn, 1e-5, loads=[
            (r1[:, :], A["L2_ffn_router_w1"]), (r2[:, :], A["L2_ffn_router_w2"]), (token[:, :], A["const_token"])])
        project(k, [("scalar", [(r1[:, :], k.xn(c))], P, CH,
                     lambda act, ps, c=c: act.activation(part(k.s1, c), ps, ACT.Silu)) for c in range(NC)])
        project(k, [("scalar", [(r2[:, :], part(k.s1, c))], E, CH, copy_out(part(logits, c))) for c in range(NC)])

        names = "step exp_done weighed written row_read turned copied marked gathered landed"
        with phase(nc, names, []) as (step, exp_done, weighed, written, row_read, turned, copied, marked, gathered, landed):
            rounds = CAP // 8
            with nc.Block() as block:
                @block.vector
                def _(dve):
                    for r in range(rounds):
                        src = logits if r == 0 else left
                        dve.max(best[:, 8 * r:8 * r + 8], src[:, :]).then_inc(step, 1)
                        dve.wait_ge(step, 3 * r + 1)
                        dve.max_index(place[:, 8 * r:8 * r + 8], best[:, 8 * r:8 * r + 8], src[:, :]).then_inc(step, 1)
                        dve.wait_ge(step, 3 * r + 2)
                        dve.match_replace(left[:, :], best[:, 8 * r:8 * r + 8], src[:, :], MASKED).then_inc(step, 1)
                        dve.wait_ge(step, 3 * r + 3)
                    n = 3 * rounds
                    dve.tensor_copy(place_f[:, :], place[:, :]).then_inc(step, 1)
                    dve.tensor_scalar(st[:, 0:1], best[:, 0:1], -1.0, None, ALU.mult).then_inc(step, 1)
                    dve.wait_ge(exp_done, 2)
                    dve.reciprocal(st[:, 2:3], st[:, 1:2]).then_inc(step, 1)
                    dve.wait_ge(step, n + 3)
                    dve.tensor_scalar(share[:, :], share[:, :], st[:, 2:3], None, ALU.mult).then_inc(step, 1)
                    dve.wait_ge(step, n + 4)
                    dve.tensor_reduce(st[:, 3:4], share[:, :], AX.X, ALU.add).then_inc(step, 1)
                    dve.wait_ge(step, n + 5)
                    dve.tensor_scalar(st[:, 4:5], st[:, 3:4], 1e-9, None, ALU.add).then_inc(step, 1)
                    dve.wait_ge(step, n + 6)
                    dve.reciprocal(st[:, 5:6], st[:, 4:5]).then_inc(step, 1)
                    dve.wait_ge(step, n + 7)
                    dve.tensor_scalar(share[:, :], share[:, :], st[:, 5:6], None, ALU.mult).then_inc(weighed, 1)
                    dve.wait_ge(row_read, 48)
                    for t in range(NT):
                        mark = k.scratch[:, t // 4, CH * (t % 4):CH * (t % 4 + 1)]
                        dve.tensor_scalar(mark, places[:, :], token[:, t:t + 1], None, ALU.is_equal).then_inc(marked, 1)
                    dve.wait_ge(gathered, 1)
                    dve.tensor_copy(x_slot[:, :], k.bank(4)).then_inc(step, 1)

                @block.scalar
                def _(act):
                    act.dma_start(w1[:, :, :], A["L2_ffn_w1"].rearrange("e p f -> p e f")).then_inc(landed, 16)
                    act.dma_start(w2[:, :, :], A["L2_ffn_w2"].rearrange("e p f -> p e f")).then_inc(landed, 16)
                    act.dma_start(w3[:, :, :, :], A["L2_ffn_w3"].rearrange("e (j p) d -> p e j d", p=P)).then_inc(landed, 16)
                    act.dma_start(iota[:, :], A["const_iota"]).then_inc(landed, 16)
                    act.wait_ge(step, 3 * rounds + 2)
                    act.activation(left[:, :], logits[:, :], ACT.Exp, bias=st[:, 0:1], accum_out=st[:, 1:2]).then_inc(exp_done, 1)
                    act.activation(share[:, :], best[:, :], ACT.Exp, bias=st[:, 0:1]).then_inc(exp_done, 1)
                    for b in range(4):
                        act.wait_ge(turned, b + 1)
                        act.activation(x_tok[:, 4 * b:4 * b + 4, :].rearrange("p a b -> p (a b)"), k.bank(b), ACT.Copy)\
                            .then_inc(copied, 1)
                    act.wait_ge(landed, 64)

                @block.sync
                def _(sp):
                    sp.wait_ge(step, 3 * rounds + 1)
                    sp.dma_start(place_dram, place_f[:, :]).then_inc(written, 16)
                    sp.wait_ge(weighed, 1)
                    sp.dma_start(share_dram, share[:, :]).then_inc(written, 16)
                    sp.wait_ge(written, 32)
                    row = place_dram.rearrange("e c -> (e c)")
                    sp.dma_start(places[:, :], row.rearrange("(a n) -> a n", a=1).to_broadcast([P, SLOT])).then_inc(row_read, 16)
                    sp.dma_start(place_col[:, :], row.rearrange("(g p) -> p g", p=P), allow_slow_non_contiguous=True).then_inc(row_read, 16)
                    sp.dma_start(share_col[:, :], share_dram.rearrange("e c -> (e c)").rearrange("(g p) -> p g", p=P),
                                 allow_slow_non_contiguous=True)\
                        .then_inc(row_read, 16)

                @block.tensor
                def _(pe):
                    for b in range(4):
                        for a in range(4):
                            mm = pe.transpose(k.bank(b)[:, P * a:P * (a + 1)], k.xn_tile(4 * b + a), k.mat("ident"))
                        mm.then_inc(turned, 1)
                    for t in range(NT):
                        pe.wait_ge(copied, t // 4 + 1)
                        pe.wait_ge(marked, t + 1)
                        mm = pe.matmul(k.bank(4), x_tok[:, t, :], k.scratch[:, t // 4, CH * (t % 4):CH * (t % 4 + 1)],
                                       start=(t == 0), stop=(t == NT - 1))
                    mm.then_inc(gathered, 1)

        names = "raised acted gated turned copied lowered weighed marked out_done added"
        with phase(nc, names, []) as (raised, acted, gated, turned, copied, lowered, weighed, marked, out_done, added):
            with nc.Block() as block:
                @block.tensor
                def _(pe):
                    for g in range(G):
                        for base, w in ((0, w1), (2, w2)):
                            for j in range(4):
                                e = 4 * g + j
                                mm = pe.matmul(k.bank(base + g // 2)[32 * j:32 * j + 32, F * (g % 2):F * (g % 2 + 1)],
                                               x_slot[:, CAP * e:CAP * (e + 1)], w[:, e, :], start=True, stop=True)
                    mm.then_inc(raised, 1)
                    for g in range(G):
                        pe.wait_ge(gated, g + 1)
                        for j in range(2):
                            mm = pe.transpose(k.bank(4 + g // 2)[:, F * (g % 2) + P * j:F * (g % 2) + P * (j + 1)],
                                              h[:, g, P * j:P * (j + 1)], k.mat("ident"))
                        mm.then_inc(turned, 1)
                    for g in range(G):
                        pe.wait_ge(copied, g // 2 + 1)
                        for e in range(4 * g, 4 * g + 4):
                            j = e % 4
                            for f in range(2):
                                mm = pe.matmul(k.bank(6)[32 * j:32 * j + 32, P * g:P * (g + 1)],
                                               h_t[:, g, f, CAP * j:CAP * (j + 1)], w3[:, e, f, :], start=(f == 0), stop=(f == 1))
                    mm.then_inc(lowered, 1)
                    pe.wait_ge(weighed, G)
                    for c in range(NC):
                        for g in range(G):
                            pe.wait_ge(marked, g + 1)
                            mm = pe.matmul(k.bank(c), result[:, g, :], k.scratch[:, g, CH * c:CH * (c + 1)],
                                           start=(g == 0), stop=(g == G - 1))
                        mm.then_inc(out_done, 1)

                @block.scalar
                def _(act):
                    act.wait_ge(raised, 1)
                    for b in range(2):
                        act.activation(gate[:, 2 * b:2 * b + 2, :].rearrange("p a b -> p (a b)"), k.bank(b), ACT.Silu)\
                            .then_inc(acted, 1)
                    for b in range(2):
                        act.wait_ge(turned, 2 * b + 2)
                        act.activation(h_t[:, 2 * b:2 * b + 2, :, :].rearrange("p a j b -> p (a j b)"), k.bank(4 + b), ACT.Copy)\
                            .then_inc(copied, 1)

                @block.vector
                def _(dve):
                    for g in range(G):
                        dve.tensor_scalar(k.scratch[:, g, :], iota[:, :], place_col[:, g:g + 1], None, ALU.is_equal)\
                            .then_inc(marked, 1)
                    for g in range(G):
                        dve.wait_ge(acted, g // 2 + 1)
                        dve.tensor_tensor(h[:, g, :], k.bank(2 + g // 2)[:, F * (g % 2):F * (g % 2 + 1)], gate[:, g, :], ALU.mult)\
                            .then_inc(gated, 1)
                    dve.wait_ge(lowered, 1)
                    for g in range(G):
                        dve.tensor_scalar(result[:, g, :], k.bank(6)[:, P * g:P * (g + 1)], share_col[:, g:g + 1], None, ALU.mult)\
                            .then_inc(weighed, 1)
                    for c in range(NC):
                        dve.wait_ge(out_done, c + 1)
                        dve.tensor_tensor(k.x(c), k.x(c), k.bank(c), ALU.add).then_inc(added, 1)


FILLS = 20


def causal_schedule():
    blocks = [(p, q, s) for p in range(8) for q in range(NC) for s in range(2)]
    n_units = 4 * len(blocks)
    order = [("fill", 0, tile) for tile in range(FILLS)] + [("score", 0, 0)]
    late = []
    for n in range(n_units + 6):
        b, i = n // 4, n % 4
        side, late_now = late, []
        if 1 <= b <= len(blocks):
            q = blocks[b - 1][1]
            keys = 4 * (q + 1)
            pairs = range(2 * (q + 1) * i // 4, 2 * (q + 1) * (i + 1) // 4)
            if i == 2:
                side = [("share", b - 1, 0)] + side
            for m in pairs:
                side += [("turn", b - 1, 2 * m), ("turn", b - 1, 2 * m + 1)]
                side.append(("mix", b - 1, m))
            if i == 3:
                side.append(("weigh", b - 1, 0))
                p, q, s = blocks[b - 1]
                if q == NC - 1 and s == 1:
                    late_now.append(("project", p, 0))
        late = late_now
        if n < n_units:
            p, q, s = blocks[b]
            local = 4 * (2 * q + s) + i
            if p < 7 and 8 <= local < 8 + FILLS:
                side.append(("fill", p + 1, local - 8))
        lists = []
        if n < n_units:
            q = blocks[b][1]
            lists.append([((j + 0.1) / (q + 1), 1, ("exp", n, j)) for j in range(q + 1)])
            if i == 3:
                lists.append([(1.0, 3, ("sum", b, 0))])
        if n + 1 < n_units:
            q = blocks[(n + 1) // 4][1]
            lists.append([((j + 0.25) / (q + 1), 2, ("score", n + 1, j)) for j in range(q + 1)])
        lists.append([(m / max(1, len(side)), 0, e) for m, e in enumerate(side)])
        order += [e for _, _, _, e in sorted((at, kind, m, e) for lst in lists for m, (at, kind, e) in enumerate(lst))]
    return blocks, order


def causal_attention(k, wq, wk, wv, proj, columns, unscale, masks, bv):
    nc = k.nc
    blocks, order = causal_schedule()
    S_BANKS = 5
    SIDE_BANKS = 7 - S_BANKS
    RING = 5
    names = ("scored part_max raw_max halved split maxed exped bank_filled copied_v copied_s mixed totalled inverted weighed")
    tiles = [("q_parts", [P, 2, 2, T], F16), ("k_low", [P, 2, 2, T], F16), ("probs", [P, 2, 4, T], F32), ("probs_t", [P, RING, CH], F32),
             ("staged", [P, 2, CH], F32), ("tops", [P, 2, 4], F32), ("raw", [P, 2], F32), ("neg_max", [P, 2], F32), ("total", [P, 16, 4], F32), ("sums", [P, 2, 4], F32),
             ("inv", [P, 2, 4], F32), ("shares", [P, 2, CH], F32), ("z", [P, 2, T], F32)]
    with phase(nc, names, tiles) as (scored, part_max, raw_max, halved, split, maxed, exped, bank_filled, copied_v, copied_s, mixed, totalled,
                                     inverted, weighed,
                                     q_parts, k_low, probs, probs_t, staged, tops, raw, neg_max, total, sums, inv, shares, z):
        k_high = k.scratch[:, 0:2, :].rearrange("p a t -> p (a t)").bitcast(F16).rearrange("p (a s t) -> p a s t", a=2, s=2)
        side = [e for e in order if e[0] in ("fill", "turn", "share", "project")]
        side_index = {e: m for m, e in enumerate(side)}
        engine_of, count_of = [], []
        n_v = n_s = 0
        for m, e in enumerate(side):
            if e[0] == "turn":
                by_s = m % 2 == 0 and not (blocks[e[1]][1] == 0 and e[2] == 1)
            else:
                by_s = e[0] == "share" or (e[0] == "fill" and e[2] < 16)
            n_s, n_v = n_s + by_s, n_v + (not by_s)
            engine_of.append("s" if by_s else "v")
            count_of.append(n_s if by_s else n_v)
        turn_index = {e[1:]: m for m, e in enumerate([e for e in side if e[0] == "turn"])}
        chunk_index = {e[1:]: m for m, e in enumerate([e for e in order if e[0] == "score"])}

        def wait_copied(eng, e):
            m = side_index[e]
            eng.wait_ge(copied_s if engine_of[m] == "s" else copied_v, count_of[m])

        def wait_side_bank(eng, e):
            if side_index[e] >= SIDE_BANKS:
                wait_copied(eng, side[side_index[e] - SIDE_BANKS])

        def chunks_through(b):
            return chunk_index[(4 * b + 3, blocks[b][1])] + 1

        def last_turn(b):
            return ("turn", b, 4 * blocks[b][1] + 3)

        def mixes_through(b):
            return turn_index[last_turn(b)[1:]] + 1

        def width(n, j):
            return CH if j < blocks[n // 4][1] else P * (n % 4 + 1)

        def first_query(b, kt):
            return max(0, kt - 4 * blocks[b][1])

        with nc.Block() as block:
            @block.tensor
            def _(pe):
                pending = []

                def mix(b, m):
                    p, q, s = blocks[b]
                    if m == 0 and b >= 1:
                        pe.wait_ge(weighed, b)
                    if m == 0:
                        wait_copied(pe, ("fill", p, FILLS - 1))
                    wait_copied(pe, ("turn", b, 2 * m))
                    wait_copied(pe, ("turn", b, 2 * m + 1))
                    for half in range(2):
                        kt = 2 * m + half
                        a = 0 if m == 0 else first_query(b, kt)
                        pe.matmul(k.bank(7)[64 * half:64 * half + 64, P * a:CH],
                                  k.scratch[:, 2 + p % 2, P * kt + 64 * s:P * kt + 64 * s + 64],
                                  probs_t[:, turn_index[(b, kt)] % RING, P * a:CH],
                                  start=(m == 0), stop=(m == 2 * q + 1)).then_inc(mixed, 1)

                for e in order:
                    kind = e[0]
                    if kind == "score":
                        n, j = e[1:]
                        p, q, s = blocks[n // 4]
                        c = chunk_index[(n, j)]
                        if c >= S_BANKS:
                            pe.wait_ge(exped, c - S_BANKS + 1)
                        if j == 0 and q == 0 and s == 0 and n % 4 == 0:
                            pe.wait_ge(split, 16 * (p + 1))
                        w = width(n, j)
                        t = 4 * q + n % 4
                        q_tile = q_parts[:, p % 2, s, P * t:P * (t + 1)]
                        keys = slice(CH * j, CH * j + w)
                        pe.matmul(k.bank(c % S_BANKS, w), q_tile, k_high[:, p % 2, s, keys], start=True, stop=False)
                        if j == q:
                            pe.matmul(k.bank(c % S_BANKS, w)[:, w - P:w], masks[:, 0, :], masks[:, 1, :], start=False, stop=False)
                        pe.matmul(k.bank(c % S_BANKS, w), q_tile, k_low[:, p % 2, s, keys], start=False, stop=True)\
                            .then_inc(scored, 1)
                    elif kind == "mix":
                        pending.append(e[1:])
                        if len(pending) > 1:
                            mix(*pending.pop(0))
                    elif kind == "weigh":
                        while pending:
                            mix(*pending.pop(0))
                    elif e in side_index:
                        bank = k.bank(S_BANKS + side_index[e] % SIDE_BANKS)
                        wait_side_bank(pe, e)
                        if kind == "fill":
                            p, tile = e[1:]
                            if tile < 16:
                                h = 2 * p + tile // 4 % 2
                                w = (wq if tile < 8 else wk)[:, 64 * h:64 * h + 64]
                                for half in range(2):
                                    mm = pe.matmul(bank[64 * half:64 * half + 64, :], w, k.xn(tile % 4), start=True, stop=True)
                            else:
                                for a in range(4):
                                    mm = pe.matmul(bank[:, P * a:P * (a + 1)], k.xn_tile(4 * (tile - 16) + a),
                                                   wv[:, P * p:P * (p + 1)], start=True, stop=True)
                        elif kind == "turn":
                            b, kt = e[1:]
                            if kt == 0:
                                pe.wait_ge(exped, chunks_through(b))
                            for a in range(first_query(b, kt), 4):
                                mm = pe.transpose(bank[:, P * a:P * (a + 1)], probs[:, b % 2, a, P * kt:P * (kt + 1)],
                                                  k.mat("ident"))
                        elif kind == "share":
                            b = e[1]
                            pe.wait_ge(inverted, b + 1)
                            for a in range(4):
                                column = inv[:, b % 2, a:a + 1].to_broadcast([P, P])
                                mm = pe.transpose(bank[:, P * a:P * (a + 1)], column, k.mat("ident"))
                        else:
                            pe.wait_ge(weighed, 8 * (e[1] + 1))
                            for j in range(16):
                                rows = z[:, :, :].rearrange("p s (r j) -> p s r j", j=16)[:, :, :, j]
                                mm = pe.matmul(bank[:, 0:2 * P], proj[:, j, :], rows, start=(j == 0), stop=(j == 15))
                        mm.then_inc(bank_filled, 1)

            def fill_place(p, tile):
                s, tokens = tile // 4 % 2, slice(CH * (tile % 4), CH * (tile % 4 + 1))
                if tile < 8:
                    return q_parts[:, p % 2, s, tokens], q_parts[64:P, p % 2, s, tokens], slice(64, P)
                return k_high[:, p % 2, s, tokens], k_low[:, p % 2, s, tokens], slice(0, P)

            def fill_column(p, tile):
                n = 16 * (tile // 8) + 2 * p + tile // 4 % 2
                return columns[:, n:n + 1]

            def before_fill(eng, p, tile):
                if p >= 2:
                    last = 8 * (p - 1) - 1
                    eng.wait_ge(scored, chunks_through(last))
                    if tile >= 16:
                        eng.wait_ge(mixed, mixes_through(last))

            def before_turn_copy(eng, e):
                t = turn_index[e[1:]]
                if t >= RING:
                    eng.wait_ge(mixed, t - RING + 1)

            @block.gpsimd
            def _(pool):
                for p in range(8):
                    for tile in range(16):
                        n = 16 * p + tile
                        wait_copied(pool, ("fill", p, tile))
                        before_fill(pool, p, tile)
                        first, second, rows = fill_place(p, tile)
                        pool.tensor_copy(first, staged[:, n % 2, :]).then_inc(halved, 1)
                        pool.wait_ge(halved, n + 1)
                        pool.tensor_tensor(second, staged[rows, n % 2, :], first[rows, :], ALU.subtract).then_inc(split, 1)
                        pool.wait_ge(split, n + 1)

            @block.scalar
            def _(act):
                for e in order:
                    if e[0] == "exp":
                        n, j = e[1:]
                        b = n // 4
                        act.wait_ge(maxed, n + 1)
                        if b >= 2 and n % 4 == 0 and j == 0:
                            act.wait_ge(bank_filled, side_index[last_turn(b - 2)] + 1)
                        if b >= 4 and n % 4 == 0 and j == 0:
                            act.wait_ge(totalled, b - 3)
                        c, w = chunk_index[(n, j)], width(n, j)
                        h = 2 * blocks[b][0] + blocks[b][2]
                        act.activation(probs[:, b % 2, n % 4, CH * j:CH * j + w], k.bank(c % S_BANKS, w), ACT.Exp,
                                       scale=unscale[:, h:h + 1], bias=neg_max[:, n % 2:n % 2 + 1], accum_out=total[:, n % 16, j:j + 1]).then_inc(exped, 1)
                    elif e in side_index and engine_of[side_index[e]] == "s":
                        m = side_index[e]
                        act.wait_ge(bank_filled, m + 1)
                        bank = k.bank(S_BANKS + m % SIDE_BANKS)
                        if e[0] == "fill":
                            n = 16 * e[1] + e[2]
                            if n >= 2:
                                act.wait_ge(split, n - 1)
                            ins = act.activation(staged[:, n % 2, :], bank, ACT.Identity, bias=fill_column(*e[1:]))
                        elif e[0] == "turn":
                            before_turn_copy(act, e)
                            a = first_query(*e[1:])
                            ins = act.activation(probs_t[:, turn_index[e[1:]] % RING, P * a:CH], bank[:, P * a:CH], ACT.Copy)
                        else:
                            b = e[1]
                            if b >= 2:
                                act.wait_ge(weighed, b - 1)
                            ins = act.activation(shares[:, b % 2, :], bank, ACT.Copy)
                        ins.then_inc(copied_s, 1)

            @block.vector
            def _(dve):
                n_part = 0
                for e in order:
                    if e[0] == "score":
                        n, j = e[1:]
                        q = blocks[n // 4][1]
                        c, w = chunk_index[(n, j)], width(n, j)
                        dve.wait_ge(scored, c + 1)
                        bank = k.bank(c % S_BANKS, w)
                        if j == q and n >= 2:
                            dve.wait_ge(exped, chunk_index[(n - 2, blocks[(n - 2) // 4][1])] + 1)
                        if q == 0:
                            dve.tensor_reduce(raw[:, n % 2:n % 2 + 1], bank, AX.X, ALU.max, negate=True).then_inc(raw_max, 1)
                        else:
                            dve.tensor_reduce(tops[:, n % 2, j:j + 1], bank, AX.X, ALU.max).then_inc(part_max, 1)
                            n_part += 1
                            if j == q:
                                dve.wait_ge(part_max, n_part)
                                dve.tensor_reduce(raw[:, n % 2:n % 2 + 1], tops[:, n % 2, 0:q + 1], AX.X, ALU.max,
                                                  negate=True).then_inc(raw_max, 1)
                        if j == q:
                            dve.wait_ge(raw_max, n + 1)
                            h = 2 * blocks[n // 4][0] + blocks[n // 4][2]
                            dve.tensor_scalar(neg_max[:, n % 2:n % 2 + 1], raw[:, n % 2:n % 2 + 1], unscale[:, h:h + 1], None,
                                              ALU.mult).then_inc(maxed, 1)
                    elif e[0] == "sum":
                        b = e[1]
                        q = blocks[b][1]
                        dve.wait_ge(exped, chunks_through(b))
                        at = 4 * b % 16
                        dve.tensor_reduce(sums[:, b % 2, :], total[:, at:at + 4, 0:q + 1], AX.X, ALU.add).then_inc(totalled, 1)
                        dve.wait_ge(totalled, b + 1)
                        if b >= 2:
                            dve.wait_ge(bank_filled, side_index[("share", b - 2, 0)] + 1)
                        dve.reciprocal(inv[:, b % 2, :], sums[:, b % 2, :]).then_inc(inverted, 1)
                    elif e[0] == "weigh":
                        b = e[1]
                        dve.wait_ge(mixed, mixes_through(b))
                        wait_copied(dve, ("share", b, 0))
                        p, q, s = blocks[b]
                        if p >= 1 and q == 0 and s == 0:
                            dve.wait_ge(bank_filled, side_index[("project", p - 1, 0)] + 1)
                        dve.scalar_tensor_tensor(out=z[:, s, CH * q:CH * (q + 1)], in0=k.bank(7), scalar=0.125,
                                                 in1=shares[:, b % 2, :], op0=ALU.mult, op1=ALU.mult).then_inc(weighed, 1)
                    elif e in side_index and engine_of[side_index[e]] == "v":
                        m = side_index[e]
                        dve.wait_ge(bank_filled, m + 1)
                        bank = k.bank(S_BANKS + m % SIDE_BANKS)
                        if e[0] == "fill":
                            p, tile = e[1:]
                            before_fill(dve, p, tile)
                            ins = dve.tensor_tensor(
                                k.scratch[:, 2 + p % 2, CH * (tile - 16):CH * (tile - 15)].rearrange("p (t d) -> p t d", t=4),
                                bank.rearrange("p (t d) -> p t d", t=4),
                                bv[:, P * p:P * (p + 1)].unsqueeze(1).to_broadcast([P, 4, P]), ALU.add)
                        elif e[0] == "turn":
                            before_turn_copy(dve, e)
                            b, kt = e[1:]
                            a = first_query(b, kt)
                            slot = probs_t[:, turn_index[(b, kt)] % RING, :]
                            if kt == 1 and a == 1:
                                dve.memset(slot[:, 0:P], 0.0)
                            ins = dve.tensor_copy(slot[:, P * a:CH], bank[:, P * a:CH])
                        else:
                            xs = k.xpad[:, 1 + 2 * P * e[1]:1 + 2 * P * (e[1] + 1)]
                            ins = dve.tensor_tensor(xs, xs, bank[:, 0:2 * P], ALU.add)
                        ins.then_inc(copied_v, 1)


def scale_heads(k, wq, wk, columns, unscale, masks):
    nc = k.nc
    names = "ones_set squared bias_squared summed bounded turned topped laid floored log_done inverted scale_done step rounded"
    tiles = [("ones", [P, 1], F32), ("bias_sq", [P, 32], F32), ("bound", [P, 32], F32), ("top", [32, 1], F32),
             ("least", [P, 32], F32), ("log", [P, 32], F32), ("root", [P, 32], F32), ("scale", [P, 32], F32),
             ("product", [P, 16], F32), ("inverse", [P, 16], F32)]
    with phase(nc, names, tiles) as (ones_set, squared, bias_squared, summed, bounded, turned, topped, laid, floored, log_done,
                                     inverted, scale_done, step, rounded,
                                     ones, bias_sq, bound, top, least, log, root, scale, product, inverse):
        with nc.Block() as block:
            @block.tensor
            def _(pe):
                pe.wait_ge(squared, 2)
                pe.wait_ge(ones_set, 1)
                for n in range(32):
                    for half in range(2):
                        mm = pe.matmul(k.bank(0)[64 * half:64 * half + 64, n:n + 1], k.s1[:, 64 * n:64 * n + 64], ones[:, :],
                                       start=True, stop=True)
                mm.then_inc(summed, 1)
                pe.wait_ge(bounded, 1)
                pe.transpose(k.bank(1, P, 32), bound[:, :], k.mat("ident")).then_inc(turned, 1)
                pe.wait_ge(topped, 1)
                pe.transpose(k.bank(2, 32), top[:, :].to_broadcast([32, P]), k.mat("ident")[0:32, 0:32]).then_inc(laid, 1)

            @block.scalar
            def _(act):
                act.preload_act_table_set("natural_log_exp_and_others")
                act.activation(k.s1[:, 0:1024], wq[:, :], ACT.Square).then_inc(squared, 1)
                act.activation(k.s1[:, 1024:2048], wk[:, :], ACT.Square).then_inc(squared, 1)
                act.wait_ge(floored, 1)
                act.activation(log[:, :], least[:, :], ACT.Ln).then_inc(log_done, 1)
                act.wait_ge(log_done, 1)
                act.activation(root[:, :], log[:, :], ACT.Exp, scale=-0.5).then_inc(inverted, 1)

            @block.vector
            def _(dve):
                dve.memset(ones[:, :], 1.0).then_inc(ones_set, 1)
                dve.tensor_copy(masks[:, 0, :], k.mat("ident")).then_inc(rounded, 1)
                dve.tensor_copy(masks[:, 1, :], k.mat("causal")).then_inc(rounded, 1)
                dve.tensor_tensor(bias_sq[:, :], columns[:, :], columns[:, :], ALU.mult).then_inc(bias_squared, 1)
                dve.wait_ge(bias_squared, 1)
                dve.wait_ge(summed, 1)
                dve.scalar_tensor_tensor(out=bound[:, :], in0=k.bank(0, 32), scalar=float(D), in1=bias_sq[:, :],
                                         op0=ALU.mult, op1=ALU.add).then_inc(bounded, 1)
                dve.wait_ge(turned, 1)
                dve.tensor_reduce(top[:, :], k.bank(1, P, 32), AX.X, ALU.max).then_inc(topped, 1)
                dve.wait_ge(laid, 1)
                dve.tensor_scalar(least[:, :], k.bank(2, 32), 2.0 ** -60, None, ALU.max).then_inc(floored, 1)
                dve.wait_ge(inverted, 1)
                dve.tensor_scalar(scale[:, :], root[:, :], 8192.0, None, ALU.mult).then_inc(scale_done, 1)
                dve.wait_ge(scale_done, 1)
                for n, w in enumerate((wq, wk)):
                    heads = w[:, :].rearrange("p (h d) -> p h d", d=64)
                    dve.tensor_tensor(heads, heads, scale[:, 16 * n:16 * n + 16].unsqueeze(2).to_broadcast([P, 16, 64]), ALU.mult)\
                        .then_inc(step, 1)
                dve.tensor_tensor(columns[:, :], columns[:, :], scale[:, :], ALU.mult).then_inc(step, 1)
                dve.tensor_tensor(product[:, :], scale[:, 0:16], scale[:, 16:32], ALU.mult).then_inc(step, 1)
                dve.wait_ge(step, 4)
                dve.reciprocal(inverse[:, :], product[:, :]).then_inc(step, 1)
                dve.wait_ge(step, 5)
                dve.tensor_scalar(unscale[:, :], inverse[:, :], 0.125, None, ALU.mult).then_inc(step, 1)


def layer3_attention(k, A):
    nc = k.nc
    with ExitStack() as ctx:
        def sb(name, shape, dt=F32):
            return ctx.enter_context(nc.sbuf_tensor(name + "_l3a", shape, dt))

        wq, wk, wv, proj = sb("wq", [P, 1024]), sb("wk", [P, 1024]), sb("wv", [P, 1024]), sb("proj", [P, 16, P])
        columns, unscale, bv = sb("columns", [P, 32]), sb("unscale", [P, 16]), sb("bv", [P, 1024])
        masks = sb("masks", [P, 2, P], BF16)
        layernorm(k, k.x, k.xn, 1e-5, loads=[
            (wq[:, :], A["L3_attn_WqT"]), (wk[:, :], A["L3_attn_WkT"]), (wv[:, :], A["L3_attn_WvT"]),
            (proj[0:64, :, :], A["L3_attn_proj"].rearrange("(j p) d -> p j d", p=64)),
            (proj[64:P, :, :], A["L3_attn_proj"].rearrange("(j p) d -> p j d", p=64)),
            (bv[:, :], A["L3_attn_bv"].rearrange("h d -> (h d)").rearrange("(a n) -> a n", a=1).to_broadcast([P, 1024])),
            (columns[:, :], A["L3_attn_columns"])])
        scale_heads(k, wq, wk, columns, unscale, masks)
        causal_attention(k, wq, wk, wv, proj, columns, unscale, masks, bv)


def layer3_ffn(k, A):
    nc = k.nc
    E, F = 8, 512
    FT = F // P
    with ExitStack() as ctx:
        def sb(name, shape, dt=F32):
            return ctx.enter_context(nc.sbuf_tensor(name + "_l3f", shape, dt))

        gate_w, up, down = sb("gate_w", [P, E]), sb("up", [P, E, 2 * F]), sb("down", [P, E, FT, P])
        logits, best, place = sb("logits", [P, NT, E]), sb("best", [P, NT, 8]), sb("place", [P, NT, 8], U32)
        place_f, iota8 = sb("place_f", [P, NT, 2]), sb("iota8", [P, E])
        gap, second, inv, share = sb("gap", [P, NT]), sb("second", [P, NT]), sb("inv", [P, NT]), sb("share", [P, 2, NT])
        pick, combine, rows = sb("pick", [P, 2, E, NT]), sb("combine", [P, E, NT]), sb("rows", [P, P])
        xe = sb("xe", [P, E, T])
        combine_dram = nc.dram_tensor("combine_dram", (E, T), F32).ap()
        weights = [(up[:, :, :], A["L3_ffn_gate_upT"].rearrange("e p f -> p e f")),
                   (down[:, :, :, :], A["L3_ffn_downT"].rearrange("e (j p) d -> p e j d", p=P))]
        (weights_landed,) = ctx.enter_context(phase(nc, "weights_landed", []))
        layernorm(k, k.x, k.xn, 1e-5, loads=[(gate_w[:, :], A["L3_ffn_gateT"]), (iota8[:, :], A["const_iota"][:, 0:E])],
                  late=weights, late_landed=weights_landed)

        names = "scored copied found placed gap_done exp_done step turned rows_done written"
        with phase(nc, names, []) as (scored, copied, found, placed, gap_done, exp_done, step, turned, rows_done, written):
            with nc.Block() as block:
                @block.tensor
                def _(pe):
                    for t in range(NT):
                        mm = pe.matmul(k.bank(0)[:, E * t:E * (t + 1)], k.xn_tile(t), gate_w[:, :], start=True, stop=True)
                    mm.then_inc(scored, 1)
                    pe.wait_ge(step, 7)
                    pe.transpose(k.bank(1, P), combine[:, :, :].rearrange("p e t -> p (e t)"), k.mat("ident")).then_inc(turned, 1)

                @block.vector
                def _(dve):
                    dve.wait_ge(scored, 1)
                    dve.tensor_copy(logits[:, :, :].rearrange("p t e -> p (t e)"), k.bank(0, NT * E)).then_inc(copied, 1)
                    dve.wait_ge(copied, 1)
                    for t in range(NT):
                        dve.max(best[:, t, :], logits[:, t, :]).then_inc(found, 1)
                    for t in range(NT):
                        dve.wait_ge(found, t + 1)
                        dve.max_index(place[:, t, :], best[:, t, :], logits[:, t, :]).then_inc(placed, 1)
                    dve.tensor_tensor(gap[:, :], best[:, :, 1], best[:, :, 0], ALU.subtract).then_inc(gap_done, 1)
                    dve.wait_ge(placed, NT)
                    dve.tensor_copy(place_f[:, :, :], place[:, :, 0:2]).then_inc(step, 1)
                    dve.wait_ge(exp_done, 1)
                    dve.tensor_scalar(inv[:, :], second[:, :], 1.0, None, ALU.add).then_inc(step, 1)
                    dve.wait_ge(step, 2)
                    dve.reciprocal(share[:, 0, :], inv[:, :]).then_inc(step, 1)
                    dve.wait_ge(step, 3)
                    dve.tensor_tensor(share[:, 1, :], share[:, 0, :], second[:, :], ALU.mult).then_inc(step, 1)
                    for b in range(2):
                        dve.tensor_tensor(pick[:, b, :, :], iota8[:, :].unsqueeze(2).to_broadcast([P, E, NT]),
                                          place_f[:, :, b].unsqueeze(1).to_broadcast([P, E, NT]), ALU.is_equal).then_inc(step, 1)
                    dve.wait_ge(step, 6)
                    for b in range(2):
                        dve.tensor_tensor(pick[:, b, :, :], pick[:, b, :, :],
                                          share[:, b, :].unsqueeze(1).to_broadcast([P, E, NT]), ALU.mult).then_inc(rows_done, 1)
                    dve.wait_ge(rows_done, 2)
                    dve.tensor_tensor(combine[:, :, :], pick[:, 0, :, :], pick[:, 1, :, :], ALU.add).then_inc(step, 1)
                    dve.wait_ge(turned, 1)
                    dve.tensor_copy(rows[:, :], k.bank(1, P)).then_inc(rows_done, 1)

                @block.scalar
                def _(act):
                    act.wait_ge(gap_done, 1)
                    act.activation(second[:, :], gap[:, :], ACT.Exp).then_inc(exp_done, 1)

                @block.sync
                def _(sp):
                    sp.wait_ge(rows_done, 3)
                    sp.dma_start(combine_dram.rearrange("e (t p) -> (e t) p", p=P), rows[:, :]).then_inc(written, 16)
                    sp.wait_ge(written, 16)

        units = [(c, e, f) for c in range(NC) for e in range(E) for f in range(FT)]
        LAG = 2
        with phase(nc, "read scaled_low scaled_high gate_done value_done acted gated out_done added",
                   [("silu", [P, 2, CH], F32), ("h", [P, 4, CH], F32)]) as (
                read, scaled_low, scaled_high, gate_done, value_done, acted, gated, out_done, added, silu, h):
            def scale(eng, c, e):
                here = xe[:, e, CH * c:CH * (c + 1)]
                return eng.tensor_tensor(here, here, k.xn(c), ALU.mult)

            with nc.Block() as block:
                @block.sync
                def _(sp):
                    for c in range(NC):
                        if c:
                            sp.wait_ge(read, 16 * c)
                        shares = combine_dram[:, CH * c:CH * (c + 1)].unsqueeze(0).to_broadcast([P, E, CH])
                        sp.dma_start(xe[:, :, CH * c:CH * (c + 1)], shares).then_inc(read, 16)
                    sp.wait_ge(read, 16 * NC)

                @block.gpsimd
                def _(pool):
                    for c in range(NC):
                        pool.wait_ge(read, 16 * (c + 1))
                        for e in range(4 if c == 0 else 0, E):
                            scale(pool, c, e).then_inc(scaled_high, 1)

                @block.tensor
                def _(pe):
                    pe.wait_ge(weights_landed, 16 * len(weights))
                    for n in range(len(units) + LAG):
                        if n < len(units):
                            c, e, f = units[n]
                            if n >= 3:
                                pe.wait_ge(acted, n - 2)
                                pe.wait_ge(gated, n - 2)
                            pe.matmul(k.bank(n % 3), up[:, e, P * f:P * (f + 1)], k.xn(c), start=True, stop=True)\
                                .then_inc(gate_done, 1)
                            if f == 0:
                                if c == 0 and e < 4:
                                    pe.wait_ge(scaled_low, e + 1)
                                else:
                                    pe.wait_ge(scaled_high, E * c + e + 1 - 4)
                            pe.matmul(k.bank(3 + n % 3), up[:, e, F + P * f:F + P * (f + 1)], xe[:, e, CH * c:CH * (c + 1)],
                                      start=True, stop=True).then_inc(value_done, 1)
                        if n >= LAG:
                            u = n - LAG
                            c, e, f = units[u]
                            first, last = (e, f) == (0, 0), (e, f) == (E - 1, FT - 1)
                            if first and c >= 2:
                                pe.wait_ge(added, c - 1)
                            pe.wait_ge(gated, u + 1)
                            mm = pe.matmul(k.bank(6 + c % 2), down[:, e, f, :], h[:, u % 4, :], start=first, stop=last)
                            mm.then_inc(out_done, 1)

                @block.scalar
                def _(act):
                    for n in range(len(units)):
                        act.wait_ge(gate_done, n + 1)
                        if n >= 2:
                            act.wait_ge(gated, n - 1)
                        act.activation(silu[:, n % 2, :], k.bank(n % 3), ACT.Silu).then_inc(acted, 1)

                @block.vector
                def _(dve):
                    dve.wait_ge(read, 16)
                    for e in range(4):
                        scale(dve, 0, e).then_inc(scaled_low, 1)
                    for n, (c, e, f) in enumerate(units):
                        dve.wait_ge(value_done, n + 1)
                        dve.wait_ge(acted, n + 1)
                        if n >= 4:
                            dve.wait_ge(out_done, n - 3)
                        dve.tensor_tensor(h[:, n % 4, :], k.bank(3 + n % 3), silu[:, n % 2, :], ALU.mult).then_inc(gated, 1)
                        if n >= 8 and n % (E * FT) == 7 and c >= 1:
                            dve.wait_ge(out_done, E * FT * c)
                            dve.tensor_tensor(k.x(c - 1), k.x(c - 1), k.bank(6 + (c - 1) % 2), ALU.add).then_inc(added, 1)
                    dve.wait_ge(out_done, len(units))
                    dve.tensor_tensor(k.x(NC - 1), k.x(NC - 1), k.bank(6 + (NC - 1) % 2), ALU.add).then_inc(added, 1)
STEPS = [layer0_attention, layer0_ffn, layer1_attention, layer1_ffn, layer2_attention, layer2_ffn,
         layer3_attention, layer3_ffn]


def build(nc, A, out, steps=STEPS):
    with ExitStack() as ctx:
        k = Core(nc, ctx)
        setup(k, A["x_t"], A["const_mats"])
        for step in steps:
            step(k, A)
        store(k, out)


def host_constants(np):
    i = np.arange(P)
    mats = np.zeros((P, N_MATS, P), np.float32)
    mats[:, 0] = np.eye(P)
    mats[:, 1] = i[:, None] // 8 == i[None, :] // 8
    mats[:, 2] = i[:, None] // 64 == i[None, :] // 64
    for m in range(P):
        mats[32 * (m // 32) + 8, 3, m] = 1.0
    mats[:, 4] = np.where(i[None, :] > i[:, None], MASKED, 0.0)

    mats[:, 5] = np.eye(P) - 1.0 / D

    t = np.arange(T, dtype=np.float32)
    f32 = np.float32
    inv = (f32(1.0) / f32(10000.0) ** (np.arange(0, 8, 2, dtype=f32) / f32(8))).astype(f32)
    ang = np.outer(inv, t).astype(f32)
    d8 = i % 8
    rope = np.stack([np.cos(ang)[d8 % 4], np.where(d8[:, None] < 4, -1.0, 1.0) * np.sin(ang)[d8 % 4]], 1).astype(f32)

    half = np.arange(0, 64, 2, dtype=f32)
    inv = (f32(1.0) / f32(10000.0) ** (half / f32(64))).astype(f32)
    ang = np.outer(inv, t).astype(f32).astype(np.float64)
    base = ((half + f32(0.4 * 64)) / f32(1.4 * 64)).astype(f32)
    power = ((t - T // 2) / f32(32)).astype(f32)
    scale = (base[:, None].astype(np.float64) ** power[None, :].astype(np.float64))
    d64 = i % 32
    cos, sin, sc = np.cos(ang)[d64], np.sin(ang)[d64], scale[d64]
    sin = np.where(i[:, None] % 64 < 32, -sin, sin)
    xpos = np.stack([8 * cos * sc, 8 * sin * sc, cos / sc, sin / sc], 1).astype(f32)

    key, query = np.arange(P)[None, :], i[:, None] % 64
    key = np.where(i[:, None] < 64, (key + 64) % P, key)
    band = np.where((key <= query + 64) & (key >= query), 0.0, MASKED)
    first = np.where((i[:, None] < 64) & (key < 64), MASKED, band)
    bands = np.stack([first, band], 1).astype(f32)
    return {"const_mats": mats, "const_rope": rope, "const_xpos": xpos, "const_bands": bands,
            "const_iota": np.broadcast_to(np.arange(T, dtype=f32), (P, T)).copy(),
            "const_token": (np.arange(NT)[None, :] * P + i[:, None]).astype(f32)}


def arrange(np, inputs):
    a = {n: np.asarray(v) for n, v in inputs.items()}
    out = {}
    for n, v in a.items():
        out[n] = v.reshape(-1, 1) if v.ndim == 1 else v
    out["x_t"] = a["L0_attn_x"][0].T
    del out["L0_attn_x"]
    for n in ("Wq", "Wk", "Wv", "Wp"):
        out[f"L0_attn_{n}T"] = a[f"L0_attn_{n}"].T
        del out[f"L0_attn_{n}"]
    w = a["L1_attn_w_qkv"]
    even = np.arange(D).reshape(16, 4, 2).transpose(0, 2, 1).reshape(-1)
    odd = np.arange(D).reshape(16, 4, 2)[:, :, ::-1].transpose(0, 2, 1).reshape(-1)
    out["L1_attn_qkT"] = np.stack([w[:D][even].T, w[:D][odd].T, w[D:2 * D][even].T, w[D:2 * D][odd].T], 1)
    out["L1_attn_vT"] = w[2 * D:].T
    out["L1_attn_outT"] = a["L1_attn_w_out"].T
    del out["L1_attn_w_qkv"], out["L1_attn_w_out"]
    w = a["L1_ffn_wqkv"]
    depth = w.shape[0]
    turned = w[:, :, :1024].reshape(depth, D, 16, 2, 32)[:, :, :, ::-1].reshape(depth, D, 1024)
    out["L1_ffn_w_turned"] = turned
    twice = {n: np.tile(a["L1_ffn_" + n], (1, 2)) for n in ("q_scale", "k_scale")}
    swapped = {n: v.reshape(depth, 2, 2, 32)[:, :, ::-1].reshape(depth, D) for n, v in twice.items()}
    out["L1_ffn_columns"] = np.stack([twice["q_scale"], swapped["q_scale"], twice["k_scale"], swapped["k_scale"],
                                      a["L1_ffn_ln_g"], a["L1_ffn_ln_b"], a["L1_ffn_b2"]], 2)
    hidden = a["L1_ffn_b1"].shape[1] // 2
    b1 = np.zeros((depth, 2, 3 * P), np.float32)
    b1[:, :, :hidden] = a["L1_ffn_b1"].reshape(depth, 2, hidden)
    out["L1_ffn_b1"] = b1.reshape(depth, 6, P).transpose(0, 2, 1)
    for n in ("q_scale", "k_scale", "ln_g", "ln_b", "b2"):
        del out["L1_ffn_" + n]
    for n in ("q", "k", "v"):
        out[f"L3_attn_W{n}T"] = a[f"L3_attn_W{n}"].reshape(16 * 64, D).T
        del out[f"L3_attn_W{n}"]
    out["L3_attn_columns"] = np.concatenate([np.tile(a["L3_attn_" + n].T, (2, 1)) for n in ("bq", "bk")], 1)
    del out["L3_attn_bq"], out["L3_attn_bk"]
    out["L3_ffn_gateT"] = a["L3_ffn_gate_w"].T
    out["L3_ffn_gate_upT"] = a["L3_ffn_gate_up_proj"].transpose(0, 2, 1)
    out["L3_ffn_downT"] = a["L3_ffn_down_proj"].transpose(0, 2, 1)
    del out["L3_ffn_gate_w"], out["L3_ffn_gate_up_proj"], out["L3_ffn_down_proj"]
    out.update(host_constants(np))
    return {n: np.ascontiguousarray(v) for n, v in out.items()}


def kernel(**inputs):
    import numpy as np
    import concourse.bacc as bacc
    from concourse.bass_utils import run_bass_kernel_spmd

    nc = bacc.Bacc("TRN2", target_bir_lowering=False, num_devices=1)
    arrays, args = {}, {}
    for name, a in arrange(np, inputs).items():
        arrays[f"in_{name}"] = a
        args[name] = nc.dram_tensor(f"in_{name}", a.shape, mybir.dt.from_np(a.dtype), kind="ExternalInput").ap()
    out = nc.dram_tensor("out_t", (D, T), F32, kind="ExternalOutput").ap()
    build(nc, args, out)
    r = run_bass_kernel_spmd(nc, [arrays], core_ids=[0])
    return np.ascontiguousarray(r.results[0]["out_t"].T).reshape(1, T, D)
```
